# Optimizing a Trainium2 kernel written in Bass

```python
import numpy as np
import jax
import jax.numpy as jnp

def _softmax(x, axis=-1):
    return jax.nn.softmax(x, axis=axis)

def _gelu(x):
    return jax.nn.gelu(x, approximate=True)

def _silu(x):
    return jax.nn.silu(x)

def _sigmoid(x):
    return jax.nn.sigmoid(x)

def _layernorm(x, axis=-1, eps=1e-05):
    m = jnp.mean(x, axis=axis, keepdims=True)
    v = jnp.var(x, axis=axis, keepdims=True)
    return (x - m) / jnp.sqrt(v + eps)

def _scatter_add(tgt, idx, src, axis=0):
    return tgt.at[idx].add(src)

def _segment_sum(src, seg, n):
    return jax.ops.segment_sum(src, seg, n)
kernel_name = 'mk_gps_d1_gnn_r8_794c06'

def setup_inputs(seed: int=0):
    np.random.seed(seed)
    _w = jnp.asarray

    def _rec_inputs():
        import jax
        import jax.numpy as jnp
        _gk = jax.random.key(seed)
        x = -0.0003713 + 1 * jax.random.normal(jax.random.fold_in(_gk, 1), (6250, 256), jnp.float32)
        src = jax.random.randint(jax.random.fold_in(_gk, 2), (100000,), 0, 6250, jnp.int32)
        dst = jax.random.randint(jax.random.fold_in(_gk, 3), (100000,), 0, 6250, jnp.int32)
        _o = jnp.argsort(dst, stable=True)
        src = src[_o]
        dst = dst[_o]
        edge_attr_16 = -0.00010739 + 0.99994 * jax.random.normal(jax.random.fold_in(_gk, 12), (100000, 16), jnp.float32)
        edge_attr_4 = jax.random.uniform(jax.random.fold_in(_gk, 13), (100000, 4), jnp.float32, 0.0, 1)
        return (x, src, dst, edge_attr_16, edge_attr_4)
    x, src, dst, edge_attr_16, edge_attr_4 = _rec_inputs()

    def _L0_gnn_setup():
        import jax, jax.numpy as jnp
        import numpy as np
        N = 6250
        E = 100000
        IN_DIM = 256
        H = 8
        D = 32
        T = 4
        F = 16
        NEG_SLOPE = 0.2
        key = jax.random.key(seed)
        ks = jax.random.split(key, 9)
        feat = jax.random.normal(ks[0], (N, IN_DIM), dtype=jnp.float32)
        e_pro = jax.random.normal(ks[1], (E, F), dtype=jnp.float32)
        mask = jax.random.uniform(ks[2], (E, T), dtype=jnp.float32)
        W_n = jax.random.normal(ks[3], (IN_DIM, H * D), dtype=jnp.float32) * (1.0 / np.sqrt(IN_DIM))
        attn_l = jax.random.normal(ks[4], (H, D, T), dtype=jnp.float32) * 0.1
        attn_r = jax.random.normal(ks[5], (H, D, T), dtype=jnp.float32) * 0.1
        attn_m = jax.random.normal(ks[6], (H, F, T), dtype=jnp.float32) * 0.1
        src = jax.random.randint(ks[7], (E,), 0, N, dtype=jnp.int32)
        dst = jax.random.randint(ks[8], (E,), 0, N, dtype=jnp.int32)
        return {'feat': feat, 'e_pro': e_pro, 'mask': mask, 'W_n': W_n, 'attn_l': attn_l, 'attn_r': attn_r, 'attn_m': attn_m, 'src': src, 'dst': dst}
    _L0_gnn_all = _L0_gnn_setup()
    _L0_gnn_in = {k: v for k, v in _L0_gnn_all.items() if k in ('W_n', 'attn_l', 'attn_r', 'attn_m')}
    del _L0_gnn_all

    def _L0_mix_setup():
        import jax, jax.numpy as jnp
        import numpy as np
        HEADS, DIM_HEAD = (8, 64)
        EPS = 1e-05

        def instance_norm(t):
            mu = jnp.mean(t, axis=-1, keepdims=True)
            var = jnp.mean((t - mu) ** 2, axis=-1, keepdims=True)
            return (t - mu) * jax.lax.rsqrt(var + EPS)
        key = jax.random.key(seed)
        k1, k2, k3, k4 = jax.random.split(key, 4)
        B, N, D = (8, 1024, 256)
        inner = HEADS * DIM_HEAD
        x = jax.random.normal(k1, (B, N, D), jnp.float32)
        w_qkv = jax.random.normal(k2, (3 * inner, D), jnp.float32) / np.sqrt(D).astype(np.float32)
        w_out = jax.random.normal(k3, (D, inner), jnp.float32) / np.sqrt(inner).astype(np.float32)
        b_out = 0.01 * jax.random.normal(k4, (D,), jnp.float32)
        return {'x': x, 'w_qkv': w_qkv, 'w_out': w_out, 'b_out': b_out}
    _L0_mix_all = _L0_mix_setup()
    _L0_mix_in = {k: v for k, v in _L0_mix_all.items() if k in ('w_qkv', 'w_out', 'b_out')}
    del _L0_mix_all

    def _L0_ffn_setup():
        import jax, jax.numpy as jnp
        import numpy as np
        N_EXPERTS = 8
        TOP_K = 2
        key = jax.random.key(seed)
        ks = jax.random.split(key, 5)
        B, T, C, E, H = (8, 256, 256, 8, 682)
        scale = 1.0 / np.sqrt(C)
        return {'x': jax.random.normal(ks[0], (B, T, C), dtype=jnp.float32), 'router_w': jax.random.normal(ks[1], (E, C), dtype=jnp.float32) * scale, 'w1': jax.random.normal(ks[2], (E, H, C), dtype=jnp.float32) * scale, 'w2': jax.random.normal(ks[3], (E, C, H), dtype=jnp.float32) * (1.0 / np.sqrt(H)), 'w3': jax.random.normal(ks[4], (E, H, C), dtype=jnp.float32) * scale}
    _L0_ffn_all = _L0_ffn_setup()
    _L0_ffn_in = {k: v for k, v in _L0_ffn_all.items() if k in ('router_w', 'w1', 'w2', 'w3')}
    del _L0_ffn_all
    return {'x': x, 'src': src, 'dst': dst, 'edge_attr_16': edge_attr_16, 'edge_attr_4': edge_attr_4, 'L0_gnn_W_n': _L0_gnn_in['W_n'], 'L0_gnn_attn_l': _L0_gnn_in['attn_l'], 'L0_gnn_attn_r': _L0_gnn_in['attn_r'], 'L0_gnn_attn_m': _L0_gnn_in['attn_m'], 'L0_mix_w_qkv': _L0_mix_in['w_qkv'], 'L0_mix_w_out': _L0_mix_in['w_out'], 'L0_mix_b_out': _L0_mix_in['b_out'], 'L0_ffn_router_w': _L0_ffn_in['router_w'], 'L0_ffn_w1': _L0_ffn_in['w1'], 'L0_ffn_w2': _L0_ffn_in['w2'], 'L0_ffn_w3': _L0_ffn_in['w3']}

def reference(x, src, dst, edge_attr_16, edge_attr_4, L0_gnn_W_n, L0_gnn_attn_l, L0_gnn_attn_r, L0_gnn_attn_m, L0_mix_w_qkv, L0_mix_w_out, L0_mix_b_out, L0_ffn_router_w, L0_ffn_w1, L0_ffn_w2, L0_ffn_w3):
    import jax
    import jax.numpy as jnp

    def _L0_gnn_ref(feat, e_pro, mask, W_n, attn_l, attn_r, attn_m, src, dst):
        import jax, jax.numpy as jnp
        import numpy as np
        N = 6250
        E = 100000
        IN_DIM = 256
        H = 8
        D = 32
        T = 4
        F = 16
        NEG_SLOPE = 0.2
        feat_src = (feat @ W_n).reshape(N, H, D)
        el = jnp.einsum('nhd,hdt->nht', feat_src, attn_l)
        er = jnp.einsum('nhd,hdt->nht', feat_src, attn_r)
        em = jnp.einsum('ef,hft->eht', e_pro, attn_m)
        left = jnp.einsum('eht,et->eh', el[src], mask)
        right = jnp.einsum('eht,et->eh', er[dst], mask)
        em_e = jnp.einsum('eht,et->eh', em, mask)
        e = (left + right + em_e) / 3.0
        e = jnp.where(e > 0, e, NEG_SLOPE * e)
        e_max = jax.ops.segment_max(e, dst, num_segments=N)
        e_exp = jnp.exp(e - e_max[dst])
        e_sum = jax.ops.segment_sum(e_exp, dst, num_segments=N)
        a = e_exp / e_sum[dst]
        msg = feat_src[src] * a[:, :, None]
        rst = jax.ops.segment_sum(msg, dst, num_segments=N)
        return rst.reshape(N, H * D)

    def _L0_mix_ref(x, w_qkv, w_out, b_out):
        import jax, jax.numpy as jnp
        import numpy as np
        HEADS, DIM_HEAD = (8, 64)
        EPS = 1e-05

        def instance_norm(t):
            mu = jnp.mean(t, axis=-1, keepdims=True)
            var = jnp.mean((t - mu) ** 2, axis=-1, keepdims=True)
            return (t - mu) * jax.lax.rsqrt(var + EPS)
        B, N, _ = x.shape
        H, Dh = (HEADS, DIM_HEAD)
        qkv = jnp.einsum('bnd,ed->bne', x, w_qkv)
        q, k, v = jnp.split(qkv, 3, axis=-1)

        def to_heads(t):
            return t.reshape(B, N, H, Dh).transpose(0, 2, 1, 3)
        q, k, v = (to_heads(q), to_heads(k), to_heads(v))
        k = instance_norm(k)
        v = instance_norm(v)
        dots = jnp.einsum('bhnd,bhne->bhde', k, v)
        out = jnp.einsum('bhnd,bhde->bhne', q, dots) / N
        out = out.transpose(0, 2, 1, 3).reshape(B, N, H * Dh)
        return jnp.einsum('bne,de->bnd', out, w_out) + b_out

    def _L0_ffn_ref(x, router_w, w1, w2, w3):
        import jax, jax.numpy as jnp
        import numpy as np
        N_EXPERTS = 8
        TOP_K = 2
        B, T, C = x.shape
        flat = x.reshape(-1, C)
        logits = flat @ router_w.T
        probs = jax.nn.softmax(logits, axis=-1)
        topk_probs, topk_idx = jax.lax.top_k(probs, TOP_K)
        topk_probs = topk_probs / (jnp.sum(topk_probs, axis=-1, keepdims=True) + 1e-09)
        onehot = jax.nn.one_hot(topk_idx, N_EXPERTS, dtype=flat.dtype)
        gates = jnp.einsum('nk,nke->ne', topk_probs, onehot)
        h1 = jnp.einsum('nc,ehc->neh', flat, w1)
        h3 = jnp.einsum('nc,ehc->neh', flat, w3)
        h = jax.nn.silu(h1) * h3
        y = jnp.einsum('neh,ech->nec', h, w2)
        out = jnp.einsum('ne,nec->nc', gates, y)
        return out.reshape(B, T, C)
    xn = _layernorm(x, axis=-1)
    x = x + _L0_gnn_ref(xn, edge_attr_16, edge_attr_4, L0_gnn_W_n, L0_gnn_attn_l, L0_gnn_attn_r, L0_gnn_attn_m, src, dst) + _L0_mix_ref(xn[None], L0_mix_w_qkv, L0_mix_w_out, L0_mix_b_out)[0]
    x = x + _L0_ffn_ref(_layernorm(x, axis=-1)[None], L0_ffn_router_w, L0_ffn_w1, L0_ffn_w2, L0_ffn_w3)[0]
    return x

_drawn_inputs = setup_inputs


def setup_inputs(seed=0):
    import zlib

    import numpy as np

    out = dict(_drawn_inputs(seed))
    spreads = {}
    factors = {'L0_mix_b_out': 2.711}
    for name, (base, spread) in spreads.items():
        noise = np.random.default_rng([zlib.crc32(name.encode()), seed]).standard_normal(out[name].shape)
        drawn = base * np.exp(spread * noise) if base else spread * noise
        out[name] = jnp.asarray(drawn.astype(out[name].dtype))
    for name, factor in factors.items():
        out[name] = (out[name] * factor).astype(out[name].dtype)
    return out
```

```python
from contextlib import ExitStack

import numpy as np
import concourse.bass as bass
from concourse import mybir

P = 128
F32 = mybir.dt.float32
I32 = mybir.dt.int32
ALU = mybir.AluOpType
ACT = mybir.ActivationFunctionType
AX = mybir.AxisListType
ds = bass.ds

NODES, DIM = 6250, 256
EDGES, EPRO, TYPES = 100000, 16, 4
GHEADS, GDIM = 8, 32
MHEADS, MDIM = 8, 64
INNER = MHEADS * MDIM
EXPERTS, HID = 8, 682
EPS = 1e-5
SLOPE = 0.2
BIG = 1e30

NT = 2 * -(-NODES // (2 * P))
NP = NT * P
KC = DIM // P
ET = 7
GROUP = ET * P
NG = 4 * -(-EDGES // (4 * GROUP))
EP = NG * GROUP
NBUF = 4
HT = GHEADS * TYPES
ROW = DIM + HT
AGG = DIM + GHEADS
HC = 6
HW = -(-HID // HC)
HP = HC * HW


def build(nc, x, src, dst, dst_first, dst_last, dst_head, dst_tail, dst_before, dst_after, dst_cols, mask, epro,
          w_n, w_nT, attn_lr, attn_m, w_kvT, w_q, w_oT, b_out, router, w1T, w3T, w2T, out):
    xnT_d = nc.dram_tensor("xn_transposed", [NT, P, KC * P], F32).ap()
    table = nc.dram_tensor("node_table", [NP, ROW], F32).ap()
    er_table = nc.dram_tensor("right_scores", [NP, HT], F32).ap()
    pens_d = nc.dram_tensor("chain_penalties", [NG + 2, 4 * P], F32).ap()
    agg_d = nc.dram_tensor("aggregate", [NP, AGG], F32).ap()
    with ExitStack() as ctx:
        ident = ctx.enter_context(nc.sbuf_tensor("ident", [P, P], F32))
        iota_row = ctx.enter_context(nc.sbuf_tensor("iota_row", [P, P], F32))
        iota_col = ctx.enter_context(nc.sbuf_tensor("iota_col", [P, 1], F32))
        zeros = ctx.enter_context(nc.sbuf_tensor("zeros", [P, 512], F32))
        eps_col = ctx.enter_context(nc.sbuf_tensor("eps_col", [P, 1], F32))
        mix = ctx.enter_context(nc.sbuf_tensor("mix_matrix", [P, KC, DIM], F32))
        constants(nc, ident, iota_row, iota_col, zeros, eps_col)
        project_nodes(nc, x, w_n, w_nT, attn_lr, ident, eps_col, zeros, xnT_d, table, er_table, agg_d)
        mix_matrix(nc, xnT_d, w_kvT, w_q, w_oT, zeros, eps_col, mix)
        edges(nc, src, dst, dst_first, dst_last, dst_head, dst_tail, dst_before, dst_after, dst_cols, mask, epro,
              attn_m, ident, iota_row, iota_col, zeros, table, er_table, pens_d, agg_d)
        feed_forward(nc, x, xnT_d, agg_d, mix, b_out, router, w1T, w3T, w2T, ident, eps_col, out)


def turns(eng, count):
    def run(body):
        body(0)
        with eng.Fori(1, count) as i:
            body(i)
    return run


def tools(nc, ctx, tag):
    def sb(name, shape, dt=F32):
        return ctx.enter_context(nc.sbuf_tensor(f"{tag}_{name}", shape, dt))

    def ps(name):
        return ctx.enter_context(nc.psum_tensor(f"{tag}_{name}", [P, 512], F32))

    taken = []
    ctx.callback(lambda: (nc.clear_and_free_semaphores(taken), nc.all_engine_barrier()))

    def sem(name):
        taken.append(nc.alloc_semaphore(f"{tag}_{name}"))
        return taken[-1]

    passed = sem("passed")

    def hold(eng):
        eng.sem_inc(passed, 1)

    def sems(name, n=2):
        return [sem(f"{name}{j}") for j in range(n)]

    return sb, ps, sem, sems, hold


def constants(nc, ident, iota_row, iota_col, zeros, eps_col):
    with ExitStack() as ctx:
        sb, ps, sem, sems, hold = tools(nc, ctx, "const")
        row_i, col_i = sb("row_i", [P, P], I32), sb("col_i", [P, 1], I32)
        blank, counted = sem("blank"), sem("counted")
        block = ctx.enter_context(nc.Block())

        @block.gpsimd
        def _(pool):
            pool.memset(zeros[:, :], 0.0)
            pool.memset(eps_col[:, :], EPS)
            pool.memset(ident[:, :], 0.0).then_inc(blank, 1)
            pool.iota(row_i[:, :], [[1, P]], base=0, channel_multiplier=0).then_inc(counted, 1)
            pool.iota(col_i[:, :], [[1, 1]], base=0, channel_multiplier=1).then_inc(counted, 1)
            pool.wait_ge(blank, 1)
            pool.affine_select(out=ident[:, :], in_=ident[:, :], compare_op=ALU.not_equal, fill=1.0,
                               base=0, pattern=[[-1, P]], channel_multiplier=1)

        @block.vector
        def _(dve):
            dve.wait_ge(counted, 2)
            dve.tensor_copy(iota_row[:, :], row_i[:, :])
            dve.tensor_copy(iota_col[:, :], col_i[:, :])


def project_nodes(nc, x, w_n, w_nT, attn_lr, ident, eps_col, zeros, xnT_d, table, er_table, agg_d):
    WID = DIM + 2 * HT
    with ExitStack() as ctx:
        sb, ps, sem, sems, hold = tools(nc, ctx, "proj")
        wn_T, lr = sb("wnT", [P, KC, DIM]), sb("lr", [P, KC, 2 * HT])
        wcat = sb("wcat", [P, KC, WID])
        xt, xn = sb("x", [P, 2, DIM]), sb("xn", [P, 2, DIM])
        stats, mv = sb("stats", [P, 2, 6]), sb("mv", [P, 2, 2])
        sd, rs = sb("sd", [P, 2]), sb("rs", [P, 2])
        xT, proj = sb("xT", [P, 2, KC, P]), sb("proj", [P, 2, WID])
        pT, pP = [ps("T0"), ps("T1")], [ps("P0"), ps("P1")]
        weights_in, scores_folded, wcat_ready = sem("weights_in"), sem("scores_folded"), sem("wcat_ready")
        x_in, stats_ok, mv_ok, sd_ok, rs_ok, xn_ok, turned, xT_ok, projected, proj_ok, stored = (
            sems(n) for n in ("x_in", "stats", "mv", "sd", "rs", "xn", "turned", "xT", "projected", "proj_ok", "stored"))
        cleared = sem("cleared")
        block = ctx.enter_context(nc.Block())

        @block.sync
        def _(sp):
            sp.dma_start(wn_T[:, :, :], w_nT.rearrange("(k p) n -> p k n", p=P)).then_inc(weights_in, 16)
            sp.dma_start(lr[:, :, :], attn_lr.rearrange("(k p) n -> p k n", p=P)).then_inc(weights_in, 16)
            sp.dma_start(wcat[:, :, 0:DIM], w_n.rearrange("(k p) n -> p k n", p=P)).then_inc(weights_in, 16)
            for t in range(NT):
                sp.dma_start(agg_d[t * P:(t + 1) * P, :], zeros[:, 0:AGG]).then_inc(cleared, 16)
            @turns(sp, NT // 2)
            def _(i):
                for b in range(2):
                    t = 2 * i + b
                    sp.wait_ge(xn_ok[b], i)
                    hold(sp)
                    sp.dma_start(xt[:, b, :], x[ds(t * P, P), :]).then_inc(x_in[b], 16)
            sp.wait_ge(cleared, 16 * NT)

        @block.gpsimd
        def _(pool):
            @turns(pool, NT // 2)
            def _(i):
                for b in range(2):
                    t = 2 * i + b
                    pool.wait_ge(xT_ok[b], i + 1)
                    pool.dma_start(xnT_d[ds(t, 1), :, :].rearrange("o p n -> (o p) n"),
                                   xT[:, b, :, :].rearrange("p k n -> p (k n)")).then_inc(stored[b], 16)
                    pool.wait_ge(proj_ok[b], i + 1)
                    pool.dma_start(table[ds(t * P, P), :], proj[:, b, 0:ROW]).then_inc(stored[b], 16)
                    pool.dma_start(er_table[ds(t * P, P), :], proj[:, b, ROW:WID]).then_inc(stored[b], 16)
            for b in range(2):
                pool.wait_ge(stored[b], 48 * (NT // 2))

        @block.vector
        def _(dve):
            dve.wait_ge(scores_folded, 1)
            for k in range(KC):
                dve.tensor_copy(wcat[:, k, DIM:WID], pP[0][:, k * 2 * HT:(k + 1) * 2 * HT]).then_inc(wcat_ready, 1)
            @turns(dve, NT // 2)
            def _(i):
                for b in range(2):
                    t = 2 * i + b
                    dve.wait_ge(x_in[b], 16 * i + 16)
                    dve.bn_stats(stats[:, b, :], xt[:, b, :]).then_inc(stats_ok[b], 1)
                    dve.wait_ge(stats_ok[b], i + 1)
                    hold(dve)
                    dve.bn_aggr(mv[:, b, :], stats[:, b, :]).then_inc(mv_ok[b], 1)
                    dve.wait_ge(sd_ok[b], i + 1)
                    dve.reciprocal(rs[:, b:b + 1], sd[:, b:b + 1]).then_inc(rs_ok[b], 1)
                    dve.wait_ge(rs_ok[b], i + 1)
                    dve.wait_ge(turned[b], i)
                    dve.tensor_scalar(xn[:, b, :], xt[:, b, :], mv[:, b, 0:1], rs[:, b:b + 1],
                                      ALU.subtract, ALU.mult).then_inc(xn_ok[b], 1)
                    dve.wait_ge(projected[b], i + 1)
                    dve.wait_ge(stored[b], 48 * i)
                    dve.tensor_copy(proj[:, b, :], pP[b][:, 0:WID]).then_inc(proj_ok[b], 1)

        @block.scalar
        def _(act):
            @turns(act, NT // 2)
            def _(i):
                for b in range(2):
                    t = 2 * i + b
                    act.wait_ge(mv_ok[b], i + 1)
                    act.activation(sd[:, b:b + 1], mv[:, b, 1:2], ACT.Sqrt, bias=eps_col[:, 0:1]).then_inc(sd_ok[b], 1)
                    act.wait_ge(turned[b], i + 1)
                    act.wait_ge(stored[b], 48 * i)
                    act.activation(xT[:, b, :, :].rearrange("p k n -> p (k n)"), pT[b][:, 0:KC * P],
                                   ACT.Copy).then_inc(xT_ok[b], 1)

        @block.tensor
        def _(pe):
            pe.wait_ge(weights_in, 48)
            for m in range(KC):
                for k in range(KC):
                    last = pe.matmul(pP[0][:, m * 2 * HT:(m + 1) * 2 * HT], wn_T[:, k, m * P:(m + 1) * P],
                                     lr[:, k, :], start=(k == 0), stop=(k == KC - 1))
            last.then_inc(scores_folded, 1)
            pe.wait_ge(wcat_ready, KC)
            @turns(pe, NT // 2)
            def _(i):
                for b in range(2):
                    t = 2 * i + b
                    pe.wait_ge(xn_ok[b], i + 1)
                    pe.wait_ge(xT_ok[b], i)
                    for k in range(KC):
                        last = pe.transpose(pT[b][:, k * P:(k + 1) * P], xn[:, b, k * P:(k + 1) * P], ident[:, :])
                    last.then_inc(turned[b], 1)
                    pe.wait_ge(xT_ok[b], i + 1)
                    pe.wait_ge(proj_ok[b], i)
                    for k in range(KC):
                        last = pe.matmul(pP[b][:, 0:WID], xT[:, b, k, :], wcat[:, k, :],
                                         start=(k == 0), stop=(k == KC - 1))
                    last.then_inc(projected[b], 1)


def mix_matrix(nc, xnT_d, w_kvT, w_q, w_oT, zeros, eps_col, mix):
    KV = 2 * INNER
    PAIRS = INNER // P
    GROUPS = KV // MDIM
    with ExitStack() as ctx:
        sb, ps, sem, sems, hold = tools(nc, ctx, "mix")
        wkv, wmean = sb("wkv", [P, KC, KV]), sb("wmean", [P, KC * GROUPS])
        wq, wo = sb("wq", [P, PAIRS, DIM]), sb("wo", [P, PAIRS, DIM])
        xT = sb("xT", [P, 2, KC * P])
        sq, var, sd = sb("sq", [P, 2, KV]), sb("var", [P, 2, GROUPS]), sb("sd", [P, 2, GROUPS])
        sdp, rr = sb("sdp", [P, 2, MHEADS]), sb("rr", [P, 2, MHEADS])
        kn, vc = sb("kn", [P, 2, INNER]), sb("vc", [P, 2, INNER])
        dT, t1 = sb("dotsT", [P, PAIRS, P]), sb("t1", [P, PAIRS, DIM])
        pkv = [[ps("k0"), ps("v0")], [ps("k1"), ps("v1")]]
        pdots, pm = ps("dots"), [ps("m0"), ps("m1")]
        weights_in, centre, centred = sem("weights_in"), sem("centre"), sem("centred")
        xT_in, kv_ok, sq_ok, var_ok, sd_ok, sdp_ok, rr_ok, kn_ok, vc_ok, dots_ok = (
            sems(n) for n in ("xT_in", "kv", "sq", "var", "sd", "sdp", "rr", "kn", "vc", "dots"))
        dots_done, dT_zero, dT_ok, t1_done, t1_ok, m_done, m_ok = (
            sem(n) for n in ("dots_done", "dT_zero", "dT_ok", "t1_done", "t1_ok", "m_done", "m_ok"))
        block = ctx.enter_context(nc.Block())

        @block.sync
        def _(sp):
            sp.dma_start(wkv[:, :, :], w_kvT.rearrange("(k p) n -> p k n", p=P)).then_inc(weights_in, 16)
            sp.dma_start(wq[:, :, :], w_q.rearrange("(k p) n -> p k n", p=P)).then_inc(weights_in, 16)
            sp.dma_start(wo[:, :, :], w_oT.rearrange("(k p) n -> p k n", p=P)).then_inc(weights_in, 16)
            @turns(sp, NT // 2)
            def _(i):
                for b in range(2):
                    t = 2 * i + b
                    sp.wait_ge(kv_ok[b], i)
                    hold(sp)
                    sp.dma_start(xT[:, b, :], xnT_d[ds(t, 1), :, :].rearrange("o p n -> (o p) n")).then_inc(xT_in[b], 16)

        @block.vector
        def _(dve):
            dve.wait_ge(weights_in, 48)
            w3 = wkv[:, :, :].rearrange("p k (g d) -> p (k g) d", d=MDIM)
            dve.tensor_reduce(wmean[:, :], w3, AX.X, ALU.add).then_inc(centre, 1)
            dve.wait_ge(centre, 1)
            dve.tensor_scalar(wmean[:, :], wmean[:, :], 1.0 / MDIM, None, ALU.mult).then_inc(centre, 1)
            dve.wait_ge(centre, 2)
            dve.tensor_tensor(w3, w3, wmean[:, :].rearrange("p (g o) -> p g o", o=1).to_broadcast([P, KC * GROUPS, MDIM]),
                              ALU.subtract).then_inc(centred, 1)
            @turns(dve, NT // 2)
            def _(i):
                for b in range(2):
                    t = 2 * i + b
                    dve.wait_ge(sq_ok[b], 2 * i + 2)
                    dve.tensor_reduce(var[:, b, :], sq[:, b, :].rearrange("p (g d) -> p g d", d=MDIM), AX.X,
                                      ALU.add).then_inc(var_ok[b], 1)
                    dve.wait_ge(sd_ok[b], i + 1)
                    dve.tensor_tensor(sdp[:, b, :], sd[:, b, 0:MHEADS], sd[:, b, MHEADS:GROUPS],
                                      ALU.mult).then_inc(sdp_ok[b], 1)
                    dve.wait_ge(sdp_ok[b], i + 1)
                    dve.reciprocal(rr[:, b, :], sdp[:, b, :]).then_inc(rr_ok[b], 1)
                    dve.wait_ge(rr_ok[b], i + 1)
                    dve.wait_ge(dots_ok[b], i)
                    dve.tensor_tensor(kn[:, b, :].rearrange("p (g d) -> p g d", d=MDIM),
                                      pkv[b][0][:, :].rearrange("p (g d) -> p g d", d=MDIM),
                                      rr[:, b, :].rearrange("p (g o) -> p g o", o=1).to_broadcast([P, MHEADS, MDIM]),
                                      ALU.mult).then_inc(kn_ok[b], 1)
            dve.memset(dT[:, :, :], 0.0).then_inc(dT_zero, 1)
            dve.wait_ge(dT_zero, 1)
            dve.wait_ge(dots_done, 1)
            pd = pdots[:, :].rearrange("p (q n) -> p q n", q=PAIRS)
            for h in range(2):
                s = slice(h * MDIM, (h + 1) * MDIM)
                dve.tensor_copy(dT[s, :, s], pd[s, :, s]).then_inc(dT_ok, 1)
            for q in range(PAIRS):
                dve.wait_ge(t1_done, q + 1)
                dve.tensor_copy(t1[:, q, :], pm[q % 2][:, 0:DIM]).then_inc(t1_ok, 1)
            for c in range(KC):
                dve.wait_ge(m_done, c + 1)
                dve.tensor_scalar(mix[:, c, :], pm[c][:, 0:DIM], 1.0 / NODES, None, ALU.mult).then_inc(m_ok, 1)

        @block.scalar
        def _(act):
            @turns(act, NT // 2)
            def _(i):
                for b in range(2):
                    t = 2 * i + b
                    act.wait_ge(kv_ok[b], i + 1)
                    act.wait_ge(var_ok[b], i)
                    for h in range(2):
                        act.activation(sq[:, b, h * INNER:(h + 1) * INNER], pkv[b][h][:, :], ACT.Square).then_inc(sq_ok[b], 1)
                    act.wait_ge(dots_ok[b], i)
                    act.activation(vc[:, b, :], pkv[b][1][:, :], ACT.Copy).then_inc(vc_ok[b], 1)
                    act.wait_ge(var_ok[b], i + 1)
                    act.activation(sd[:, b, :], var[:, b, :], ACT.Sqrt, bias=eps_col[:, 0:1],
                                   scale=1.0 / MDIM).then_inc(sd_ok[b], 1)

        @block.tensor
        def _(pe):
            pe.wait_ge(centred, 1)
            pe.matmul(pdots[:, :], zeros[:, 0:P], zeros[:, :], start=True, stop=False, skip_group_check=True)

            def dots(i, b):
                pe.wait_ge(kn_ok[b], i + 1)
                pe.wait_ge(vc_ok[b], i + 1)
                for q in range(PAIRS):
                    last = pe.matmul(pdots[:, q * P:(q + 1) * P], vc[:, b, q * P:(q + 1) * P],
                                     kn[:, b, q * P:(q + 1) * P], start=False, stop=False, skip_group_check=True)
                last.then_inc(dots_ok[b], 1)
                return last

            @turns(pe, NT // 2)
            def _(i):
                for b in range(2):
                    t = 2 * i + b
                    pe.wait_ge(xT_in[b], 16 * i + 16)
                    pe.wait_ge(kn_ok[b], i)
                    pe.wait_ge(vc_ok[b], i)
                    for h in range(2):
                        for k in range(KC):
                            last = pe.matmul(pkv[b][h][:, :], xT[:, b, k * P:(k + 1) * P],
                                             wkv[:, k, h * INNER:(h + 1) * INNER], start=(k == 0), stop=(k == KC - 1))
                    last.then_inc(kv_ok[b], 1)
                for b in range(2):
                    dots(i, b)
            pe.matmul(pdots[:, :], zeros[:, 0:P], zeros[:, :], start=False, stop=True,
                      skip_group_check=True).then_inc(dots_done, 1)
            pe.wait_ge(dT_ok, 2)
            for q in range(PAIRS):
                if q >= 2:
                    pe.wait_ge(t1_ok, q - 1)
                pe.matmul(pm[q % 2][:, 0:DIM], dT[:, q, :], wo[:, q, :], start=True, stop=True).then_inc(t1_done, 1)
            pe.wait_ge(t1_ok, PAIRS)
            for c in range(KC):
                for q in range(PAIRS):
                    last = pe.matmul(pm[c][:, 0:DIM], wq[:, q, c * P:(c + 1) * P], t1[:, q, :],
                                     start=(q == 0), stop=(q == PAIRS - 1))
                last.then_inc(m_done, 1)


def edges(nc, src, dst, dst_first, dst_last, dst_head, dst_tail, dst_before, dst_after, dst_cols, mask, epro, attn_m,
          ident, iota_row, iota_col, zeros, table, er_table, pens_d, agg_d):
    GA = NG + 2
    H, TT = GHEADS, TYPES
    with ExitStack() as ctx:
        sb, ps, sem, sems, hold = tools(nc, ctx, "edge")
        src_all, dst_i, dstf = sb("src_all", [P, NG, ET], I32), sb("dst_i", [P, NG, ET], I32), sb("dstf", [P, NG, ET])
        mask_all = sb("mask_all", [P, NG, ET, TT])
        first_i, last_i = sb("first_i", [P, GA], I32), sb("last_i", [P, GA], I32)
        first_f, wcol, span, last_ind = sb("first_f", [P, GA]), sb("wcol", [P, GA]), sb("span", [P, GA]), sb("last_ind", [P, GA])
        rel = sb("rel", [P, NG, ET])
        pen_prev, pen_next, pen_head, pen_tail = (sb(n, [P, NG, ET]) for n in ("pprev", "pnext", "phead", "ptail"))
        chain_i, chain_f = sb("chain_i", [GA, 4, P], I32), sb("chain_f", [GA, 4, P])
        chain_eq, chain_pen = sb("chain_eq", [GA, 3, P]), sb("chain_pen", [GA, 4, P])
        am = sb("am", [EPRO, HT])
        e0 = sb("e0", [1, P])
        dstb, oht, oh = sb("dstb", [P, 2, GROUP], I32), sb("oht", [P, 2, GROUP]), sb("oh", [P, 2, ET, P])
        ep, erw, pens = sb("ep", [EPRO, 2, GROUP]), sb("erw", [P, 2, HT]), sb("pens", [H, 2, 4, P])
        idx = sb("idx", [P, NBUF, ET], I32)
        G = sb("G", [P, NBUF, ET, ROW])
        penx, lastc = sb("penx", [P, 2, 2, H * ET]), sb("lastc", [P, 2])
        z, e, f1, b1, m, m2, q = (sb(n, [P, 2, w]) for n, w in (("z", ET * HT), ("e", H * ET), ("f1", H * ET), ("b1", H * ET),
                                                               ("m", H * ET), ("m2", H * ET), ("q", H * ET)))
        m3, uc, ud = sb("m3", [P, 2, H * ET]), sb("uc", [P, 2, H * ET]), sb("ud", [P, 2, H * ET])
        rb, lb, cc, dd = sb("rb", [H, 2, P + 1]), sb("lb", [H, 2, P + 1]), sb("cc", [H, 2, P]), sb("dd", [H, 2, P])
        fd, fac, cs = sb("fd", [1, 2, H]), sb("fac", [1, 2, H]), sb("cs", [1, 2, AGG])
        osum = sb("osum", [P, 2, AGG])
        pR, pA, pO, pC = [ps("R0"), ps("R1")], [ps("A0"), ps("A1")], [ps("O0"), ps("O1")], ps("C")
        pB = ps("B")

        indices_in, chain_in, small_in = sem("indices_in"), sem("chain_in"), sem("small_in")
        pre, chained, pens_stored = sem("pre"), sem("chained"), sem("pens_stored")
        ready = sem("ready")
        group_in, oht_ok, oh_ok, r_done, z_ok, zm_ok, s_ok, e_ok, f_ok, b_ok, m_ok, tails_up = (
            sems(n) for n in ("group_in", "oht", "oh", "r_done", "z", "zm", "s", "e", "f", "b", "m", "tails_up"))
        seed_ok, rscan_ok, lscan_ok, c_ok, d_ok, cd_up, uc_ok, ud_ok, m2_ok, m3_ok, q_ok, fd_ok, fac_ok, cs_ok = (
            sems(n) for n in ("seed", "rscan", "lscan", "c", "d", "cd_up", "uc", "ud", "m2", "m3", "q", "fd", "fac", "cs"))
        penx_ok, osum_ok, stored, carry_up = (sems(n) for n in ("penx", "osum", "stored", "carry_up"))
        idx_ok, gathered, p_ok, msg_ok, out_done = (sems(n, NBUF) for n in ("idx", "gathered", "p", "msg", "out_done"))

        def wait_sums_of_two_before(eng, i, b):
            eng.wait_ge(out_done[(b + 2) % 4], i + b // 2)

        block = ctx.enter_context(nc.Block())

        @block.sync
        def _(sp):
            sp.dma_start(src_all[:, :, :], src).then_inc(indices_in, 16)
            sp.dma_start(dst_i[:, :, :], dst).then_inc(indices_in, 16)
            sp.dma_start(first_i[:, :], dst_first.to_broadcast([P, GA])).then_inc(indices_in, 16)
            sp.dma_start(last_i[:, :], dst_last.to_broadcast([P, GA])).then_inc(indices_in, 16)
            for n, a in enumerate((dst_head, dst_tail, dst_before, dst_after)):
                sp.dma_start(chain_i[:, n, :], a).then_inc(chain_in, 16)
            sp.dma_start(mask_all[:, :, :, :], mask).then_inc(small_in, 16)
            sp.dma_start(am[:, :], attn_m).then_inc(small_in, 16)
            sp.wait_ge(chained, 1)
            sp.dma_start(pens_d.rearrange("g (k p) -> g k p", k=4), chain_pen[:, :, :]).then_inc(pens_stored, 16)
            sp.wait_ge(pens_stored, 16)

            def load(g, c, u):
                w = sp.value_load(dst_first[0:1, ds(g, 1)], min_val=0, max_val=NP - P)
                sp.wait_ge(oht_ok[c], u)
                hold(sp)
                sp.dma_start(dstb[:, c, :], dst_cols[ds(g, 1), :].to_broadcast([P, GROUP])).then_inc(group_in[c], 16)
                sp.wait_ge(r_done[c], u)
                hold(sp)
                sp.dma_start(ep[:, c, :], epro[:, ds(g * GROUP, GROUP)]).then_inc(group_in[c], 16)
                sp.dma_start(erw[:, c, :], er_table[ds(w, P), :]).then_inc(group_in[c], 16)
                sp.wait_ge(c_ok[c], u)
                sp.wait_ge(d_ok[c], u)
                hold(sp)
                sp.dma_start(pens[:, c, :, :], pens_d[ds(g, 1), :].rearrange("g (k p) -> g k p", k=4)
                             .to_broadcast([H, 4, P])).then_inc(group_in[c], 16)

            load(0, 0, 0)
            load(1, 1, 0)
            @turns(sp, NG // 4)
            def _(i):
                for b in range(4):
                    g, c, u = 4 * i + b, b % 2, 2 * i + b // 2
                    w = sp.value_load(dst_first[0:1, ds(g, 1)], min_val=0, max_val=NP - P)
                    sp.wait_ge(osum_ok[c], u + 1)
                    hold(sp)
                    sp.wait_ge(stored[1 - c], 16 * (2 * i + (b + 1) // 2))
                    hold(sp)
                    sp.dma_start(agg_d[ds(w, P), :], osum[:, c, :]).then_inc(stored[c], 16)
                    load(g + 2, c, u + 1)
            for c in range(2):
                sp.wait_ge(stored[c], 16 * (NG // 2))
                sp.wait_ge(group_in[c], 64 * (NG // 2 + 1))

        @block.gpsimd
        def _(pool):
            pool.wait_ge(indices_in, 64)
            @turns(pool, NG // 4)
            def _(i):
                for b in range(4):
                    g = 4 * i + b
                    pool.wait_ge(out_done[b], i)
                    pool.tensor_copy(idx[:, b, :], src_all[:, ds(g, 1), :].rearrange("p o t -> p (o t)")).then_inc(idx_ok[b], 1)
                    pool.wait_ge(idx_ok[b], i + 1)
                    hold(pool)
                    for t in range(ET):
                        pool.indirect_dma_start(G[:, b, t, :], None, table, bass.IndirectOffsetOnAxis(idx[:, b, t:t + 1], 0)
                                                ).then_inc(gathered[b], 16)

        @block.vector
        def _(dve):
            dve.wait_ge(indices_in, 64)
            n = 0

            def then(ins):
                nonlocal n
                n += 1
                ins.then_inc(pre, 1)
                dve.wait_ge(pre, n)

            then(dve.tensor_copy(dstf[:, :, :], dst_i[:, :, :]))
            then(dve.tensor_copy(first_f[:, :], first_i[:, :]))
            then(dve.tensor_copy(span[:, :], last_i[:, :]))
            then(dve.tensor_tensor(span[:, :], span[:, :], first_f[:, :], ALU.subtract))
            then(dve.tensor_scalar(last_ind[:, :], span[:, :], iota_col[:, 0:1], None, ALU.is_equal))
            then(dve.tensor_scalar(wcol[:, :], first_f[:, :], iota_col[:, 0:1], None, ALU.add))
            then(dve.tensor_tensor(rel[:, :, :], dstf[:, :, :], first_f[:, 0:NG].rearrange("p (g o) -> p g o", o=1)
                                   .to_broadcast([P, NG, ET]), ALU.subtract))
            then(dve.memset(pen_prev[:, :, :], 0.0))
            then(dve.memset(pen_next[:, :, :], 0.0))
            then(dve.tensor_tensor(pen_prev[:, :, 1:ET], dstf[:, :, 1:ET], dstf[:, :, 0:ET - 1], ALU.is_equal))
            then(dve.tensor_tensor(pen_next[:, :, 0:ET - 1], dstf[:, :, 1:ET], dstf[:, :, 0:ET - 1], ALU.is_equal))
            then(dve.tensor_tensor(pen_head[:, :, :], dstf[:, :, :], dstf[:, :, 0:1].to_broadcast([P, NG, ET]), ALU.is_equal))
            then(dve.tensor_tensor(pen_tail[:, :, :], dstf[:, :, :], dstf[:, :, ET - 1:ET].to_broadcast([P, NG, ET]), ALU.is_equal))
            for a in (pen_prev, pen_next, pen_head, pen_tail):
                then(dve.tensor_scalar(a[:, :, :], a[:, :, :], -1.0, BIG, ALU.add, ALU.mult))
            dve.wait_ge(chain_in, 64)
            then(dve.tensor_copy(chain_f[:, :, :], chain_i[:, :, :]))
            head, tail, before, after = (chain_f[:, k, :] for k in range(4))
            for k, (x0, x1) in enumerate(((head, before), (tail, after), (head, tail))):
                then(dve.tensor_tensor(chain_eq[:, k, :], x0, x1, ALU.is_equal))
            then(dve.tensor_scalar(chain_eq[:, :, :], chain_eq[:, :, :], -1.0, BIG, ALU.add, ALU.mult))
            then(dve.tensor_copy(chain_pen[:, 0:2, :], chain_eq[:, 0:2, :]))
            then(dve.tensor_tensor(chain_pen[:, 2:4, :], chain_eq[:, 0:2, :], chain_eq[:, 2:3, :].to_broadcast([GA, 2, P]), ALU.add))
            dve.memset(e0[:, :], 0.0).then_inc(chained, 1)
            then(dve.memset(rb[:, :, :], -BIG))
            then(dve.memset(lb[:, :, :], -BIG))
            dve.wait_ge(chained, 1)
            dve.memset(e0[:, 0:1], 1.0).then_inc(ready, 1)
            dve.wait_ge(small_in, 32)

            def one_hot_nodes(g, c, u):
                dve.wait_ge(group_in[c], 64 * u + 64)
                dve.wait_ge(r_done[c], u)
                dve.tensor_scalar(oht[:, c, :], dstb[:, c, :], wcol[:, ds(g, 1)], None, ALU.is_equal).then_inc(oht_ok[c], 1)

            one_hot_nodes(0, 0, 0)
            @turns(dve, NG // 4)
            def _(i):
                for b in range(4):
                    g, c, u = 4 * i + b, b % 2, 2 * i + b // 2
                    dve.wait_ge(gathered[b], 16 * ET * (i + 1))
                    dve.wait_ge(r_done[c], u + 1)
                    z3 = z[:, c, :].rearrange("p (t n) -> p t n", t=ET)
                    dve.tensor_tensor(z3, G[:, b, :, DIM:ROW], pR[c][:, 0:ET * HT].rearrange("p (t n) -> p t n", t=ET),
                                      ALU.add).then_inc(z_ok[c], 1)
                    dve.wait_ge(z_ok[c], u + 1)
                    z4 = z[:, c, :].rearrange("p (t h y) -> p t h y", t=ET, h=H)
                    mk = mask_all[:, ds(g, 1), :, :].rearrange("p o t (h y) -> p (o t) h y", h=1).to_broadcast([P, ET, H, TT])
                    dve.tensor_tensor(z4, z4, mk, ALU.mult).then_inc(zm_ok[c], 1)
                    dve.wait_ge(zm_ok[c], u + 1)
                    e_th = e[:, c, :].rearrange("p (h t) -> p t h", h=H)
                    dve.tensor_reduce(e_th, z4, AX.X, ALU.add).then_inc(s_ok[c], 1)
                    dve.wait_ge(s_ok[c], u + 1)
                    dve.scalar_tensor_tensor(e[:, c, :], e[:, c, :], SLOPE, e[:, c, :], ALU.mult, ALU.max).then_inc(e_ok[c], 1)
                    dve.wait_ge(e_ok[c], u + 1)
                    dve.wait_ge(penx_ok[c], 2 * u + 2)
                    dve.tensor_tensor_scan(f1[:, c, :], penx[:, c, 0, :], e[:, c, :], -BIG, ALU.add, ALU.max).then_inc(f_ok[c], 1)
                    dve.tensor_tensor_scan(b1[:, c, ::-1], penx[:, c, 1, ::-1], e[:, c, ::-1], -BIG, ALU.add, ALU.max).then_inc(b_ok[c], 1)
                    wait_sums_of_two_before(dve, i, b)
                    dve.tensor_tensor(oh[:, c, :, :], iota_row[:, :].rearrange("p (o n) -> p o n", o=1).to_broadcast([P, ET, P]),
                                      rel[:, ds(g, 1), :].rearrange("p o (t n) -> p (o t) n", n=1).to_broadcast([P, ET, P]),
                                      ALU.is_equal).then_inc(oh_ok[c], 1)
                    dve.wait_ge(b_ok[c], u + 1)
                    dve.tensor_tensor(m[:, c, :], f1[:, c, :], b1[:, c, :], ALU.max).then_inc(m_ok[c], 1)
                    dve.wait_ge(rscan_ok[1 - c], 2 * i + (b + 1) // 2)
                    dve.tensor_copy(rb[:, c, 0:1], rb[:, 1 - c, P:P + 1]).then_inc(seed_ok[c], 1)
                    dve.wait_ge(tails_up[c], u + 1)
                    dve.tensor_tensor_scan(rb[:, c, 1:P + 1], pens[:, c, 2, :], pA[c][0:H, 0:P], rb[:, 1 - c, P:P + 1],
                                           ALU.add, ALU.max).then_inc(rscan_ok[c], 1)
                    dve.tensor_tensor_scan(lb[:, c, P - 1::-1], pens[:, c, 3, ::-1], pA[c][0:H, 2 * P - 1:P - 1:-1], -BIG,
                                           ALU.add, ALU.max).then_inc(lscan_ok[c], 1)
                    dve.wait_ge(rscan_ok[c], u + 1)
                    dve.wait_ge(seed_ok[c], u + 1)
                    dve.wait_ge(cd_up[c], u)
                    dve.tensor_tensor(cc[:, c, :], rb[:, c, 0:P], pens[:, c, 0, :], ALU.add).then_inc(c_ok[c], 1)
                    dve.wait_ge(lscan_ok[c], u + 1)
                    dve.tensor_tensor(dd[:, c, :], lb[:, c, 1:P + 1], pens[:, c, 1, :], ALU.add).then_inc(d_ok[c], 1)
                    one_hot_nodes(g + 1, 1 - c, 2 * i + (b + 1) // 2)
                    dve.wait_ge(cd_up[c], u + 1)
                    m_ht = [a[:, c, :].rearrange("p (h t) -> p h t", h=H) for a in (m, uc, ud, m2, m3)]
                    pc = [pB[:, c * 2 * H + k * H:c * 2 * H + (k + 1) * H].rearrange("p (h o) -> p h o", o=1).to_broadcast([P, H, ET]) for k in range(2)]
                    pen = [a[:, ds(g, 1), :].to_broadcast([P, H, ET]) for a in (pen_head, pen_tail)]
                    dve.tensor_tensor(m_ht[1], pen[0], pc[0], ALU.add).then_inc(uc_ok[c], 1)
                    dve.tensor_tensor(m_ht[2], pen[1], pc[1], ALU.add).then_inc(ud_ok[c], 1)
                    dve.wait_ge(uc_ok[c], u + 1)
                    dve.wait_ge(m_ok[c], u + 1)
                    dve.tensor_tensor(m2[:, c, :], m[:, c, :], uc[:, c, :], ALU.max).then_inc(m2_ok[c], 1)
                    dve.wait_ge(ud_ok[c], u + 1)
                    dve.wait_ge(m2_ok[c], u + 1)
                    dve.tensor_tensor(m3[:, c, :], m2[:, c, :], ud[:, c, :], ALU.max).then_inc(m3_ok[c], 1)
                    dve.wait_ge(m3_ok[c], u + 1)
                    dve.tensor_tensor(q[:, c, :], e[:, c, :], m3[:, c, :], ALU.subtract).then_inc(q_ok[c], 1)
                    dve.tensor_tensor(fd[:, c, :], pB[0:1, c * 2 * H:c * 2 * H + H], m_ht[4][0:1, :, 0], ALU.subtract).then_inc(fd_ok[c], 1)
                    dve.wait_ge(fac_ok[c], u + 1)
                    dve.wait_ge(carry_up[1 - c], 2 * i + (b + 1) // 2 + 1 - c)
                    wait_sums_of_two_before(dve, i, b)
                    dve.tensor_tensor(cs[:, c, 0:DIM].rearrange("p (h d) -> p h d", h=H), pC[0:1, 0:DIM].rearrange("p (h d) -> p h d", h=H),
                                      fac[:, c, :].rearrange("p (h o) -> p h o", o=1).to_broadcast([1, H, GDIM]), ALU.mult).then_inc(cs_ok[c], 1)
                    dve.tensor_tensor(cs[:, c, DIM:AGG], pC[0:1, DIM:AGG], fac[:, c, :], ALU.mult).then_inc(cs_ok[c], 1)
                    dve.wait_ge(p_ok[b], i + 1)
                    g4 = G[:, b, :, 0:DIM].rearrange("p t (h d) -> p t h d", h=H)
                    dve.tensor_tensor(g4, g4, G[:, b, :, DIM:AGG].rearrange("p t (h o) -> p t h o", o=1)
                                      .to_broadcast([P, ET, H, GDIM]), ALU.mult).then_inc(msg_ok[b], 1)

        @block.scalar
        def _(act):
            act.wait_ge(ready, 1)
            @turns(act, NG // 4)
            def _(i):
                for b in range(4):
                    g, c, u = 4 * i + b, b % 2, 2 * i + b // 2
                    act.wait_ge(b_ok[c], u)
                    for k, a in enumerate((pen_prev, pen_next)):
                        act.activation(penx[:, c, k, :].rearrange("p (h t) -> p h t", h=H), a[:, ds(g, 1), :].to_broadcast([P, H, ET]),
                                       ACT.Copy).then_inc(penx_ok[c], 1)
                    act.wait_ge(carry_up[c], u + c)
                    act.activation(lastc[:, c:c + 1], last_ind[:, ds(g, 1)], ACT.Copy)
                    act.wait_ge(q_ok[c], u + 1)
                    act.activation(G[:, b, :, DIM:AGG].rearrange("p t h -> p h t"), q[:, c, :].rearrange("p (h t) -> p h t", h=H),
                                   ACT.Exp, scale=1.0 / 3).then_inc(p_ok[b], 1)
                    act.wait_ge(fd_ok[c], u + 1)
                    act.wait_ge(cs_ok[c], 2 * u)
                    act.activation(fac[:, c, :], fd[:, c, :], ACT.Exp, scale=1.0 / 3).then_inc(fac_ok[c], 1)
                    act.wait_ge(out_done[b], i + 1)
                    act.wait_ge(stored[c], 16 * u)
                    act.wait_ge(carry_up[c], u + c)
                    act.activation(osum[:, c, :], pO[c][:, 0:AGG], ACT.Copy).then_inc(osum_ok[c], 1)

        @block.tensor
        def _(pe):
            pe.wait_ge(ready, 1)
            pe.wait_ge(small_in, 32)

            def scores(c, u):
                pe.wait_ge(oht_ok[c], u + 1)
                pe.wait_ge(group_in[c], 64 * u + 64)
                pe.wait_ge(z_ok[c], u)
                for t in range(ET):
                    o = pR[c][:, t * HT:(t + 1) * HT]
                    pe.matmul(o, ep[:, c, t * P:(t + 1) * P], am[:, :], start=True, stop=False)
                    last = pe.matmul(o, oht[:, c, t * P:(t + 1) * P], erw[:, c, :], start=False, stop=True)
                last.then_inc(r_done[c], 1)

            pe.matmul(pC[0:1, 0:AGG], zeros[:, 0:1], zeros[:, 0:AGG], start=True, stop=True).then_inc(carry_up[1], 1)
            scores(0, 0)
            @turns(pe, NG // 4)
            def _(i):
                for b in range(4):
                    g, c, u = 4 * i + b, b % 2, 2 * i + b // 2
                    ends = [a[:, c, :].rearrange("p (h t) -> p h t", h=H) for a in (f1, b1)]
                    pe.wait_ge(f_ok[c], u + 1)
                    pe.wait_ge(b_ok[c], u + 1)
                    pe.wait_ge(rscan_ok[c], u)
                    pe.wait_ge(lscan_ok[c], u)
                    pe.transpose(pA[c][0:H, 0:P], ends[0][:, :, ET - 1], ident[:, :])
                    pe.transpose(pA[c][0:H, P:2 * P], ends[1][:, :, 0], ident[:, :]).then_inc(tails_up[c], 1)
                    pe.wait_ge(c_ok[c], u + 1)
                    pe.wait_ge(d_ok[c], u + 1)
                    pe.wait_ge(fd_ok[c], u)
                    pe.wait_ge(ud_ok[c], u)
                    hold(pe)
                    pe.transpose(pB[:, c * 2 * H:c * 2 * H + H], cc[:, c, :], ident[0:H, 0:H])
                    pe.transpose(pB[:, c * 2 * H + H:c * 2 * H + 2 * H], dd[:, c, :], ident[0:H, 0:H]).then_inc(cd_up[c], 1)
                    scores(1 - c, 2 * i + (b + 1) // 2)
                    pe.wait_ge(msg_ok[b], i + 1)
                    pe.wait_ge(oh_ok[c], u + 1)
                    pe.wait_ge(osum_ok[c], u)
                    for t in range(ET):
                        pe.matmul(pO[c][:, 0:AGG], oh[:, c, t, :], G[:, b, t, 0:AGG], start=(t == 0), stop=False)
                    pe.wait_ge(cs_ok[c], 2 * u + 2)
                    pe.matmul(pO[c][:, 0:AGG], e0[:, :], cs[:, c, :], start=False, stop=True).then_inc(out_done[b], 1)
                    pe.wait_ge(osum_ok[c], u + 1)
                    pe.matmul(pC[0:1, 0:AGG], lastc[:, c:c + 1], osum[:, c, :], start=True, stop=True).then_inc(carry_up[c], 1)


def feed_forward(nc, x, xnT_d, agg_d, mix, b_out, router, w1T, w3T, w2T, ident, eps_col, out):
    E = EXPERTS
    x2_d = nc.dram_tensor("x_after_mixing", [NP, DIM], F32).ap()
    xT2_d = nc.dram_tensor("xn2_transposed", [NT, P, KC * P], F32).ap()
    with ExitStack() as outer:
        gates = outer.enter_context(nc.sbuf_tensor("gates", [P, NT, E], F32))
        combine(nc, x, xnT_d, agg_d, mix, b_out, router, ident, eps_col, x2_d, xT2_d, gates)
        experts(nc, x2_d, xT2_d, w1T, w3T, w2T, gates, out)


def combine(nc, x, xnT_d, agg_d, mix, b_out, router, ident, eps_col, x2_d, xT2_d, gates):
    E = EXPERTS
    with ExitStack() as ctx:
        sb, ps, sem, sems, hold = tools(nc, ctx, "comb")
        xt, ag, xT = sb("x", [P, 2, DIM]), sb("agg", [P, 2, AGG]), sb("xT", [P, 2, KC * P])
        bias, rw, iota8 = sb("bias", [P, DIM]), sb("rw", [P, KC, E]), sb("iota8", [P, E])
        iota8_i = sb("iota8_i", [P, E], I32)
        den, rden, gr, x2 = sb("den", [P, 2, GHEADS]), sb("rden", [P, 2, GHEADS]), sb("gr", [P, 2, DIM]), sb("x2", [P, 2, DIM])
        xa, xb = sb("xa", [P, 2, DIM]), sb("xb", [P, 2, DIM])
        stats, mv, sd, rs = sb("stats", [P, 2, 6]), sb("mv", [P, 2, 2]), sb("sd", [P, 2]), sb("rs", [P, 2])
        xn, xT2 = sb("xn", [P, 2, DIM]), sb("xT2", [P, 2, KC * P])
        lg, top, nm, pr, sm, rsm = sb("lg", [P, 2, E]), sb("top", [P, 2, E]), sb("nm", [P, 2]), sb("pr", [P, 2, E]), sb("sm", [P, 2]), sb("rsm", [P, 2])
        topi, topf = sb("topi", [P, 2, E], mybir.dt.uint32), sb("topf", [P, 2, E])
        oh = sb("oh", [P, 2, 2, E])
        prn, tp, dn, rdn, gt = sb("prn", [P, 2, E]), sb("tp", [P, 2, E]), sb("dn", [P, 2]), sb("rdn", [P, 2]), sb("gt", [P, 2, E])
        pm, pT, pl = [ps("m0"), ps("m1")], [ps("T0"), ps("T1")], [ps("l0"), ps("l1")]
        const_in, counted, iota_ok = sem("const_in"), sem("counted"), sem("iota_ok")
        tile_in, mixed, turned, xT2_ok, routed, stored, sd_ok, x2_ok, xn_ok, mv_ok, pr_ok, nm_ok, lg_ok = (
            sems(n) for n in ("tile_in", "mixed", "turned", "xT2", "routed", "stored", "sd", "x2", "xn", "mv", "pr", "nm", "lg"))
        own = sems("own")
        OWN = 21
        block = ctx.enter_context(nc.Block())

        @block.sync
        def _(sp):
            sp.dma_start(bias[:, :], b_out.to_broadcast([P, DIM])).then_inc(const_in, 16)
            sp.dma_start(rw[:, :, :], router.rearrange("(k p) e -> p k e", p=P)).then_inc(const_in, 16)
            @turns(sp, NT // 2)
            def _(i):
                for b in range(2):
                    t = 2 * i + b
                    sp.wait_ge(x2_ok[b], i)
                    hold(sp)
                    sp.dma_start(xt[:, b, :], x[ds(t * P, P), :]).then_inc(tile_in[b], 16)
                    sp.dma_start(ag[:, b, :], agg_d[ds(t * P, P), :]).then_inc(tile_in[b], 16)
                    sp.dma_start(xT[:, b, :], xnT_d[ds(t, 1), :, :].rearrange("o p n -> (o p) n")).then_inc(tile_in[b], 16)

        @block.gpsimd
        def _(pool):
            pool.iota(iota8_i[:, :], [[1, E]], base=0, channel_multiplier=0).then_inc(counted, 1)
            @turns(pool, NT // 2)
            def _(i):
                for b in range(2):
                    t = 2 * i + b
                    pool.wait_ge(x2_ok[b], i + 1)
                    pool.dma_start(x2_d[ds(t * P, P), :], x2[:, b, :]).then_inc(stored[b], 16)
                    pool.wait_ge(xT2_ok[b], i + 1)
                    pool.dma_start(xT2_d[ds(t, 1), :, :].rearrange("o p n -> (o p) n"), xT2[:, b, :]).then_inc(stored[b], 16)
            for b in range(2):
                pool.wait_ge(stored[b], 32 * (NT // 2))

        @block.vector
        def _(dve):
            dve.wait_ge(counted, 1)
            dve.tensor_copy(iota8[:, :], iota8_i[:, :]).then_inc(iota_ok, 1)
            dve.wait_ge(iota_ok, 1)
            dve.wait_ge(const_in, 32)
            @turns(dve, NT // 2)
            def _(i):
                for b in range(2):
                    t = 2 * i + b
                    n = 0

                    def then(ins):
                        nonlocal n
                        n += 1
                        ins.then_inc(own[b], 1)
                        dve.wait_ge(own[b], OWN * i + n)

                    col = lambda a: a[:, b:b + 1]
                    dve.wait_ge(tile_in[b], 48 * i + 48)
                    then(dve.tensor_scalar(den[:, b, :], ag[:, b, DIM:AGG], 1e-30, None, ALU.max))
                    then(dve.reciprocal(rden[:, b, :], den[:, b, :]))
                    then(dve.tensor_tensor(gr[:, b, :].rearrange("p (h d) -> p h d", h=GHEADS), ag[:, b, 0:DIM].rearrange("p (h d) -> p h d", h=GHEADS),
                                           rden[:, b, :].rearrange("p (h o) -> p h o", o=1).to_broadcast([P, GHEADS, GDIM]), ALU.mult))
                    then(dve.tensor_tensor(xa[:, b, :], gr[:, b, :], xt[:, b, :], ALU.add))
                    dve.wait_ge(mixed[b], i + 1)
                    then(dve.tensor_tensor(xb[:, b, :], pm[b][:, 0:DIM], bias[:, :], ALU.add))
                    dve.wait_ge(stored[b], 32 * i)
                    dve.tensor_tensor(x2[:, b, :], xa[:, b, :], xb[:, b, :], ALU.add).then_inc(x2_ok[b], 1)
                    dve.wait_ge(x2_ok[b], i + 1)
                    then(dve.bn_stats(stats[:, b, :], x2[:, b, :]))
                    hold(dve)
                    dve.bn_aggr(mv[:, b, :], stats[:, b, :]).then_inc(mv_ok[b], 1)
                    dve.wait_ge(sd_ok[b], i + 1)
                    then(dve.reciprocal(col(rs), col(sd)))
                    dve.wait_ge(turned[b], i)
                    dve.tensor_scalar(xn[:, b, :], x2[:, b, :], mv[:, b, 0:1], col(rs), ALU.subtract, ALU.mult).then_inc(xn_ok[b], 1)
                    dve.wait_ge(routed[b], i + 1)
                    dve.tensor_copy(lg[:, b, :], pl[b][:, 0:E]).then_inc(lg_ok[b], 1)
                    dve.wait_ge(lg_ok[b], i + 1)
                    hold(dve)
                    then(dve.max(top[:, b, :], lg[:, b, :]))
                    hold(dve)
                    then(dve.max_index(topi[:, b, :], top[:, b, :], lg[:, b, :]))
                    then(dve.tensor_copy(topf[:, b, :], topi[:, b, :]))
                    dve.tensor_scalar(col(nm), top[:, b, 0:1], -1.0, None, ALU.mult).then_inc(nm_ok[b], 1)
                    dve.wait_ge(pr_ok[b], i + 1)
                    then(dve.tensor_reduce(col(sm), pr[:, b, :], AX.X, ALU.add))
                    then(dve.reciprocal(col(rsm), col(sm)))
                    then(dve.tensor_scalar(prn[:, b, :], pr[:, b, :], col(rsm), None, ALU.mult))
                    for k in range(2):
                        then(dve.tensor_scalar(oh[:, b, k, :], iota8[:, :], topf[:, b, k:k + 1], None, ALU.is_equal))
                    then(dve.tensor_tensor(tp[:, b, :], oh[:, b, 0, :], oh[:, b, 1, :], ALU.add))
                    then(dve.tensor_tensor(gt[:, b, :], tp[:, b, :], prn[:, b, :], ALU.mult))
                    then(dve.tensor_reduce(col(dn), gt[:, b, :], AX.X, ALU.add))
                    then(dve.tensor_scalar(col(rdn), col(dn), 1e-9, None, ALU.add))
                    then(dve.reciprocal(col(dn), col(rdn)))
                    then(dve.tensor_scalar(gates[:, ds(t, 1), :].rearrange("p o e -> p (o e)"), gt[:, b, :], col(dn), None, ALU.mult))
                    assert n == OWN, n

        @block.scalar
        def _(act):
            @turns(act, NT // 2)
            def _(i):
                for b in range(2):
                    act.wait_ge(mv_ok[b], i + 1)
                    act.activation(sd[:, b:b + 1], mv[:, b, 1:2], ACT.Sqrt, bias=eps_col[:, 0:1]).then_inc(sd_ok[b], 1)
                    act.wait_ge(turned[b], i + 1)
                    act.wait_ge(stored[b], 32 * i)
                    act.activation(xT2[:, b, :], pT[b][:, 0:KC * P], ACT.Copy).then_inc(xT2_ok[b], 1)
                    act.wait_ge(nm_ok[b], i + 1)
                    act.activation(pr[:, b, :], lg[:, b, :], ACT.Exp, bias=nm[:, b:b + 1]).then_inc(pr_ok[b], 1)

        @block.tensor
        def _(pe):
            pe.wait_ge(const_in, 32)
            @turns(pe, NT // 2)
            def _(i):
                for b in range(2):
                    pe.wait_ge(tile_in[b], 48 * i + 48)
                    pe.wait_ge(x2_ok[b], i)
                    for k in range(KC):
                        last = pe.matmul(pm[b][:, 0:DIM], xT[:, b, k * P:(k + 1) * P], mix[:, k, :], start=(k == 0), stop=(k == KC - 1))
                    last.then_inc(mixed[b], 1)
                    pe.wait_ge(xn_ok[b], i + 1)
                    pe.wait_ge(xT2_ok[b], i)
                    for k in range(KC):
                        last = pe.transpose(pT[b][:, k * P:(k + 1) * P], xn[:, b, k * P:(k + 1) * P], ident[:, :])
                    last.then_inc(turned[b], 1)
                    pe.wait_ge(xT2_ok[b], i + 1)
                    pe.wait_ge(lg_ok[b], i)
                    for k in range(KC):
                        last = pe.matmul(pl[b][:, 0:E], xT2[:, b, k * P:(k + 1) * P], rw[:, k, :], start=(k == 0), stop=(k == KC - 1))
                    last.then_inc(routed[b], 1)


def experts(nc, x2_d, xT2_d, w1T, w3T, w2T, gates, out):
    E, B = EXPERTS, 3 * P
    with ExitStack() as ctx:
        sb, ps, sem, sems, hold = tools(nc, ctx, "ffn")
        w1, w3, w2 = sb("w1", [P, E, KC, HP]), sb("w3", [P, E, KC, HP]), sb("w2", [HW, E, HC, DIM])
        xT, acc = sb("xT", [P, 2, KC * P]), sb("acc", [P, 2, DIM])
        s1, h = sb("s1", [HW, 2, B]), sb("h", [HW, 2, 2, B])
        ph1, ph3, py = [ps("h1a"), ps("h1b")], [ps("h3a"), ps("h3b")], [ps("y0"), ps("y1")]
        w_in = sem("w_in")
        tile_in, stored, acc_ok, own = (sems(n) for n in ("tile_in", "stored", "acc", "own"))
        h_up, s_ok, h_ok, y_up, y_used = (sems(n) for n in ("h_up", "s", "h", "y_up", "y_used"))
        block = ctx.enter_context(nc.Block())

        @block.sync
        def _(sp):
            for e in range(E):
                sp.dma_start(w1[:, e, :, :], w1T[e].rearrange("(k p) n -> p k n", p=P)).then_inc(w_in, 16)
                sp.dma_start(w3[:, e, :, :], w3T[e].rearrange("(k p) n -> p k n", p=P)).then_inc(w_in, 16)
                sp.dma_start(w2[:, e, :, :], w2T[e].rearrange("(k p) n -> p k n", p=HW)).then_inc(w_in, 16)
            @turns(sp, NT // 2)
            def _(i):
                for b in range(2):
                    t = 2 * i + b
                    sp.wait_ge(stored[b], 16 * i)
                    hold(sp)
                    sp.dma_start(xT[:, b, :], xT2_d[ds(t, 1), :, :].rearrange("o p n -> (o p) n")).then_inc(tile_in[b], 16)
                    sp.dma_start(acc[:, b, :], x2_d[ds(t * P, P), :]).then_inc(tile_in[b], 16)

        @block.gpsimd
        def _(pool):
            @turns(pool, NT // 2)
            def _(i):
                for b in range(2):
                    t = 2 * i + b
                    pool.wait_ge(acc_ok[b], E * (i + 1))
                    pool.dma_start(out[ds(t * P, P), :], acc[:, b, :]).then_inc(stored[b], 16)
            for b in range(2):
                pool.wait_ge(stored[b], 16 * (NT // 2))

        @block.tensor
        def _(pe):
            pe.wait_ge(w_in, 48 * E)
            @turns(pe, NT // 2)
            def _(i):
                for b in range(2):
                    pe.wait_ge(tile_in[b], 32 * i + 32)
                    for e in range(E):
                        step = (2 * i + b) * E + e
                        for f in range(2):
                            pe.wait_ge(h_ok[f], step)
                            for w, p in ((w1, ph1), (w3, ph3)):
                                for m in range(3):
                                    for k in range(KC):
                                        c0 = (3 * f + m) * HW
                                        last = pe.matmul(p[f][0:HW, m * P:(m + 1) * P], w[:, e, k, c0:c0 + HW], xT[:, b, k * P:(k + 1) * P],
                                                         start=(k == 0), stop=(k == KC - 1))
                            last.then_inc(h_up[f], 1)
                        y = e % 2
                        pe.wait_ge(y_used[y], (2 * i + b) * (E // 2) + e // 2)
                        for f in range(2):
                            pe.wait_ge(h_ok[f], step + 1)
                            for m in range(3):
                                last = pe.matmul(py[y][:, 0:DIM], h[:, y, f, m * P:(m + 1) * P], w2[:, e, 3 * f + m, :],
                                                 start=(f == 0 and m == 0), stop=(f == 1 and m == 2))
                        last.then_inc(y_up[y], 1)

        @block.scalar
        def _(act):
            @turns(act, NT // 2)
            def _(i):
                for b in range(2):
                    for e in range(E):
                        step = (2 * i + b) * E + e
                        for f in range(2):
                            act.wait_ge(h_up[f], step + 1)
                            act.wait_ge(h_ok[f], step)
                            act.activation(s1[:, f, :], ph1[f][0:HW, 0:B], ACT.Silu).then_inc(s_ok[f], 1)

        @block.vector
        def _(dve):
            @turns(dve, NT // 2)
            def _(i):
                for b in range(2):
                    t = 2 * i + b
                    dve.wait_ge(tile_in[b], 32 * i + 32)

                    def add_y(e):
                        y = e % 2
                        dve.wait_ge(y_up[y], (2 * i + b) * (E // 2) + e // 2 + 1)
                        if e:
                            dve.wait_ge(acc_ok[b], E * i + e)
                        dve.scalar_tensor_tensor(acc[:, b, :], py[y][:, 0:DIM], gates[:, ds(t, 1), e:e + 1].rearrange("p o e -> p (o e)"), acc[:, b, :],
                                                 ALU.mult, ALU.add).then_inc(acc_ok[b], 1)
                        dve.wait_ge(acc_ok[b], E * i + e + 1)
                        dve.sem_inc(y_used[y], 1)

                    for e in range(E):
                        step = (2 * i + b) * E + e
                        for f in range(2):
                            dve.wait_ge(s_ok[f], step + 1)
                            dve.tensor_tensor(h[:, e % 2, f, :], s1[:, f, :], ph3[f][0:HW, 0:B], ALU.mult).then_inc(h_ok[f], 1)
                        if e:
                            add_y(e - 1)
                    add_y(E - 1)


_OUT = (NODES, DIM)


def kernel(**inputs):
    import concourse.bacc as bacc
    from concourse.bass_utils import run_bass_kernel_spmd

    a = {k: np.asarray(v) for k, v in inputs.items()}

    def rows(v, n):
        return np.concatenate([v, np.zeros((n - v.shape[0],) + v.shape[1:], v.dtype)])

    src = rows(a["src"], EP)
    dst = np.concatenate([a["dst"], np.full(EP - EDGES, NODES, a["dst"].dtype)])
    grouped = dst.reshape(NG, P, ET)
    head, tail = grouped[:, :, 0].reshape(-1), grouped[:, :, -1].reshape(-1)
    before = np.concatenate([np.full(1, -1, dst.dtype), tail[:-1]])
    after = np.concatenate([head[1:], np.full(1, -1, dst.dtype)])
    chain = [rows(v.reshape(NG, P), NG + 2) for v in (head, tail, before, after)]
    first, last = rows(grouped[:, 0, 0], NG + 2)[None], rows(grouped[:, -1, -1], NG + 2)[None]
    columns = rows(grouped.transpose(0, 2, 1).reshape(NG, GROUP), NG + 2)
    mask = rows(a["edge_attr_4"], EP).reshape(NG, P, ET, TYPES).transpose(1, 0, 2, 3)
    epro = rows(rows(a["edge_attr_16"], EP).reshape(NG, P, ET, EPRO).transpose(0, 2, 1, 3).reshape(NG, GROUP, EPRO), NG + 2)
    epro = epro.reshape((NG + 2) * GROUP, EPRO).T
    lr = np.zeros((GHEADS, GDIM, 2, GHEADS, TYPES), np.float32)
    for h in range(GHEADS):
        lr[h, :, 0, h] = a["L0_gnn_attn_l"][h]
        lr[h, :, 1, h] = a["L0_gnn_attn_r"][h]
    attn_m = a["L0_gnn_attn_m"].transpose(1, 0, 2).reshape(EPRO, HT)
    w_qkv = a["L0_mix_w_qkv"]

    def hidden_columns(w):
        out = np.zeros((EXPERTS, DIM, HP), w.dtype)
        out[:, :, :HID] = w.transpose(0, 2, 1)
        return out

    w2T = np.zeros((EXPERTS, HP, DIM), np.float32)
    w2T[:, :HID] = a["L0_ffn_w2"].transpose(0, 2, 1)
    arrays = dict(
        x=rows(a["x"], NP), src=src.reshape(NG, P, ET).transpose(1, 0, 2), dst=grouped.transpose(1, 0, 2),
        dst_first=first, dst_last=last, dst_head=chain[0], dst_tail=chain[1], dst_before=chain[2], dst_after=chain[3],
        dst_cols=columns, mask=mask, epro=epro, w_n=a["L0_gnn_W_n"], w_nT=a["L0_gnn_W_n"].T,
        attn_lr=lr.reshape(DIM, 2 * HT), attn_m=attn_m, w_kvT=w_qkv[INNER:].T, w_q=w_qkv[:INNER],
        w_oT=a["L0_mix_w_out"].T, b_out=a["L0_mix_b_out"][None], router=a["L0_ffn_router_w"].T,
        w1T=hidden_columns(a["L0_ffn_w1"]), w3T=hidden_columns(a["L0_ffn_w3"]), w2T=w2T)
    arrays = {f"in_{k}": np.ascontiguousarray(v) for k, v in arrays.items()}
    nc = bacc.Bacc("TRN2", target_bir_lowering=False, num_devices=1)
    aps = [nc.dram_tensor(k, v.shape, mybir.dt.from_np(v.dtype), kind="ExternalInput").ap() for k, v in arrays.items()]
    out = nc.dram_tensor("out_x", [NP, DIM], F32, kind="ExternalOutput").ap()
    build(nc, *aps, out)
    r = run_bass_kernel_spmd(nc, [arrays], core_ids=[0])
    return r.results[0]["out_x"][:NODES]
```

```python
from contextlib import ExitStack

import numpy as np
import concourse.bass as bass
from concourse import mybir

P = 128
F32 = mybir.dt.float32
I32 = mybir.dt.int32
ALU = mybir.AluOpType
ACT = mybir.ActivationFunctionType
AX = mybir.AxisListType
ds = bass.ds

NODES, DIM = 6250, 256
EDGES, EPRO, TYPES = 100000, 16, 4
GHEADS, GDIM = 8, 32
MHEADS, MDIM = 8, 64
INNER = MHEADS * MDIM
EXPERTS, HID = 8, 682
EPS = 1e-5
SLOPE = 0.2
BIG = 1e30

NT = 2 * -(-NODES // (2 * P))
NP = NT * P
KC = DIM // P
ET = 7
GROUP = ET * P
NG = 4 * -(-EDGES // (4 * GROUP))
EP = NG * GROUP
NBUF = 4
WINDOW = P - EPRO
NWIN = NT - 1
HT = GHEADS * TYPES
ROW = DIM + HT
AGG = DIM + GHEADS
HC = 6
HW = -(-HID // HC)
HP = HC * HW
SENT = DIM + 2
BLK = 2 * P
CAP = NP + BLK
NBLK = 2 * -(-((2 * NODES + EXPERTS * (BLK - 1)) // BLK) // 2)
TRASH = float(1 << 20)


def build(nc, x, src, dst, dst_first, dst_last, dst_head, dst_tail, dst_before, dst_after, dst_cols, mask, epro,
          w_n, w_nT, attn_lr, attn_m, w_kvT, w_q, w_oT, b_out, router, w1T, w3T, w2T, out):
    xnT_d = nc.dram_tensor("xn_transposed", [NT, P, KC * P], F32).ap()
    table = nc.dram_tensor("node_table", [NP, ROW], F32).ap()
    er_table = nc.dram_tensor("right_scores", [NP, HT], F32).ap()
    pens_d = nc.dram_tensor("chain_penalties", [NG + 2, 4 * P], F32).ap()
    agg_d = nc.dram_tensor("aggregate", [2 * NP, AGG], F32)
    with ExitStack() as ctx:
        ident = ctx.enter_context(nc.sbuf_tensor("ident", [P, P], F32))
        iota_row = ctx.enter_context(nc.sbuf_tensor("iota_row", [P, P], F32))
        iota_col = ctx.enter_context(nc.sbuf_tensor("iota_col", [P, 1], F32))
        zeros = ctx.enter_context(nc.sbuf_tensor("zeros", [P, 512], F32))
        eps_col = ctx.enter_context(nc.sbuf_tensor("eps_col", [P, 1], F32))
        mix = ctx.enter_context(nc.sbuf_tensor("mix_matrix", [P, KC, DIM], F32))
        constants(nc, ident, iota_row, iota_col, zeros, eps_col)
        project_and_mix(nc, x, w_n, w_nT, attn_lr, w_kvT, w_q, w_oT, ident, eps_col, zeros, xnT_d, table, er_table, agg_d, mix)
        edges(nc, src, dst, dst_first, dst_last, dst_head, dst_tail, dst_before, dst_after, dst_cols, mask, epro,
              attn_m, ident, iota_row, iota_col, zeros, table, er_table, pens_d, agg_d)
        feed_forward(nc, x, xnT_d, agg_d, mix, b_out, router, w1T, w3T, w2T, ident, eps_col, zeros, out)


def turns(eng, count, last=False):
    def run(body):
        body(0)
        with eng.Fori(1, count - last) as i:
            body(i)
        if last:
            body(count - 1)
    return run


def is_first(i):
    return isinstance(i, int) and i == 0


def tools(nc, ctx, tag):
    def sb(name, shape, dt=F32):
        return ctx.enter_context(nc.sbuf_tensor(f"{tag}_{name}", shape, dt))

    def ps(name):
        return ctx.enter_context(nc.psum_tensor(f"{tag}_{name}", [P, 512], F32))

    taken = []
    ctx.callback(lambda: (nc.clear_and_free_semaphores(taken), nc.all_engine_barrier()))

    def sem(name):
        taken.append(nc.alloc_semaphore(f"{tag}_{name}"))
        return taken[-1]

    passed = sem("passed")

    def hold(eng):
        eng.sem_inc(passed, 1)

    def sems(name, n=2):
        return [sem(f"{name}{j}") for j in range(n)]

    return sb, ps, sem, sems, hold


def constants(nc, ident, iota_row, iota_col, zeros, eps_col):
    with ExitStack() as ctx:
        sb, ps, sem, sems, hold = tools(nc, ctx, "const")
        row_i, col_i = sb("row_i", [P, P], I32), sb("col_i", [P, 1], I32)
        blank, counted = sem("blank"), sem("counted")
        block = ctx.enter_context(nc.Block())

        @block.gpsimd
        def _(pool):
            pool.memset(zeros[:, :], 0.0)
            pool.memset(eps_col[:, :], EPS)
            pool.memset(ident[:, :], 0.0).then_inc(blank, 1)
            pool.iota(row_i[:, :], [[1, P]], base=0, channel_multiplier=0).then_inc(counted, 1)
            pool.iota(col_i[:, :], [[1, 1]], base=0, channel_multiplier=1).then_inc(counted, 1)
            pool.wait_ge(blank, 1)
            pool.affine_select(out=ident[:, :], in_=ident[:, :], compare_op=ALU.not_equal, fill=1.0,
                               base=0, pattern=[[-1, P]], channel_multiplier=1)

        @block.vector
        def _(dve):
            dve.wait_ge(counted, 2)
            dve.tensor_copy(iota_row[:, :], row_i[:, :])
            dve.tensor_copy(iota_col[:, :], col_i[:, :])


def project_and_mix(nc, x, w_n, w_nT, attn_lr, w_kvT, w_q, w_oT, ident, eps_col, zeros, xnT_d, table, er_table, agg_d, mix):
    WID = DIM + 2 * HT
    KV = 2 * INNER
    PAIRS = INNER // P
    GROUPS = KV // MDIM
    TURNS = NT // 2
    with ExitStack() as ctx:
        sb, ps, sem, sems, hold = tools(nc, ctx, "proj")
        wn_T, lr = sb("wnT", [P, KC, DIM]), sb("lr", [P, KC, 2 * HT])
        wcat = sb("wcat", [P, KC, WID])
        wkv, wmean = sb("wkv", [P, KC, KV]), sb("wmean", [P, KC * GROUPS])
        wq, wo = sb("wq", [P, PAIRS, DIM]), sb("wo", [P, PAIRS, DIM])
        xt, xn = sb("x", [P, 2, DIM]), sb("xn", [P, 2, DIM])
        stats, mv = sb("stats", [P, 2, 6]), sb("mv", [P, 2, 2])
        sd, rs = sb("sd", [P, 2]), sb("rs", [P, 2])
        xT, proj = sb("xT", [P, 2, KC, P]), sb("proj", [P, 2, WID])
        sq, var, kv_sd = sb("sq", [P, 2, KV]), sb("var", [P, 2, GROUPS]), sb("kv_sd", [P, 2, GROUPS])
        sdp, rr = sb("sdp", [P, 2, MHEADS]), sb("rr", [P, 2, MHEADS])
        kn, vc = sb("kn", [P, 2, INNER]), sb("vc", [P, 2, INNER])
        dT, t1 = sb("dotsT", [P, PAIRS, P]), sb("t1", [P, PAIRS, DIM])
        pT, pP, pdots = ps("T"), [ps("P0"), ps("P1")], ps("dots")
        pkv = [[ps("k0"), ps("v0")], [ps("k1"), ps("v1")]]
        weights_in, scores_folded, wcat_ready, centre, centred, cleared = (
            sem(n) for n in ("weights_in", "scores_folded", "wcat_ready", "centre", "centred", "cleared"))
        x_in, stats_ok, mv_ok, sd_ok, rs_ok, xn_ok, turned, xT_ok, projected, proj_ok, stored = (
            sems(n) for n in ("x_in", "stats", "mv", "sd", "rs", "xn", "turned", "xT", "projected", "proj_ok", "stored"))
        kv_ok, sq_ok, var_ok, kv_sd_ok, sdp_ok, rr_ok, kn_ok, vc_ok, dots_ok = (
            sems(n) for n in ("kv", "sq", "var", "kv_sd", "sdp", "rr", "kn", "vc", "dots"))
        dots_done, dT_zero, dT_ok, t1_done, t1_ok, m_done, m_ok = (
            sem(n) for n in ("dots_done", "dT_zero", "dT_ok", "t1_done", "t1_ok", "m_done", "m_ok"))

        def other(i, b, d):
            return i + (b + d) // 2, (b + d) % 2

        def exists(i, b, d):
            return not isinstance(i, int) or 0 <= 2 * i + b + d < NT

        block = ctx.enter_context(nc.Block())

        @block.sync
        def _(sp):
            def load(i, b):
                sp.wait_ge(xn_ok[b], i)
                hold(sp)
                sp.dma_start(xt[:, b, :], x[ds((2 * i + b) * P, P), :]).then_inc(x_in[b], 16)

            load(0, 0)
            load(0, 1)
            sp.dma_start(wn_T[:, :, :], w_nT.rearrange("(k p) n -> p k n", p=P)).then_inc(weights_in, 16)
            sp.dma_start(lr[:, :, :], attn_lr.rearrange("(k p) n -> p k n", p=P)).then_inc(weights_in, 16)
            sp.dma_start(wcat[:, :, 0:DIM], w_n.rearrange("(k p) n -> p k n", p=P)).then_inc(weights_in, 16)
            sp.dma_start(wkv[:, :, :], w_kvT.rearrange("(k p) n -> p k n", p=P)).then_inc(weights_in, 16)
            sp.dma_start(wq[:, :, :], w_q.rearrange("(k p) n -> p k n", p=P)).then_inc(weights_in, 16)
            sp.dma_start(wo[:, :, :], w_oT.rearrange("(k p) n -> p k n", p=P)).then_inc(weights_in, 16)
            sp.dma_start(agg_d[0:NP, :].rearrange("(t p) n -> p t n", p=P), zeros[:, 0:AGG].rearrange("p (o n) -> p o n", o=1)
                         .to_broadcast([P, NT, AGG])).then_inc(cleared, 16)
            with sp.Fori(1, TURNS) as i:
                for b in range(2):
                    load(i, b)
            sp.wait_ge(cleared, 16)

        @block.gpsimd
        def _(pool):
            @turns(pool, TURNS)
            def _(i):
                for b in range(2):
                    t = 2 * i + b
                    pool.wait_ge(xT_ok[b], i + 1)
                    pool.dma_start(xnT_d[ds(t, 1), :, :].rearrange("o p n -> (o p) n"),
                                   xT[:, b, :, :].rearrange("p k n -> p (k n)")).then_inc(stored[b], 16)
                    pool.wait_ge(proj_ok[b], i + 1)
                    pool.dma_start(table[ds(t * P, P), :], proj[:, b, 0:ROW]).then_inc(stored[b], 16)
                    pool.dma_start(er_table[ds(t * P, P), :], proj[:, b, ROW:WID]).then_inc(stored[b], 16)
            for b in range(2):
                pool.wait_ge(stored[b], 48 * TURNS)

        @block.vector
        def _(dve):
            def moments(i, b):
                dve.wait_ge(x_in[b], 16 * i + 16)
                dve.bn_stats(stats[:, b, :], xt[:, b, :]).then_inc(stats_ok[b], 1)
                dve.wait_ge(stats_ok[b], i + 1)
                hold(dve)
                dve.bn_aggr(mv[:, b, :], stats[:, b, :]).then_inc(mv_ok[b], 1)

            def normalise(i, b):
                dve.wait_ge(sd_ok[b], i + 1)
                dve.reciprocal(rs[:, b:b + 1], sd[:, b:b + 1]).then_inc(rs_ok[b], 1)
                dve.wait_ge(rs_ok[b], i + 1)
                dve.wait_ge(turned[b], i)
                dve.tensor_scalar(xn[:, b, :], xt[:, b, :], mv[:, b, 0:1], rs[:, b:b + 1],
                                  ALU.subtract, ALU.mult).then_inc(xn_ok[b], 1)

            def variances(i, b):
                dve.wait_ge(sq_ok[b], 2 * i + 2)
                dve.tensor_reduce(var[:, b, :], sq[:, b, :].rearrange("p (g d) -> p g d", d=MDIM), AX.X,
                                  ALU.add).then_inc(var_ok[b], 1)

            def scale_keys(i, b):
                dve.wait_ge(kv_sd_ok[b], i + 1)
                dve.tensor_tensor(sdp[:, b, :], kv_sd[:, b, 0:MHEADS], kv_sd[:, b, MHEADS:GROUPS],
                                  ALU.mult).then_inc(sdp_ok[b], 1)
                dve.wait_ge(sdp_ok[b], i + 1)
                dve.reciprocal(rr[:, b, :], sdp[:, b, :]).then_inc(rr_ok[b], 1)
                dve.wait_ge(rr_ok[b], i + 1)
                dve.wait_ge(dots_ok[b], i)
                dve.tensor_tensor(kn[:, b, :].rearrange("p (g d) -> p g d", d=MDIM),
                                  pkv[b][0][:, :].rearrange("p (g d) -> p g d", d=MDIM),
                                  rr[:, b, :].rearrange("p (g o) -> p g o", o=1).to_broadcast([P, MHEADS, MDIM]),
                                  ALU.mult).then_inc(kn_ok[b], 1)

            def keep_projection(i, b):
                dve.wait_ge(projected[b], i + 1)
                dve.wait_ge(stored[b], 48 * i)
                dve.tensor_copy(proj[:, b, :], pP[b][:, 0:WID]).then_inc(proj_ok[b], 1)

            moments(0, 0)
            normalise(0, 0)
            moments(0, 1)
            normalise(0, 1)
            dve.wait_ge(scores_folded, 1)
            for k in range(KC):
                dve.tensor_copy(wcat[:, k, DIM:WID], pP[0][:, k * 2 * HT:(k + 1) * 2 * HT]).then_inc(wcat_ready, 1)
            dve.wait_ge(weights_in, 96)
            w3 = wkv[:, :, :].rearrange("p k (g d) -> p (k g) d", d=MDIM)
            dve.tensor_reduce(wmean[:, :], w3, AX.X, ALU.add).then_inc(centre, 1)
            dve.wait_ge(centre, 1)
            dve.tensor_scalar(wmean[:, :], wmean[:, :], 1.0 / MDIM, None, ALU.mult).then_inc(centre, 1)
            dve.wait_ge(centre, 2)
            dve.tensor_tensor(w3, w3, wmean[:, :].rearrange("p (g o) -> p g o", o=1).to_broadcast([P, KC * GROUPS, MDIM]),
                              ALU.subtract).then_inc(centred, 1)

            @turns(dve, TURNS, last=True)
            def _(i):
                for b in range(2):
                    if exists(i, b, -1):
                        variances(*other(i, b, -1))
                    if exists(i, b, 2):
                        moments(*other(i, b, 2))
                    if exists(i, b, -1):
                        scale_keys(*other(i, b, -1))
                    if exists(i, b, 2):
                        normalise(*other(i, b, 2))
                    keep_projection(i, b)
            variances(TURNS - 1, 1)
            scale_keys(TURNS - 1, 1)
            dve.memset(dT[:, :, :], 0.0).then_inc(dT_zero, 1)
            dve.wait_ge(dT_zero, 1)
            dve.wait_ge(dots_done, 1)
            pd = pdots[:, :].rearrange("p (q n) -> p q n", q=PAIRS)
            for h in range(2):
                s = slice(h * MDIM, (h + 1) * MDIM)
                dve.tensor_copy(dT[s, :, s], pd[s, :, s]).then_inc(dT_ok, 1)
            for q in range(PAIRS):
                dve.wait_ge(t1_done, q + 1)
                dve.tensor_copy(t1[:, q, :], pP[q % 2][:, 0:DIM]).then_inc(t1_ok, 1)
            for c in range(KC):
                dve.wait_ge(m_done, c + 1)
                dve.tensor_scalar(mix[:, c, :], pP[c][:, 0:DIM], 1.0 / NODES, None, ALU.mult).then_inc(m_ok, 1)

        @block.scalar
        def _(act):
            def deviation(i, b):
                act.wait_ge(mv_ok[b], i + 1)
                act.activation(sd[:, b:b + 1], mv[:, b, 1:2], ACT.Sqrt, bias=eps_col[:, 0:1]).then_inc(sd_ok[b], 1)

            def keep_turned(i, b):
                act.wait_ge(turned[b], i + 1)
                act.wait_ge(stored[b], 48 * i)
                act.wait_ge(kv_ok[b], i)
                act.activation(xT[:, b, :, :].rearrange("p k n -> p (k n)"), pT[:, b * KC * P:(b + 1) * KC * P],
                               ACT.Copy).then_inc(xT_ok[b], 1)

            def squares(i, b):
                act.wait_ge(kv_ok[b], i + 1)
                act.wait_ge(var_ok[b], i)
                for h in range(2):
                    act.activation(sq[:, b, h * INNER:(h + 1) * INNER], pkv[b][h][:, :], ACT.Square).then_inc(sq_ok[b], 1)

            def keep_values(i, b):
                act.wait_ge(dots_ok[b], i)
                act.activation(vc[:, b, :], pkv[b][1][:, :], ACT.Copy).then_inc(vc_ok[b], 1)

            def key_deviations(i, b):
                act.wait_ge(var_ok[b], i + 1)
                act.activation(kv_sd[:, b, :], var[:, b, :], ACT.Sqrt, bias=eps_col[:, 0:1],
                               scale=1.0 / MDIM).then_inc(kv_sd_ok[b], 1)

            deviation(0, 0)
            deviation(0, 1)
            keep_turned(0, 0)

            @turns(act, TURNS, last=True)
            def _(i):
                for b in range(2):
                    if exists(i, b, -1):
                        squares(*other(i, b, -1))
                    if exists(i, b, 1):
                        keep_turned(*other(i, b, 1))
                    if exists(i, b, -1):
                        keep_values(*other(i, b, -1))
                        key_deviations(*other(i, b, -1))
                    if exists(i, b, 2):
                        deviation(*other(i, b, 2))
            squares(TURNS - 1, 1)
            keep_values(TURNS - 1, 1)
            key_deviations(TURNS - 1, 1)

        @block.tensor
        def _(pe):
            def turn_nodes(i, b):
                pe.wait_ge(xn_ok[b], i + 1)
                pe.wait_ge(xT_ok[1 - b], i + b)
                for k in range(KC):
                    last = pe.transpose(pT[:, (b * KC + k) * P:(b * KC + k + 1) * P], xn[:, b, k * P:(k + 1) * P], ident[:, :])
                last.then_inc(turned[b], 1)

            def project(i, b):
                pe.wait_ge(xT_ok[b], i + 1)
                pe.wait_ge(proj_ok[b], i)
                for k in range(KC):
                    last = pe.matmul(pP[b][:, 0:WID], xT[:, b, k, :], wcat[:, k, :], start=(k == 0), stop=(k == KC - 1))
                last.then_inc(projected[b], 1)

            def keys_and_values(i, b):
                pe.wait_ge(kn_ok[b], i)
                pe.wait_ge(vc_ok[b], i)
                for h in range(2):
                    for k in range(KC):
                        last = pe.matmul(pkv[b][h][:, :], xT[:, b, k, :], wkv[:, k, h * INNER:(h + 1) * INNER],
                                         start=(k == 0), stop=(k == KC - 1))
                last.then_inc(kv_ok[b], 1)

            def dots(i, b):
                pe.wait_ge(kn_ok[b], i + 1)
                pe.wait_ge(vc_ok[b], i + 1)
                for q in range(PAIRS):
                    last = pe.matmul(pdots[:, q * P:(q + 1) * P], vc[:, b, q * P:(q + 1) * P],
                                     kn[:, b, q * P:(q + 1) * P], start=False, stop=False, skip_group_check=True)
                last.then_inc(dots_ok[b], 1)

            pe.wait_ge(weights_in, 96)
            for m in range(KC):
                for k in range(KC):
                    last = pe.matmul(pP[0][:, m * 2 * HT:(m + 1) * 2 * HT], wn_T[:, k, m * P:(m + 1) * P],
                                     lr[:, k, :], start=(k == 0), stop=(k == KC - 1))
            last.then_inc(scores_folded, 1)
            pe.matmul(pdots[:, :], zeros[:, 0:P], zeros[:, :], start=True, stop=False, skip_group_check=True)
            turn_nodes(0, 0)
            pe.wait_ge(wcat_ready, KC)
            pe.wait_ge(centred, 1)

            @turns(pe, TURNS, last=True)
            def _(i):
                for b in range(2):
                    if exists(i, b, 1):
                        turn_nodes(*other(i, b, 1))
                    project(i, b)
                    keys_and_values(i, b)
                    if exists(i, b, -1):
                        dots(*other(i, b, -1))
            dots(TURNS - 1, 1)
            pe.matmul(pdots[:, :], zeros[:, 0:P], zeros[:, :], start=False, stop=True,
                      skip_group_check=True).then_inc(dots_done, 1)
            pe.wait_ge(dT_ok, 2)
            pe.wait_ge(proj_ok[0], TURNS)
            pe.wait_ge(proj_ok[1], TURNS)
            for q in range(PAIRS):
                if q >= 2:
                    pe.wait_ge(t1_ok, q - 1)
                pe.matmul(pP[q % 2][:, 0:DIM], dT[:, q, :], wo[:, q, :], start=True, stop=True).then_inc(t1_done, 1)
            pe.wait_ge(t1_ok, PAIRS)
            for c in range(KC):
                for q in range(PAIRS):
                    last = pe.matmul(pP[c][:, 0:DIM], wq[:, q, c * P:(c + 1) * P], t1[:, q, :],
                                     start=(q == 0), stop=(q == PAIRS - 1))
                last.then_inc(m_done, 1)


def edges(nc, src, dst, dst_first, dst_last, dst_head, dst_tail, dst_before, dst_after, dst_cols, mask, epro, attn_m,
          ident, iota_row, iota_col, zeros, table, er_table, pens_d, agg_d):
    GA = NG + 2
    H, TT = GHEADS, TYPES
    with ExitStack() as ctx:
        sb, ps, sem, sems, hold = tools(nc, ctx, "edge")
        src_all, dst_i, dstf = sb("src_all", [P, NG, ET], I32), sb("dst_i", [P, NG, ET], I32), sb("dstf", [P, NG, ET])
        mask_all = sb("mask_all", [P, NG, ET, TT])
        first_i, last_i = sb("first_i", [P, GA], I32), sb("last_i", [P, GA], I32)
        first_f, wcol, span, last_ind = sb("first_f", [P, GA]), sb("wcol", [P, GA]), sb("span", [P, GA]), sb("last_ind", [P, GA])
        rel = sb("rel", [P, NG, ET])
        widest_f, widest = sb("widest_f", [P, 1]), sb("widest", [P, 1], I32)
        pen_prev, pen_next, pen_head, pen_tail = (sb(n, [P, GA, ET]) for n in ("pprev", "pnext", "phead", "ptail"))
        chain_i, chain_f = sb("chain_i", [GA, 4, P], I32), sb("chain_f", [GA, 4, P])
        chain_eq, chain_pen = sb("chain_eq", [GA, 3, P]), sb("chain_pen", [GA, 4, P])
        e0 = sb("e0", [1, P])
        wneg, one, gap = sb("wneg", [P, GA]), sb("one", [P, 1]), sb("gap", [WINDOW, 2, GROUP])
        dstb, oht, oh = sb("dstb", [P, 2, GROUP], I32), sb("oht", [P, 2, GROUP]), sb("oh", [P, 2, ET, P])
        erw, pens = sb("erw", [P, 2, HT]), sb("pens", [H, 2, 4, P])
        idx = sb("idx", [P, NBUF, ET], I32)
        G = sb("G", [P, NBUF, ET, ROW])
        penx, lastc = sb("penx", [P, 2, 2, H * ET]), sb("lastc", [P, 2])
        z, e, f1, b1, m, m2, q = (sb(n, [P, 2, w]) for n, w in (("z", ET * HT), ("e", H * ET), ("f1", H * ET), ("b1", H * ET),
                                                               ("m", H * ET), ("m2", H * ET), ("q", H * ET)))
        m3, uc, ud = sb("m3", [P, 2, H * ET]), sb("uc", [P, 2, H * ET]), sb("ud", [P, 2, H * ET])
        rb, lb, cc, dd = sb("rb", [H, 2, P + 1]), sb("lb", [H, 2, P + 1]), sb("cc", [H, 2, P]), sb("dd", [H, 2, P])
        fd, fac, cs = sb("fd", [1, 2, H]), sb("fac", [1, 2, H]), sb("cs", [1, 2, AGG])
        osum = sb("osum", [P, 2, AGG])
        pR, pA, pO, pC = [ps("R0"), ps("R1")], [ps("A0"), ps("A1")], [ps("O0"), ps("O1")], ps("C")
        pB = ps("B")

        indices_in, chain_in, small_in = sem("indices_in"), sem("chain_in"), sem("small_in")
        pre, chained, pens_stored = sem("pre"), sem("chained"), sem("pens_stored")
        ready = sem("ready")
        cols_in, feats_in, pens_in, oht_ok, oh_ok, r_done, z_ok, zm_ok, s_ok, e_ok, f_ok, b_ok, m_ok, tails_up = (
            sems(n) for n in ("cols_in", "feats_in", "pens_in", "oht", "oh", "r_done", "z", "zm", "s", "e", "f", "b", "m", "tails_up"))
        seed_ok, rscan_ok, lscan_ok, c_ok, d_ok, cd_up, uc_ok, ud_ok, m2_ok, m3_ok, q_ok, fd_ok, fac_ok, cs_ok = (
            sems(n) for n in ("seed", "rscan", "lscan", "c", "d", "cd_up", "uc", "ud", "m2", "m3", "q", "fd", "fac", "cs"))
        gap_ok = sems("gap")
        penx_ok, osum_ok, stored, carry_up = (sems(n) for n in ("penx", "osum", "stored", "carry_up"))
        idx_ok, gathered, p_ok, msg_ok, out_done = (sems(n, NBUF) for n in ("idx", "gathered", "p", "msg", "out_done"))

        def place(i, b):
            return 4 * i + b, b % 2, 2 * i + b // 2

        def before(i, b):
            return (i, b - 1) if b else (i - 1, 3)

        def after(i, b):
            return (i, b + 1) if b < 3 else (i + 1, 0)

        def wait_sums_of_two_before(eng, i, b):
            eng.wait_ge(out_done[(b + 2) % 4], i + b // 2)

        narrow = ExitStack()
        block = narrow.enter_context(nc.Block())

        @block.sync
        def _(sp):
            sp.dma_start(src_all[:, :, :], src).then_inc(indices_in, 16)
            sp.dma_start(dst_i[:, :, :], dst).then_inc(indices_in, 16)
            sp.dma_start(first_i[:, :], dst_first.to_broadcast([P, GA])).then_inc(indices_in, 16)
            sp.dma_start(last_i[:, :], dst_last.to_broadcast([P, GA])).then_inc(indices_in, 16)
            for n, a in enumerate((dst_head, dst_tail, dst_before, dst_after)):
                sp.dma_start(chain_i[:, n, :], a).then_inc(chain_in, 16)
            sp.dma_start(mask_all[:, :, :, :], mask).then_inc(small_in, 16)
            for c in range(2):
                sp.dma_start(erw[WINDOW:P, c, :], attn_m).then_inc(small_in, 16)
            sp.wait_ge(chained, 1)
            sp.dma_start(pens_d.rearrange("g (k p) -> g k p", k=4), chain_pen[:, :, :]).then_inc(pens_stored, 16)
            sp.wait_ge(pens_stored, 16)

            def load(g, c, u):
                w = sp.value_load(dst_first[0:1, ds(g, 1)], min_val=0, max_val=NP - P)
                sp.wait_ge(oht_ok[c], u)
                hold(sp)
                sp.dma_start(dstb[:, c, :], dst_cols[ds(g, 1), :].to_broadcast([P, GROUP])).then_inc(cols_in[c], 16)
                sp.wait_ge(r_done[c], u)
                hold(sp)
                sp.dma_start(oht[WINDOW:P, c, :], epro[:, ds(g * GROUP, GROUP)]).then_inc(feats_in[c], 16)
                sp.dma_start(erw[0:WINDOW, c, :], er_table[ds(w, WINDOW), :]).then_inc(feats_in[c], 16)
                sp.wait_ge(c_ok[c], u)
                sp.wait_ge(d_ok[c], u)
                hold(sp)
                sp.dma_start(pens[:, c, :, :], pens_d[ds(g, 1), :].rearrange("g (k p) -> g k p", k=4)
                             .to_broadcast([H, 4, P])).then_inc(pens_in[c], 16)

            def store(g, c, u):
                w = sp.value_load(dst_first[0:1, ds(g, 1)], min_val=0, max_val=NP - P)
                sp.wait_ge(osum_ok[c], u + 1)
                hold(sp)
                sp.wait_ge(stored[1 - c], 16 * (u + c))
                hold(sp)
                sp.dma_start(agg_d[ds(w, P), :], osum[:, c, :]).then_inc(stored[c], 16)

            load(0, 0, 0)
            load(1, 1, 0)

            @turns(sp, NG // 4)
            def _(i):
                for b in range(4):
                    g, c, u = 4 * i + b, b % 2, 2 * i + b // 2
                    if not (is_first(i) and b < 2):
                        store(g - 2, c, u - 1)
                    load(g + 2, c, u + 1)
            for c in range(2):
                store(NG - 2 + c, c, NG // 2 - 1)
            for c in range(2):
                sp.wait_ge(stored[c], 16 * (NG // 2))
                sp.wait_ge(cols_in[c], 16 * (NG // 2 + 1))
                sp.wait_ge(feats_in[c], 32 * (NG // 2 + 1))
                sp.wait_ge(pens_in[c], 16 * (NG // 2 + 1))

        @block.gpsimd
        def _(pool):
            pool.wait_ge(indices_in, 64)
            @turns(pool, NG // 4)
            def _(i):
                for b in range(4):
                    g = 4 * i + b
                    pool.wait_ge(out_done[b], i)
                    pool.tensor_copy(idx[:, b, :], src_all[:, ds(g, 1), :].rearrange("p o t -> p (o t)")).then_inc(idx_ok[b], 1)
                    pool.wait_ge(idx_ok[b], i + 1)
                    hold(pool)
                    for t in range(ET):
                        pool.indirect_dma_start(G[:, b, t, :], None, table, bass.IndirectOffsetOnAxis(idx[:, b, t:t + 1], 0)
                                                ).then_inc(gathered[b], 16)

        @block.vector
        def _(dve):
            dve.wait_ge(indices_in, 64)
            n = 0

            def then(ins):
                nonlocal n
                n += 1
                ins.then_inc(pre, 1)
                dve.wait_ge(pre, n)

            then(dve.tensor_copy(dstf[:, :, :], dst_i[:, :, :]))
            then(dve.tensor_copy(first_f[:, :], first_i[:, :]))
            then(dve.tensor_copy(span[:, :], last_i[:, :]))
            then(dve.tensor_tensor(span[:, :], span[:, :], first_f[:, :], ALU.subtract))
            then(dve.tensor_reduce(widest_f[:, :], span[:, :], AX.X, ALU.max))
            then(dve.tensor_copy(widest[:, :], widest_f[:, :]))
            then(dve.tensor_scalar(last_ind[:, :], span[:, :], iota_col[:, 0:1], None, ALU.is_equal))
            then(dve.tensor_scalar(wcol[:, :], first_f[:, :], iota_col[:, 0:1], None, ALU.add))
            then(dve.tensor_scalar(wneg[:, :], wcol[:, :], -1.0, None, ALU.mult))
            then(dve.memset(one[:, :], 1.0))
            then(dve.tensor_tensor(rel[:, :, :], dstf[:, :, :], first_f[:, 0:NG].rearrange("p (g o) -> p g o", o=1)
                                   .to_broadcast([P, NG, ET]), ALU.subtract))
            for a in (pen_prev, pen_next, pen_head, pen_tail):
                then(dve.memset(a[:, :, :], 0.0))
            then(dve.tensor_tensor(pen_prev[:, 0:NG, 1:ET], dstf[:, :, 1:ET], dstf[:, :, 0:ET - 1], ALU.is_equal))
            then(dve.tensor_tensor(pen_next[:, 0:NG, 0:ET - 1], dstf[:, :, 1:ET], dstf[:, :, 0:ET - 1], ALU.is_equal))
            then(dve.tensor_tensor(pen_head[:, 0:NG, :], dstf[:, :, :], dstf[:, :, 0:1].to_broadcast([P, NG, ET]), ALU.is_equal))
            then(dve.tensor_tensor(pen_tail[:, 0:NG, :], dstf[:, :, :], dstf[:, :, ET - 1:ET].to_broadcast([P, NG, ET]), ALU.is_equal))
            for a in (pen_prev, pen_next, pen_head, pen_tail):
                then(dve.tensor_scalar(a[:, :, :], a[:, :, :], -1.0, BIG, ALU.add, ALU.mult))
            dve.wait_ge(chain_in, 64)
            then(dve.tensor_copy(chain_f[:, :, :], chain_i[:, :, :]))
            head, tail, prev_tail, next_head = (chain_f[:, k, :] for k in range(4))
            for k, (x0, x1) in enumerate(((head, prev_tail), (tail, next_head), (head, tail))):
                then(dve.tensor_tensor(chain_eq[:, k, :], x0, x1, ALU.is_equal))
            then(dve.tensor_scalar(chain_eq[:, :, :], chain_eq[:, :, :], -1.0, BIG, ALU.add, ALU.mult))
            then(dve.tensor_copy(chain_pen[:, 0:2, :], chain_eq[:, 0:2, :]))
            then(dve.tensor_tensor(chain_pen[:, 2:4, :], chain_eq[:, 0:2, :], chain_eq[:, 2:3, :].to_broadcast([GA, 2, P]), ALU.add))
            dve.memset(e0[:, :], 0.0).then_inc(chained, 1)
            then(dve.memset(rb[:, :, :], -BIG))
            then(dve.memset(lb[:, :, :], -BIG))
            dve.wait_ge(chained, 1)
            dve.memset(e0[:, 0:1], 1.0).then_inc(ready, 1)
            dve.wait_ge(small_in, 48)

            def step(i, b, front, back):
                g, c, u = place(i, b)
                ip, bp = before(i, b)
                gp, cp, up = place(ip, bp)
                m_ht = [a[:, cp, :].rearrange("p (h t) -> p h t", h=H) for a in (m, uc, ud, m2, m3)]
                z4 = z[:, c, :].rearrange("p (t h y) -> p t h y", t=ET, h=H)
                if front:
                    dve.wait_ge(gathered[b], 16 * ET * (i + 1))
                    dve.wait_ge(r_done[c], u + 1)
                    dve.tensor_tensor(z[:, c, :].rearrange("p (t n) -> p t n", t=ET), G[:, b, :, DIM:ROW],
                                      pR[c][:, 0:ET * HT].rearrange("p (t n) -> p t n", t=ET), ALU.add).then_inc(z_ok[c], 1)
                if back:
                    pc = [pB[:, cp * 2 * H + k * H:cp * 2 * H + (k + 1) * H].rearrange("p (h o) -> p h o", o=1).to_broadcast([P, H, ET]) for k in range(2)]
                    pen = [a[:, ds(gp, 1), :].to_broadcast([P, H, ET]) for a in (pen_head, pen_tail)]
                    dve.wait_ge(cd_up[cp], up + 1)
                    dve.tensor_tensor(m_ht[1], pen[0], pc[0], ALU.add).then_inc(uc_ok[cp], 1)
                    dve.tensor_tensor(m_ht[2], pen[1], pc[1], ALU.add).then_inc(ud_ok[cp], 1)
                if front:
                    mk = mask_all[:, ds(g, 1), :, :].rearrange("p o t (h y) -> p (o t) h y", h=1).to_broadcast([P, ET, H, TT])
                    dve.wait_ge(z_ok[c], u + 1)
                    dve.tensor_tensor(z4, z4, mk, ALU.mult).then_inc(zm_ok[c], 1)
                if back:
                    dve.wait_ge(uc_ok[cp], up + 1)
                    dve.wait_ge(m_ok[cp], up + 1)
                    dve.tensor_tensor(m2[:, cp, :], m[:, cp, :], uc[:, cp, :], ALU.max).then_inc(m2_ok[cp], 1)
                if front:
                    dve.wait_ge(zm_ok[c], u + 1)
                    dve.tensor_reduce(e[:, c, :].rearrange("p (h t) -> p t h", h=H), z4, AX.X, ALU.add).then_inc(s_ok[c], 1)
                if back:
                    dve.wait_ge(ud_ok[cp], up + 1)
                    dve.wait_ge(m2_ok[cp], up + 1)
                    dve.tensor_tensor(m3[:, cp, :], m2[:, cp, :], ud[:, cp, :], ALU.max).then_inc(m3_ok[cp], 1)
                if front:
                    dve.wait_ge(s_ok[c], u + 1)
                    dve.scalar_tensor_tensor(e[:, c, :], e[:, c, :], SLOPE, e[:, c, :], ALU.mult, ALU.max).then_inc(e_ok[c], 1)
                if back:
                    dve.wait_ge(m3_ok[cp], up + 1)
                    dve.tensor_tensor(q[:, cp, :], e[:, cp, :], m3[:, cp, :], ALU.subtract).then_inc(q_ok[cp], 1)
                    dve.tensor_tensor(fd[:, cp, :], pB[0:1, cp * 2 * H:cp * 2 * H + H], m_ht[4][0:1, :, 0], ALU.subtract).then_inc(fd_ok[cp], 1)
                if front:
                    dve.wait_ge(e_ok[c], u + 1)
                    dve.wait_ge(penx_ok[c], 2 * u + 2)
                    dve.tensor_tensor_scan(f1[:, c, :], penx[:, c, 0, :], e[:, c, :], -BIG, ALU.add, ALU.max).then_inc(f_ok[c], 1)
                    dve.tensor_tensor_scan(b1[:, c, ::-1], penx[:, c, 1, ::-1], e[:, c, ::-1], -BIG, ALU.add, ALU.max).then_inc(b_ok[c], 1)
                    dve.wait_ge(b_ok[c], u + 1)
                    dve.tensor_tensor(m[:, c, :], f1[:, c, :], b1[:, c, :], ALU.max).then_inc(m_ok[c], 1)
                if back:
                    g4 = G[:, bp, :, 0:DIM].rearrange("p t (h d) -> p t h d", h=H)
                    dve.wait_ge(p_ok[bp], ip + 1)
                    dve.tensor_tensor(g4, g4, G[:, bp, :, DIM:AGG].rearrange("p t (h o) -> p t h o", o=1)
                                      .to_broadcast([P, ET, H, GDIM]), ALU.mult).then_inc(msg_ok[bp], 1)
                if front:
                    if back:
                        dve.wait_ge(rscan_ok[cp], up + 1)
                    dve.tensor_copy(rb[:, c, 0:1], rb[:, 1 - c, P:P + 1]).then_inc(seed_ok[c], 1)
                    dve.wait_ge(tails_up[c], u + 1)
                    dve.wait_ge(pens_in[c], 16 * u + 16)
                    dve.tensor_tensor_scan(rb[:, c, 1:P + 1], pens[:, c, 2, :], pA[c][0:H, 0:P], rb[:, 1 - c, P:P + 1],
                                           ALU.add, ALU.max).then_inc(rscan_ok[c], 1)
                    dve.tensor_tensor_scan(lb[:, c, P - 1::-1], pens[:, c, 3, ::-1], pA[c][0:H, 2 * P - 1:P - 1:-1], -BIG,
                                           ALU.add, ALU.max).then_inc(lscan_ok[c], 1)
                if front:
                    dve.wait_ge(rscan_ok[c], u + 1)
                    dve.wait_ge(seed_ok[c], u + 1)
                    dve.wait_ge(cd_up[c], u)
                    dve.tensor_tensor(cc[:, c, :], rb[:, c, 0:P], pens[:, c, 0, :], ALU.add).then_inc(c_ok[c], 1)
                    dve.wait_ge(lscan_ok[c], u + 1)
                    dve.tensor_tensor(dd[:, c, :], lb[:, c, 1:P + 1], pens[:, c, 1, :], ALU.add).then_inc(d_ok[c], 1)
                    if not (is_first(i) and b < 2):
                        wait_sums_of_two_before(dve, i, b)
                    dve.tensor_tensor(oh[:, c, :, :], iota_row[:, :].rearrange("p (o n) -> p o n", o=1).to_broadcast([P, ET, P]),
                                      rel[:, ds(g, 1), :].rearrange("p o (t n) -> p (o t) n", n=1).to_broadcast([P, ET, P]),
                                      ALU.is_equal).then_inc(oh_ok[c], 1)
                if back:
                    if not (is_first(ip) and bp < 2):
                        wait_sums_of_two_before(dve, ip, bp)
                    dve.wait_ge(fac_ok[cp], up + 1)
                    dve.wait_ge(carry_up[1 - cp], up + 1)
                    dve.tensor_tensor(cs[:, cp, 0:DIM].rearrange("p (h d) -> p h d", h=H), pC[0:1, 0:DIM].rearrange("p (h d) -> p h d", h=H),
                                      fac[:, cp, :].rearrange("p (h o) -> p h o", o=1).to_broadcast([1, H, GDIM]), ALU.mult).then_inc(cs_ok[cp], 1)
                    dve.tensor_tensor(cs[:, cp, DIM:AGG], pC[0:1, DIM:AGG], fac[:, cp, :], ALU.mult).then_inc(cs_ok[cp], 1)

            @turns(dve, NG // 4)
            def _(i):
                for b in range(4):
                    step(i, b, True, not (is_first(i) and b == 0))
            step(NG // 4, 0, False, True)

        @block.scalar
        def _(act):
            act.wait_ge(ready, 1)

            def one_hot_nodes(i, b):
                g, c, u = place(i, b)
                act.wait_ge(cols_in[c], 16 * u + 16)
                act.activation(gap[:, c, :], dstb[0:WINDOW, c, :], ACT.Abs, bias=wneg[0:WINDOW, ds(g, 1)]).then_inc(gap_ok[c], 1)
                act.wait_ge(gap_ok[c], u + 1)
                act.wait_ge(r_done[c], u)
                act.activation(oht[0:WINDOW, c, :], gap[:, c, :], ACT.Relu, bias=one[0:WINDOW, 0:1], scale=-1.0).then_inc(oht_ok[c], 1)

            def spread_penalties(i, b):
                g, c, u = place(i, b)
                act.wait_ge(b_ok[c], u)
                for k, a in enumerate((pen_prev, pen_next)):
                    act.activation(penx[:, c, k, :].rearrange("p (h t) -> p h t", h=H), a[:, ds(g, 1), :].to_broadcast([P, H, ET]),
                                   ACT.Copy).then_inc(penx_ok[c], 1)

            def keep_sums(i, b):
                g, c, u = place(i, b)
                if not (is_first(i) and b < 2):
                    act.wait_ge(carry_up[c], u + c)
                act.activation(lastc[:, c:c + 1], last_ind[:, ds(g, 1)], ACT.Copy)
                act.wait_ge(out_done[b], i + 1)
                if not (is_first(i) and b < 2):
                    act.wait_ge(stored[c], 16 * u)
                act.activation(osum[:, c, :], pO[c][:, 0:AGG], ACT.Copy).then_inc(osum_ok[c], 1)

            def weights(i, b):
                g, c, u = place(i, b)
                act.wait_ge(q_ok[c], u + 1)
                act.activation(G[:, b, :, DIM:AGG].rearrange("p t h -> p h t"), q[:, c, :].rearrange("p (h t) -> p h t", h=H),
                               ACT.Exp, scale=1.0 / 3).then_inc(p_ok[b], 1)
                act.wait_ge(fd_ok[c], u + 1)
                act.wait_ge(cs_ok[c], 2 * u)
                act.activation(fac[:, c, :], fd[:, c, :], ACT.Exp, scale=1.0 / 3).then_inc(fac_ok[c], 1)

            spread_penalties(0, 0)
            one_hot_nodes(0, 0)

            def step(i, b, front, back, sums):
                if back:
                    weights(*before(i, b))
                if front:
                    one_hot_nodes(*after(i, b))
                    spread_penalties(*after(i, b))
                if sums:
                    keep_sums(*before(*before(i, b)))

            @turns(act, NG // 4)
            def _(i):
                for b in range(4):
                    step(i, b, True, not (is_first(i) and b < 1), not (is_first(i) and b < 2))
            step(NG // 4, 0, False, True, True)
            step(NG // 4, 1, False, False, True)

        @block.tensor
        def _(pe):
            pe.wait_ge(ready, 1)
            pe.wait_ge(small_in, 48)

            def scores(i, b):
                g, c, u = place(i, b)
                pe.wait_ge(oht_ok[c], u + 1)
                pe.wait_ge(feats_in[c], 32 * u + 32)
                pe.wait_ge(z_ok[c], u)
                for t in range(ET):
                    last = pe.matmul(pR[c][:, t * HT:(t + 1) * HT], oht[:, c, t * P:(t + 1) * P], erw[:, c, :], start=True, stop=True)
                last.then_inc(r_done[c], 1)

            def carry(i, b):
                g, c, u = place(i, b)
                pe.wait_ge(osum_ok[c], u + 1)
                pe.matmul(pC[0:1, 0:AGG], lastc[:, c:c + 1], osum[:, c, :], start=True, stop=True).then_inc(carry_up[c], 1)

            def turn_ends(i, b):
                g, c, u = place(i, b)
                ends = [a[:, c, :].rearrange("p (h t) -> p h t", h=H) for a in (f1, b1)]
                pe.wait_ge(f_ok[c], u + 1)
                pe.wait_ge(b_ok[c], u + 1)
                pe.wait_ge(rscan_ok[c], u)
                pe.wait_ge(lscan_ok[c], u)
                pe.transpose(pA[c][0:H, 0:P], ends[0][:, :, ET - 1], ident[:, :])
                pe.transpose(pA[c][0:H, P:2 * P], ends[1][:, :, 0], ident[:, :]).then_inc(tails_up[c], 1)

            def turn_back(i, b):
                g, c, u = place(i, b)
                pe.wait_ge(c_ok[c], u + 1)
                pe.wait_ge(d_ok[c], u + 1)
                pe.wait_ge(fd_ok[c], u)
                pe.wait_ge(ud_ok[c], u)
                hold(pe)
                pe.transpose(pB[:, c * 2 * H:c * 2 * H + H], cc[:, c, :], ident[0:H, 0:H])
                pe.transpose(pB[:, c * 2 * H + H:c * 2 * H + 2 * H], dd[:, c, :], ident[0:H, 0:H]).then_inc(cd_up[c], 1)

            def sums(i, b):
                g, c, u = place(i, b)
                pe.wait_ge(msg_ok[b], i + 1)
                pe.wait_ge(oh_ok[c], u + 1)
                pe.wait_ge(osum_ok[c], u)
                for t in range(ET):
                    pe.matmul(pO[c][:, 0:AGG], oh[:, c, t, :], G[:, b, t, 0:AGG], start=(t == 0), stop=False)

            def add_carried(i, b):
                g, c, u = place(i, b)
                pe.wait_ge(cs_ok[c], 2 * u + 2)
                pe.matmul(pO[c][:, 0:AGG], e0[:, :], cs[:, c, :], start=False, stop=True).then_inc(out_done[b], 1)

            def step(i, b, front, back, carried):
                if front:
                    turn_ends(i, b)
                    scores(*after(i, b))
                if carried:
                    carry(*before(*before(i, b)))
                if front:
                    turn_back(i, b)
                if back:
                    sums(*before(i, b))
                    add_carried(*before(i, b))

            pe.matmul(pC[0:1, 0:AGG], zeros[:, 0:1], zeros[:, 0:AGG], start=True, stop=True).then_inc(carry_up[1], 1)
            scores(0, 0)

            @turns(pe, NG // 4)
            def _(i):
                for b in range(4):
                    step(i, b, True, not (is_first(i) and b < 1), not (is_first(i) and b < 2))
            step(NG // 4, 0, False, True, True)
            step(NG // 4, 1, False, False, True)

        narrow.close()
        edges_of_wide_groups(nc, widest, src_all, dst_i, dst_first, rel, span, mask_all, (pen_prev, pen_next, pen_head, pen_tail),
                             e0, oht, erw, pens, oh[:, 0], (pR[0], pA[0], pB, pO[0], pC), G, z, rb, lb, osum, epro, ident, iota_row, iota_col, table, er_table,
                             pens_d, agg_d)


def edges_of_wide_groups(nc, widest, src_all, dst_i, dst_first, rel, span, mask_all, edge_pens, e0, features, erw, pens,
                         oh, banks, G, z, rb, lb, osum, epro, ident, iota_row, iota_col, table, er_table, pens_d, agg_d):
    H = GHEADS
    pen_prev, pen_next, pen_head, pen_tail = edge_pens
    with ExitStack() as ctx:
        sb, ps, sem, sems, hold = tools(nc, ctx, "wide")
        idx, rows_of_target = sb("idx", [P, 2, ET], I32), sb("rows_of_target", [P, ET, HT])
        pair = [P, 2, H * ET]
        penx, scan = sb("penx", pair), sb("scan", pair)
        e, m, ends = sb("e", [P, H * ET]), sb("m", [P, H * ET]), sb("ends", pair)
        turn, fd, fac = sb("turn", [H, 2, P]), sb("fd", [1, H]), sb("fac", [1, H])
        kept, carried = sb("kept", [1, AGG]), sb("carried", [1, AGG])
        distance, to_last, is_last = sb("distance", [P, ET]), sb("to_last", [P, 1]), sb("is_last", [P, 1])
        pR, pA, pB, pO, pC = banks

        cleared, loaded, gathered, indexed, edge_scores, spread = (
            sem(n) for n in ("cleared", "loaded", "gathered", "indexed", "edge_scores", "spread"))
        scored, scanned, tails_up, chain_scanned, turned, turned_back, shifted, scaled, weighted, fac_ok, fd_ok = (
            sem(n) for n in ("scored", "scanned", "tails_up", "chain_scanned", "turned", "turned_back", "shifted", "scaled",
                             "weighted", "fac", "fd"))
        messages, carried_ok, oh_ok, moved, summed, kept_ok, last_up, stored, osum_ok = (
            sem(n) for n in ("messages", "carried", "oh", "moved", "summed", "kept", "last_up", "stored", "osum"))

        block = ctx.enter_context(nc.Block())

        def windows(eng, g, body):
            body(g * NWIN, 0)
            with eng.Fori(1, NWIN) as j:
                body(g * NWIN + j, j)

        @block.sync
        def _(sp):
            def group(g):
                sp.wait_ge(kept_ok, g * NWIN)
                sp.wait_ge(cleared, 1)
                hold(sp)
                sp.dma_start(features[WINDOW:P, 0, :], epro[:, ds(g * GROUP, GROUP)]).then_inc(loaded, 16)
                sp.dma_start(pens[:, 0, :, :], pens_d[ds(g, 1), :].rearrange("g (k p) -> g k p", k=4)
                             .to_broadcast([H, 4, P])).then_inc(loaded, 16)
                w = sp.value_load(dst_first[0:1, ds(g, 1)], min_val=0, max_val=NP - P)

                def window(v, j):
                    sp.wait_ge(osum_ok, v + 1)
                    hold(sp)
                    sp.dma_start(agg_d[ds(w + j * P, P), :], osum[:, 0, :]).then_inc(stored, 16)
                    sp.wait_ge(stored, v * 16 + 16)
                    hold(sp)

                windows(sp, g, window)

            span_max = sp.value_load(widest[0:1, 0:1], min_val=0, max_val=NP)
            with sp.If(span_max >= WINDOW):
                turns(sp, NG)(group)

        @block.gpsimd
        def _(pool):
            def group(g):
                pool.wait_ge(kept_ok, g * NWIN)
                pool.tensor_copy(idx[:, 0, :], src_all[:, ds(g, 1), :].rearrange("p o t -> p (o t)")).then_inc(indexed, 1)
                pool.tensor_copy(idx[:, 1, :], dst_i[:, ds(g, 1), :].rearrange("p o t -> p (o t)")).then_inc(indexed, 1)
                pool.wait_ge(indexed, 2 * g + 2)
                hold(pool)
                for t in range(ET):
                    pool.indirect_dma_start(G[:, 0, t, :], None, table, bass.IndirectOffsetOnAxis(idx[:, 0, t:t + 1], 0)
                                            ).then_inc(gathered, 16)
                    pool.indirect_dma_start(rows_of_target[:, t, :], None, er_table, bass.IndirectOffsetOnAxis(idx[:, 1, t:t + 1], 0)
                                            ).then_inc(gathered, 16)

            span_max = pool.value_load(widest[0:1, 0:1], min_val=0, max_val=NP)
            with pool.If(span_max >= WINDOW):
                turns(pool, NG)(group)

        @block.vector
        def _(dve):
            def group(g):
                z3 = z[:, 0, :].rearrange("p (t n) -> p t n", t=ET)
                z4 = z[:, 0, :].rearrange("p (t h y) -> p t h y", t=ET, h=H)
                dve.wait_ge(gathered, 32 * ET * (g + 1))
                dve.wait_ge(edge_scores, g + 1)
                dve.tensor_tensor(z3, G[:, 0, :, DIM:ROW], pR[:, 0:ET * HT].rearrange("p (t n) -> p t n", t=ET),
                                  ALU.add).then_inc(scored, 1)
                dve.wait_ge(scored, 5 * g + 1)
                dve.tensor_tensor(z3, z3, rows_of_target[:, :, :], ALU.add).then_inc(scored, 1)
                dve.wait_ge(scored, 5 * g + 2)
                mk = mask_all[:, ds(g, 1), :, :].rearrange("p o t (h y) -> p (o t) h y", h=1).to_broadcast([P, ET, H, TYPES])
                dve.tensor_tensor(z4, z4, mk, ALU.mult).then_inc(scored, 1)
                dve.wait_ge(scored, 5 * g + 3)
                dve.tensor_reduce(e[:, :].rearrange("p (h t) -> p t h", h=H), z4, AX.X, ALU.add).then_inc(scored, 1)
                dve.wait_ge(scored, 5 * g + 4)
                dve.scalar_tensor_tensor(e[:, :], e[:, :], SLOPE, e[:, :], ALU.mult, ALU.max).then_inc(scored, 1)
                dve.wait_ge(scored, 5 * g + 5)
                dve.wait_ge(spread, 2 * g + 2)
                dve.tensor_tensor_scan(scan[:, 0, :], penx[:, 0, :], e[:, :], -BIG, ALU.add, ALU.max).then_inc(scanned, 1)
                dve.tensor_tensor_scan(scan[:, 1, ::-1], penx[:, 1, ::-1], e[:, ::-1], -BIG, ALU.add, ALU.max).then_inc(scanned, 1)
                dve.wait_ge(scanned, 3 * g + 2)
                dve.tensor_tensor(m[:, :], scan[:, 0, :], scan[:, 1, :], ALU.max).then_inc(scanned, 1)
                dve.wait_ge(chain_scanned, 3 * g)
                dve.tensor_copy(rb[:, 0, 0:1], rb[:, 0, P:P + 1]).then_inc(chain_scanned, 1)
                dve.wait_ge(chain_scanned, 3 * g + 1)
                dve.wait_ge(tails_up, g + 1)
                dve.wait_ge(loaded, 32 * g + 32)
                dve.tensor_tensor_scan(rb[:, 0, 1:P + 1], pens[:, 0, 2, :], pA[0:H, 0:P], rb[:, 0, 0:1],
                                       ALU.add, ALU.max).then_inc(chain_scanned, 1)
                dve.tensor_tensor_scan(lb[:, 0, P - 1::-1], pens[:, 0, 3, ::-1], pA[0:H, 2 * P - 1:P - 1:-1], -BIG,
                                       ALU.add, ALU.max).then_inc(chain_scanned, 1)
                dve.wait_ge(chain_scanned, 3 * g + 3)
                dve.tensor_tensor(turn[:, 0, :], rb[:, 0, 0:P], pens[:, 0, 0, :], ALU.add).then_inc(turned, 1)
                dve.tensor_tensor(turn[:, 1, :], lb[:, 0, 1:P + 1], pens[:, 0, 1, :], ALU.add).then_inc(turned, 1)
                dve.wait_ge(turned_back, g + 1)
                for k, pen in enumerate((pen_head, pen_tail)):
                    dve.tensor_tensor(ends[:, k, :].rearrange("p (h t) -> p h t", h=H), pen[:, ds(g, 1), :].to_broadcast([P, H, ET]),
                                      pB[:, k * H:(k + 1) * H].rearrange("p (h o) -> p h o", o=1).to_broadcast([P, H, ET]),
                                      ALU.add).then_inc(shifted, 1)
                dve.wait_ge(shifted, 5 * g + 2)
                dve.wait_ge(scanned, 3 * g + 3)
                dve.tensor_tensor(m[:, :], m[:, :], ends[:, 0, :], ALU.max).then_inc(shifted, 1)
                dve.wait_ge(shifted, 5 * g + 3)
                dve.tensor_tensor(m[:, :], m[:, :], ends[:, 1, :], ALU.max).then_inc(shifted, 1)
                dve.wait_ge(shifted, 5 * g + 4)
                dve.tensor_tensor(e[:, :], e[:, :], m[:, :], ALU.subtract).then_inc(shifted, 1)
                dve.tensor_tensor(fd[:, :], pB[0:1, 0:H], m[0:1, :].rearrange("p (h t) -> p h t", h=H)[:, :, 0],
                                  ALU.subtract).then_inc(fd_ok, 1)
                g4 = G[:, 0, :, 0:DIM].rearrange("p t (h d) -> p t h d", h=H)
                dve.wait_ge(weighted, g + 1)
                dve.tensor_tensor(g4, g4, G[:, 0, :, DIM:AGG].rearrange("p t (h o) -> p t h o", o=1)
                                  .to_broadcast([P, ET, H, GDIM]), ALU.mult).then_inc(messages, 1)
                dve.wait_ge(fac_ok, g + 1)
                dve.wait_ge(kept_ok, g * NWIN)
                dve.tensor_tensor(carried[:, 0:DIM].rearrange("p (h d) -> p h d", h=H), kept[:, 0:DIM].rearrange("p (h d) -> p h d", h=H),
                                  fac[:, :].rearrange("p (h o) -> p h o", o=1).to_broadcast([1, H, GDIM]), ALU.mult).then_inc(carried_ok, 1)
                dve.tensor_tensor(carried[:, DIM:AGG], kept[:, DIM:AGG], fac[:, :], ALU.mult).then_inc(carried_ok, 1)
                dve.wait_ge(carried_ok, 2 * g + 2)

                def window(v, j):
                    dve.wait_ge(oh_ok, 2 * v)
                    if isinstance(j, int):
                        dve.tensor_copy(distance[:, :], rel[:, ds(g, 1), :].rearrange("p o t -> p (o t)")).then_inc(moved, 1)
                        dve.tensor_tensor(to_last[:, :], span[:, ds(g, 1)], iota_col[:, :], ALU.subtract).then_inc(moved, 1)
                    else:
                        dve.tensor_scalar(distance[:, :], distance[:, :], -float(P), None, ALU.add).then_inc(moved, 1)
                        dve.tensor_scalar(to_last[:, :], to_last[:, :], -float(P), None, ALU.add).then_inc(moved, 1)
                    dve.wait_ge(moved, 2 * v + 2)
                    dve.wait_ge(summed, v)
                    dve.wait_ge(last_up, v)
                    dve.tensor_tensor(oh[:, :, :], iota_row[:, :].rearrange("p (o n) -> p o n", o=1).to_broadcast([P, ET, P]),
                                      distance[:, :].rearrange("p (t n) -> p t n", n=1).to_broadcast([P, ET, P]),
                                      ALU.is_equal).then_inc(oh_ok, 1)
                    dve.tensor_scalar(is_last[:, :], to_last[:, :], 0.0, None, ALU.is_equal).then_inc(oh_ok, 1)
                    dve.wait_ge(last_up, v + 1)
                    if isinstance(j, int):
                        dve.tensor_copy(kept[:, :], pC[0:1, 0:AGG]).then_inc(kept_ok, 1)
                    else:
                        dve.wait_ge(kept_ok, v)
                        dve.tensor_tensor(kept[:, :], kept[:, :], pC[0:1, 0:AGG], ALU.add).then_inc(kept_ok, 1)

                windows(dve, g, window)

            span_max = dve.value_load(widest[0:1, 0:1], min_val=0, max_val=NP)
            with dve.If(span_max >= WINDOW):
                dve.memset(features[0:WINDOW, 0, :], 0.0)
                dve.memset(rb[:, 0, :], -BIG)
                dve.memset(kept[:, :], 0.0)
                dve.memset(erw[0:WINDOW, 0, :], 0.0).then_inc(cleared, 1)
                dve.wait_ge(cleared, 1)
                turns(dve, NG)(group)

        @block.scalar
        def _(act):
            def group(g):
                for k, a in enumerate((pen_prev, pen_next)):
                    act.wait_ge(kept_ok, g * NWIN)
                    act.activation(penx[:, k, :].rearrange("p (h t) -> p h t", h=H), a[:, ds(g, 1), :].to_broadcast([P, H, ET]),
                                   ACT.Copy).then_inc(spread, 1)
                act.wait_ge(shifted, 5 * g + 5)
                act.activation(G[:, 0, :, DIM:AGG].rearrange("p t h -> p h t"), e[:, :].rearrange("p (h t) -> p h t", h=H),
                               ACT.Exp, scale=1.0 / 3).then_inc(weighted, 1)
                act.wait_ge(fd_ok, g + 1)
                act.activation(fac[:, :], fd[:, :], ACT.Exp, scale=1.0 / 3).then_inc(fac_ok, 1)

                def window(v, j):
                    act.wait_ge(summed, v + 1)
                    act.wait_ge(stored, v * 16)
                    act.activation(osum[:, 0, :], pO[:, 0:AGG], ACT.Copy).then_inc(osum_ok, 1)

                windows(act, g, window)

            span_max = act.value_load(widest[0:1, 0:1], min_val=0, max_val=NP)
            with act.If(span_max >= WINDOW):
                turns(act, NG)(group)

        @block.tensor
        def _(pe):
            def group(g):
                pe.wait_ge(cleared, 1)
                pe.wait_ge(loaded, 32 * g + 32)
                for t in range(ET):
                    part = pe.matmul(pR[:, t * HT:(t + 1) * HT], features[:, 0, t * P:(t + 1) * P], erw[:, 0, :], start=True, stop=True)
                part.then_inc(edge_scores, 1)
                pe.wait_ge(scanned, 3 * g + 2)
                pe.transpose(pA[0:H, 0:P], scan[:, 0, :].rearrange("p (h t) -> p h t", h=H)[:, :, ET - 1], ident[:, :])
                pe.transpose(pA[0:H, P:2 * P], scan[:, 1, :].rearrange("p (h t) -> p h t", h=H)[:, :, 0], ident[:, :]).then_inc(tails_up, 1)
                pe.wait_ge(turned, 2 * g + 2)
                hold(pe)
                pe.transpose(pB[:, 0:H], turn[:, 0, :], ident[0:H, 0:H])
                pe.transpose(pB[:, H:2 * H], turn[:, 1, :], ident[0:H, 0:H]).then_inc(turned_back, 1)

                def window(v, j):
                    pe.wait_ge(messages, g + 1)
                    pe.wait_ge(carried_ok, 2 * g + 2)
                    pe.wait_ge(oh_ok, 2 * v + 2)
                    pe.wait_ge(osum_ok, v)
                    for t in range(ET):
                        part = pe.matmul(pO[:, 0:AGG], oh[:, t, :], G[:, 0, t, 0:AGG], start=(t == 0),
                                         stop=(t == ET - 1 and not isinstance(j, int)))
                    if isinstance(j, int):
                        part = pe.matmul(pO[:, 0:AGG], e0[:, :], carried[:, :], start=False, stop=True)
                    part.then_inc(summed, 1)
                    pe.wait_ge(osum_ok, v + 1)
                    pe.wait_ge(kept_ok, v)
                    pe.matmul(pC[0:1, 0:AGG], is_last[:, :], osum[:, 0, :], start=True, stop=True).then_inc(last_up, 1)

                windows(pe, g, window)

            span_max = pe.value_load(widest[0:1, 0:1], min_val=0, max_val=NP)
            with pe.If(span_max >= WINDOW):
                turns(pe, NG)(group)


def feed_forward(nc, x, xnT_d, agg_d, mix, b_out, router, w1T, w3T, w2T, ident, eps_col, zeros, out):
    E = EXPERTS
    x2_d = nc.dram_tensor("x_after_mixing", [NP, DIM], F32).ap()
    sent_d = nc.dram_tensor("rows_by_expert", [E * CAP + BLK, SENT], F32).ap()
    y_d = nc.dram_tensor("expert_outputs", [2 * NP, DIM], F32).ap()
    with ExitStack() as outer:
        counts = outer.enter_context(nc.sbuf_tensor("counts", [P, E], F32))
        combine(nc, x, xnT_d, agg_d, mix, b_out, router, ident, eps_col, x2_d, sent_d, counts)
        experts(nc, sent_d, counts, w1T, w3T, w2T, ident, zeros, y_d)
        finish(nc, x2_d, y_d, out)


def combine(nc, x, xnT_d, agg_d, mix, b_out, router, ident, eps_col, x2_d, sent_d, counts):
    E = EXPERTS
    with ExitStack() as ctx:
        sb, ps, sem, sems, hold = tools(nc, ctx, "comb")
        xt, ag, xT = sb("x", [P, 2, DIM]), sb("agg", [P, 2, AGG]), sb("xT", [P, 2, KC * P])
        bias, rw, iota8 = sb("bias", [P, DIM]), sb("rw", [P, KC, E]), sb("iota8", [P, E])
        iota8_i = sb("iota8_i", [P, E], I32)
        den, rden, gr, x2 = sb("den", [P, 2, GHEADS]), sb("rden", [P, 2, GHEADS]), sb("gr", [P, 2, DIM]), sb("x2", [P, 2, DIM])
        xa, xb = sb("xa", [P, 2, DIM]), sb("xb", [P, 2, DIM])
        stats, mv, sd, rs = sb("stats", [P, 2, 6]), sb("mv", [P, 2, 2]), sb("sd", [P, 2]), sb("rs", [P, 2])
        xn, xT2 = sb("xn", [P, 2, DIM]), sb("xT2", [P, 2, KC * P])
        lg, top, nm, pr, sm, rsm = sb("lg", [P, 2, E]), sb("top", [P, 2, E]), sb("nm", [P, 2]), sb("pr", [P, 2, E]), sb("sm", [P, 2]), sb("rsm", [P, 2])
        topi, topf = sb("topi", [P, 2, E], mybir.dt.uint32), sb("topf", [P, 2, E])
        oh = sb("oh", [P, 2, 2, E])
        prn, tp, dn, rdn, gt = sb("prn", [P, 2, E]), sb("tp", [P, 2, E]), sb("dn", [P, 2]), sb("rdn", [P, 2]), sb("gt", [P, 2, E])
        pm, pT, pl = [ps("m0"), ps("m1")], [ps("T0"), ps("T1")], [ps("l0"), ps("l1")]
        const_in, counted, iota_ok = sem("const_in"), sem("counted"), sem("iota_ok")
        tile_in, mixed, turned, xT2_ok, routed, stored, sd_ok, x2_ok, xn_ok, mv_ok, pr_ok, nm_ok, lg_ok = (
            sems(n) for n in ("tile_in", "mixed", "turned", "xT2", "routed", "stored", "sd", "x2", "xn", "mv", "pr", "nm", "lg"))
        own = sems("own")
        OWN = 25
        valid, code, lim, trash = sb("valid", [P, NT]), sb("code", [P, NT, 2], I32), sb("lim", [P, NT]), sb("trash", [P, NT])
        node_i, ind, pos = sb("node_i", [P, NT], I32), sb("ind", [P, 2, E]), sb("pos", [P, 2, E])
        nxt, upper, ones = sb("nxt", [P, 2, E]), sb("upper", [P, P]), sb("ones", [P, P])
        pick, slot, slot_i = sb("pick", [P, 2, 2, E]), sb("slot", [P, 2, 2]), sb("slot_i", [P, 2, 2], I32)
        oh2, rows = sb("oh2", [P, 2, 2, E]), sb("rows", [P, 2, 2, SENT])
        ind_ok, ranked, pos_ok, slot_ok, sent, rows_ok = (sems(n) for n in ("ind", "ranked", "pos", "slot", "sent", "rows"))
        tri, consts = sem("tri"), sem("consts")
        block = ctx.enter_context(nc.Block())

        @block.sync
        def _(sp):
            sp.dma_start(bias[:, :], b_out.to_broadcast([P, DIM])).then_inc(const_in, 16)
            sp.dma_start(rw[:, :, :], router.rearrange("(k p) e -> p k e", p=P)).then_inc(const_in, 16)
            @turns(sp, NT // 2)
            def _(i):
                for b in range(2):
                    t = 2 * i + b
                    sp.wait_ge(x2_ok[b], i)
                    hold(sp)
                    sp.dma_start(xt[:, b, :], x[ds(t * P, P), :]).then_inc(tile_in[b], 16)
                    sp.dma_start(ag[:, b, :], agg_d[ds(t * P, P), :]).then_inc(tile_in[b], 16)
                    sp.dma_start(xT[:, b, :], xnT_d[ds(t, 1), :, :].rearrange("o p n -> (o p) n")).then_inc(tile_in[b], 16)

        @block.gpsimd
        def _(pool):
            pool.iota(iota8_i[:, :], [[1, E]], base=0, channel_multiplier=0).then_inc(counted, 1)
            pool.iota(node_i[:, :], [[P, NT]], base=0, channel_multiplier=1).then_inc(counted, 1)
            pool.iota(code[:, :, :], [[2 * P, NT], [1, 2]], base=0, channel_multiplier=2).then_inc(counted, 1)
            pool.memset(ones[:, :], 1.0).then_inc(counted, 1)
            pool.memset(upper[:, :], 1.0).then_inc(tri, 1)
            pool.wait_ge(tri, 1)
            pool.affine_select(out=upper[:, :], in_=upper[:, :], compare_op=ALU.is_gt, fill=0.0,
                               base=0, pattern=[[1, P]], channel_multiplier=-1).then_inc(counted, 1)
            @turns(pool, NT // 2)
            def _(i):
                for b in range(2):
                    t = 2 * i + b
                    pool.wait_ge(x2_ok[b], i + 1)
                    pool.dma_start(x2_d[ds(t * P, P), :], x2[:, b, :]).then_inc(stored[b], 16)
                    pool.wait_ge(slot_ok[b], i + 1)
                    pool.wait_ge(rows_ok[b], 3 * i + 3)
                    hold(pool)
                    for k in range(2):
                        pool.indirect_dma_start(sent_d, bass.IndirectOffsetOnAxis(slot_i[:, b, k:k + 1], 0), rows[:, b, k, :], None,
                                                bounds_check=E * CAP - 1, oob_is_err=False).then_inc(sent[b], 16)
            for b in range(2):
                pool.wait_ge(stored[b], 16 * (NT // 2))
                pool.wait_ge(sent[b], 32 * (NT // 2))

        @block.vector
        def _(dve):
            dve.wait_ge(counted, 5)
            dve.tensor_copy(iota8[:, :], iota8_i[:, :]).then_inc(iota_ok, 1)
            dve.tensor_copy(lim[:, :], node_i[:, :]).then_inc(iota_ok, 1)
            dve.wait_ge(iota_ok, 2)
            dve.tensor_scalar(valid[:, :], lim[:, :], float(NODES), None, ALU.is_lt).then_inc(iota_ok, 1)
            dve.tensor_scalar(nxt[:, 0, :], iota8[:, :], float(CAP), None, ALU.mult).then_inc(iota_ok, 1)
            dve.wait_ge(iota_ok, 4)
            dve.tensor_scalar(trash[:, :], valid[:, :], -TRASH, TRASH, ALU.mult, ALU.add).then_inc(iota_ok, 1)
            dve.wait_ge(iota_ok, 5)
            dve.wait_ge(const_in, 32)
            @turns(dve, NT // 2)
            def _(i):
                for b in range(2):
                    t = 2 * i + b
                    n = 0

                    def then(ins):
                        nonlocal n
                        n += 1
                        ins.then_inc(own[b], 1)
                        dve.wait_ge(own[b], OWN * i + n)

                    col = lambda a: a[:, b:b + 1]
                    dve.wait_ge(tile_in[b], 48 * i + 48)
                    then(dve.tensor_scalar(den[:, b, :], ag[:, b, DIM:AGG], 1e-30, None, ALU.max))
                    then(dve.reciprocal(rden[:, b, :], den[:, b, :]))
                    then(dve.tensor_tensor(gr[:, b, :].rearrange("p (h d) -> p h d", h=GHEADS), ag[:, b, 0:DIM].rearrange("p (h d) -> p h d", h=GHEADS),
                                           rden[:, b, :].rearrange("p (h o) -> p h o", o=1).to_broadcast([P, GHEADS, GDIM]), ALU.mult))
                    then(dve.tensor_tensor(xa[:, b, :], gr[:, b, :], xt[:, b, :], ALU.add))
                    dve.wait_ge(mixed[b], i + 1)
                    then(dve.tensor_tensor(xb[:, b, :], pm[b][:, 0:DIM], bias[:, :], ALU.add))
                    dve.wait_ge(stored[b], 16 * i)
                    dve.tensor_tensor(x2[:, b, :], xa[:, b, :], xb[:, b, :], ALU.add).then_inc(x2_ok[b], 1)
                    dve.wait_ge(x2_ok[b], i + 1)
                    then(dve.bn_stats(stats[:, b, :], x2[:, b, :]))
                    hold(dve)
                    dve.bn_aggr(mv[:, b, :], stats[:, b, :]).then_inc(mv_ok[b], 1)
                    dve.wait_ge(sd_ok[b], i + 1)
                    then(dve.reciprocal(col(rs), col(sd)))
                    dve.wait_ge(turned[b], i)
                    dve.wait_ge(rows_ok[b], 3 * i)
                    dve.tensor_scalar(xn[:, b, :], x2[:, b, :], mv[:, b, 0:1], col(rs), ALU.subtract, ALU.mult).then_inc(xn_ok[b], 1)
                    dve.wait_ge(routed[b], i + 1)
                    dve.tensor_copy(lg[:, b, :], pl[b][:, 0:E]).then_inc(lg_ok[b], 1)
                    dve.wait_ge(lg_ok[b], i + 1)
                    hold(dve)
                    then(dve.max(top[:, b, :], lg[:, b, :]))
                    hold(dve)
                    then(dve.max_index(topi[:, b, :], top[:, b, :], lg[:, b, :]))
                    then(dve.tensor_copy(topf[:, b, :], topi[:, b, :]))
                    dve.tensor_scalar(col(nm), top[:, b, 0:1], -1.0, None, ALU.mult).then_inc(nm_ok[b], 1)
                    dve.wait_ge(pr_ok[b], i + 1)
                    then(dve.tensor_reduce(col(sm), pr[:, b, :], AX.X, ALU.add))
                    then(dve.reciprocal(col(rsm), col(sm)))
                    then(dve.tensor_scalar(prn[:, b, :], pr[:, b, :], col(rsm), None, ALU.mult))
                    for k in range(2):
                        then(dve.tensor_scalar(oh[:, b, k, :], iota8[:, :], topf[:, b, k:k + 1], None, ALU.is_equal))
                    then(dve.tensor_tensor(tp[:, b, :], oh[:, b, 0, :], oh[:, b, 1, :], ALU.add))
                    dve.tensor_scalar(ind[:, b, :], tp[:, b, :], valid[:, ds(t, 1)], None, ALU.mult).then_inc(ind_ok[b], 1)
                    then(dve.tensor_tensor(gt[:, b, :], tp[:, b, :], prn[:, b, :], ALU.mult))
                    then(dve.tensor_reduce(col(dn), gt[:, b, :], AX.X, ALU.add))
                    then(dve.tensor_scalar(col(rdn), col(dn), 1e-9, None, ALU.add))
                    then(dve.reciprocal(col(dn), col(rdn)))
                    then(dve.tensor_scalar(tp[:, b, :], gt[:, b, :], col(dn), None, ALU.mult))
                    both = lambda a: a[:, b, :].rearrange("p (o e) -> p o e", o=1).to_broadcast([P, 2, E])
                    then(dve.tensor_tensor(oh2[:, b, :, :], oh[:, b, :, :], both(tp), ALU.mult))
                    dve.wait_ge(sent[b], 32 * i)
                    dve.tensor_reduce(rows[:, b, :, DIM + 1], oh2[:, b, :, :], AX.X, ALU.add).then_inc(rows_ok[b], 1)
                    dve.tensor_copy(rows[:, b, :, DIM:DIM + 1].bitcast(I32), code[:, ds(t, 1), :].rearrange("p o (k n) -> p (o k) n", n=1)).then_inc(rows_ok[b], 1)
                    dve.wait_ge(ranked[b], i + 1)
                    then(dve.tensor_tensor(pos[:, b, :], nxt[:, b, :], pl[b][:, E:2 * E], ALU.add))
                    dve.tensor_tensor(nxt[:, 1 - b, :], nxt[:, b, :], pl[b][:, 2 * E:3 * E], ALU.add).then_inc(pos_ok[b], 1)
                    then(dve.tensor_tensor(pick[:, b, :, :], oh[:, b, :, :], both(pos), ALU.mult))
                    then(dve.tensor_reduce(slot[:, b, :], pick[:, b, :, :], AX.X, ALU.add))
                    dve.tensor_scalar(slot_i[:, b, :], slot[:, b, :], trash[:, ds(t, 1)], None, ALU.add).then_inc(slot_ok[b], 1)
                    dve.wait_ge(pos_ok[b], i + 1)
                    assert n == OWN, n

            dve.tensor_copy(counts[:, :], nxt[:, 0, :]).then_inc(consts, 1)

        @block.scalar
        def _(act):
            @turns(act, NT // 2)
            def _(i):
                for b in range(2):
                    act.wait_ge(mv_ok[b], i + 1)
                    act.activation(sd[:, b:b + 1], mv[:, b, 1:2], ACT.Sqrt, bias=eps_col[:, 0:1]).then_inc(sd_ok[b], 1)
                    act.wait_ge(turned[b], i + 1)
                    act.wait_ge(stored[b], 16 * i)
                    act.activation(xT2[:, b, :], pT[b][:, 0:KC * P], ACT.Copy).then_inc(xT2_ok[b], 1)
                    act.wait_ge(sent[b], 32 * i)
                    act.activation(rows[:, b, :, 0:DIM], xn[:, b, :].rearrange("p (o n) -> p o n", o=1).to_broadcast([P, 2, DIM]),
                                   ACT.Copy).then_inc(rows_ok[b], 1)
                    act.wait_ge(nm_ok[b], i + 1)
                    act.activation(pr[:, b, :], lg[:, b, :], ACT.Exp, bias=nm[:, b:b + 1]).then_inc(pr_ok[b], 1)

        @block.tensor
        def _(pe):
            pe.wait_ge(const_in, 32)
            pe.wait_ge(counted, 5)
            @turns(pe, NT // 2)
            def _(i):
                for b in range(2):
                    pe.wait_ge(tile_in[b], 48 * i + 48)
                    pe.wait_ge(x2_ok[b], i)
                    for k in range(KC):
                        last = pe.matmul(pm[b][:, 0:DIM], xT[:, b, k * P:(k + 1) * P], mix[:, k, :], start=(k == 0), stop=(k == KC - 1))
                    last.then_inc(mixed[b], 1)
                    pe.wait_ge(xn_ok[b], i + 1)
                    pe.wait_ge(xT2_ok[b], i)
                    for k in range(KC):
                        last = pe.transpose(pT[b][:, k * P:(k + 1) * P], xn[:, b, k * P:(k + 1) * P], ident[:, :])
                    last.then_inc(turned[b], 1)
                    pe.wait_ge(xT2_ok[b], i + 1)
                    pe.wait_ge(lg_ok[b], i)
                    for k in range(KC):
                        last = pe.matmul(pl[b][:, 0:E], xT2[:, b, k * P:(k + 1) * P], rw[:, k, :], start=(k == 0), stop=(k == KC - 1))
                    last.then_inc(routed[b], 1)
                    pe.wait_ge(ind_ok[b], i + 1)
                    pe.wait_ge(pos_ok[b], i)
                    pe.matmul(pl[b][:, E:2 * E], upper[:, :], ind[:, b, :], start=True, stop=True)
                    pe.matmul(pl[b][:, 2 * E:3 * E], ones[:, :], ind[:, b, :], start=True, stop=True).then_inc(ranked[b], 1)


def experts(nc, sent_d, counts, w1T, w3T, w2T, ident, zeros, y_d):
    E, TB = EXPERTS, BLK // P
    with ExitStack() as ctx:
        sb, ps, sem, sems, hold = tools(nc, ctx, "ffn")
        w1, w3, w2 = sb("w1", [P, 2, KC, HP]), sb("w3", [P, 2, KC, HP]), sb("w2", [HW, 2, HC, DIM])
        xr, xT, y = sb("xr", [P, 2, TB, SENT]), sb("xT", [P, 2, KC, BLK]), sb("y", [P, 2, TB, DIM])
        s1, h = sb("s1", [HW, 2, 2, BLK]), sb("h", [HW, 3, 2, BLK])
        J = NP // BLK
        filler = sb("filler", [P, TB, SENT])
        cap_i, cap_f, cnt, step_i, step_f = sb("cap_i", [1, E], I32), sb("cap_f", [1, E]), sb("cnt", [1, E]), sb("step_i", [1, J], I32), sb("step_f", [1, J])
        more, nblk, ends = sb("more", [1, E, J]), sb("nblk", [1, E]), sb("ends", [1, E])
        blk_i, blk_f = sb("blk_i", [1, NBLK], I32), sb("blk_f", [1, NBLK])
        past, which, took, start = sb("past", [1, NBLK, E]), sb("which", [1, NBLK]), sb("took", [1, NBLK, E]), sb("start", [1, NBLK])
        row_f, row0, ex_f = sb("row_f", [1, NBLK]), sb("row0", [1, NBLK]), sb("ex_f", [1, NBLK])
        tab, fill_i, fill_f = sb("tab", [1, 2, NBLK], I32), sb("fill_i", [1, E], I32), sb("fill_f", [1, E])
        ph1, ph3, py, pT = [ps("h1a"), ps("h1b")], [ps("h3a"), ps("h3b")], [ps("ya"), ps("yb")], [ps("Ta"), ps("Tb")]
        counted, own, table_ok, filled = sem("counted"), sem("own"), sem("table_ok"), sem("filled")
        w_in, x_in, turned, xT_ok, y_up, y_ok, stored = (sems(n) for n in ("w_in", "x_in", "turned", "xT", "y_up", "y", "stored"))
        h_up, s_ok = sems("h_up"), sems("s")
        h_ok = sems("h", 3)
        y_used = sem("y_used")
        block = ctx.enter_context(nc.Block())

        @block.gpsimd
        def _(pool):
            pool.iota(cap_i[:, :], [[CAP, E]], base=0, channel_multiplier=0).then_inc(counted, 1)
            pool.iota(step_i[:, :], [[BLK, J]], base=0, channel_multiplier=0).then_inc(counted, 1)
            pool.iota(blk_i[:, :], [[1, NBLK]], base=0, channel_multiplier=0).then_inc(counted, 1)
            pool.iota(filler[:, :, DIM:DIM + 1].bitcast(I32), [[0, TB], [0, 1]], base=2 * NP, channel_multiplier=0).then_inc(counted, 1)

            @turns(pool, NBLK // 2)
            def _(i):
                for b in range(2):
                    pool.wait_ge(y_ok[b], TB * i + TB)
                    hold(pool)
                    for tt in range(TB):
                        pool.indirect_dma_start(y_d, bass.IndirectOffsetOnAxis(xr[:, b, tt, DIM:DIM + 1].bitcast(I32), 0),
                                                y[:, b, tt, :], None, bounds_check=2 * NODES - 1, oob_is_err=False).then_inc(stored[b], 16)
            for b in range(2):
                pool.wait_ge(stored[b], 16 * TB * (NBLK // 2))

        @block.vector
        def _(dve):
            n = 0

            def then(ins, sem=own):
                nonlocal n
                n += 1
                ins.then_inc(own, 1)
                dve.wait_ge(own, n)

            dve.wait_ge(counted, 4)
            then(dve.memset(filler[:, :, 0:DIM], 0.0))
            then(dve.memset(filler[:, :, DIM + 1:SENT], 0.0))
            then(dve.tensor_copy(cap_f[:, :], cap_i[:, :]))
            then(dve.tensor_copy(step_f[:, :], step_i[:, :]))
            then(dve.tensor_copy(blk_f[:, :], blk_i[:, :]))
            then(dve.tensor_copy(fill_i[:, :], counts[0:1, :]))
            then(dve.tensor_tensor(cnt[:, :], counts[0:1, :], cap_f[:, :], ALU.subtract))
            then(dve.tensor_tensor(more[:, :, :], cnt[:, :].rearrange("p (e o) -> p e o", o=1).to_broadcast([1, E, J]),
                                   step_f[:, :].rearrange("p (o j) -> p o j", o=1).to_broadcast([1, E, J]), ALU.is_gt))
            then(dve.tensor_reduce(nblk[:, :], more[:, :, :], AX.X, ALU.add))
            then(dve.tensor_copy(ends[:, :], nblk[:, :]))
            for e in range(1, E):
                then(dve.tensor_tensor(ends[:, e:e + 1], ends[:, e:e + 1], ends[:, e - 1:e], ALU.add))
            then(dve.tensor_tensor(past[:, :, :], blk_f[:, :].rearrange("p (s o) -> p s o", o=1).to_broadcast([1, NBLK, E]),
                                   ends[:, :].rearrange("p (o e) -> p o e", o=1).to_broadcast([1, NBLK, E]), ALU.is_ge))
            then(dve.tensor_reduce(which[:, :], past[:, :, :], AX.X, ALU.add))
            then(dve.tensor_tensor(took[:, :, :], past[:, :, :], nblk[:, :].rearrange("p (o e) -> p o e", o=1).to_broadcast([1, NBLK, E]), ALU.mult))
            then(dve.tensor_reduce(start[:, :], took[:, :, :], AX.X, ALU.add))
            then(dve.tensor_tensor(row0[:, :], blk_f[:, :], start[:, :], ALU.subtract))
            then(dve.tensor_scalar(row0[:, :], row0[:, :], float(BLK), None, ALU.mult))
            then(dve.scalar_tensor_tensor(row_f[:, :], which[:, :], float(CAP), row0[:, :], ALU.mult, ALU.add))
            then(dve.tensor_scalar(tab[:, 0, :], row_f[:, :], float(E * CAP), None, ALU.min))
            then(dve.tensor_scalar(tab[:, 1, :], which[:, :], float(E - 1), None, ALU.min))
            dve.sem_inc(table_ok, 1)

            @turns(dve, NBLK // 2)
            def _(i):
                for b in range(2):
                    s = 2 * i + b
                    for g in range(3):
                        q = (3 * b + g) % 2
                        nq = 3 * i + (3 * b + g) // 2
                        dve.wait_ge(s_ok[q], nq + 1)
                        dve.wait_ge(y_up[1 - b], TB * i + TB * b)
                        dve.tensor_tensor(h[:, g, :, :].rearrange("p c n -> p (c n)"), s1[:, q, :, :].rearrange("p c n -> p (c n)"),
                                          ph3[q][0:HW, :], ALU.mult).then_inc(h_ok[g], 1)
                    dve.wait_ge(stored[b], 16 * TB * i)
                    dve.wait_ge(y_up[b], TB * i + TB)
                    for tt in range(TB):
                        dve.tensor_scalar(y[:, b, tt, :], py[tt][:, 0:DIM], xr[:, b, tt, DIM + 1:SENT], None, ALU.mult).then_inc(y_ok[b], 1)

        @block.sync
        def _(sp):
            sp.wait_ge(table_ok, 1)
            for e in range(E):
                r0 = sp.value_load(fill_i[0:1, e:e + 1], min_val=0, max_val=E * CAP - BLK)
                sp.dma_start(sent_d[ds(r0, BLK), :].rearrange("(t p) n -> p t n", p=P), filler[:, :, :]).then_inc(filled, 16)
            sp.dma_start(sent_d[E * CAP:E * CAP + BLK, :].rearrange("(t p) n -> p t n", p=P), filler[:, :, :]).then_inc(filled, 16)
            sp.wait_ge(filled, 16 * (E + 1))

            @turns(sp, NBLK // 2)
            def _(i):
                for b in range(2):
                    s = 2 * i + b
                    r0 = sp.value_load(tab[0:1, 0, ds(s, 1)], min_val=0, max_val=E * CAP)
                    ex = sp.value_load(tab[0:1, 1, ds(s, 1)], min_val=0, max_val=E - 1)
                    sp.wait_ge(stored[b], 16 * TB * i)
                    hold(sp)
                    sp.dma_start(xr[:, b, :, :], sent_d[ds(r0, BLK), :].rearrange("(t p) n -> p t n", p=P)).then_inc(x_in[b], 16)
                    sp.wait_ge(y_up[b], TB * i)
                    hold(sp)
                    for w, wT in ((w1, w1T), (w3, w3T)):
                        sp.dma_start(w[:, b, :, :], wT[ds(ex, 1), :, :].rearrange("o (k p) n -> p (o k) n", p=P)).then_inc(w_in[b], 16)
                    sp.dma_start(w2[:, b, :, :], w2T[ds(ex, 1), :, :].rearrange("o (k p) n -> p (o k) n", p=HW)).then_inc(w_in[b], 16)

            sp.wait_ge(stored[0], 16 * TB * (NBLK // 2))
            sp.dma_start(xr[:, 0, :, :], sent_d[E * CAP:E * CAP + BLK, :].rearrange("(t p) n -> p t n", p=P)).then_inc(x_in[0], 16)

        @block.scalar
        def _(act):
            def transposed(i, b):
                act.wait_ge(turned[b], i + 1)
                act.activation(xT[:, b, :, :].rearrange("p k n -> p (k n)"), pT[b][:, :], ACT.Copy).then_inc(xT_ok[b], 1)

            @turns(act, NBLK // 2)
            def _(i):
                for b in range(2):
                    transposed(i, b)
                    for g in range(3):
                        q = (3 * b + g) % 2
                        nq = 3 * i + (3 * b + g) // 2
                        act.wait_ge(h_up[q], nq + 1)
                        act.activation(s1[:, q, :, :].rearrange("p c n -> p (c n)"), ph1[q][0:HW, :], ACT.Silu).then_inc(s_ok[q], 1)

        @block.tensor
        def _(pe):
            def transposes(i, b):
                pe.wait_ge(x_in[b], 16 * i + 16)
                pe.wait_ge(xT_ok[b], i)
                for k in range(KC):
                    for tt in range(TB):
                        last = pe.transpose(pT[b][:, k * BLK + tt * P:k * BLK + (tt + 1) * P], xr[:, b, tt, k * P:(k + 1) * P], ident[:, :])
                last.then_inc(turned[b], 1)

            def hidden(i, b, g):
                q = (3 * b + g) % 2
                for w, p in ((w1, ph1), (w3, ph3)):
                    for m in range(2):
                        for k in range(KC):
                            c0 = (2 * g + m) * HW
                            last = pe.matmul(p[q][0:HW, m * BLK:(m + 1) * BLK], w[:, b, k, c0:c0 + HW], xT[:, b, k, :],
                                             start=(k == 0), stop=(k == KC - 1))
                last.then_inc(h_up[q], 1)

            def outputs(s, b, g):
                pe.wait_ge(h_ok[g], s + 1)
                for tt in range(TB):
                    for m in range(2):
                        last = pe.matmul(py[tt][:, 0:DIM], h[:, g, m, tt * P:(tt + 1) * P], w2[:, b, 2 * g + m, :],
                                         start=(g == 0 and m == 0), stop=(g == 2 and m == 1))
                    if g == 2:
                        last.then_inc(y_up[b], 1)

            transposes(0, 0)

            @turns(pe, NBLK // 2)
            def _(i):
                for b in range(2):
                    s = 2 * i + b
                    pe.wait_ge(w_in[b], 48 * i + 48)
                    pe.wait_ge(xT_ok[b], i + 1)
                    pe.wait_ge(h_ok[1], s)
                    hidden(i, b, 0)
                    pe.wait_ge(h_ok[2], s)
                    hidden(i, b, 1)
                    pe.wait_ge(y_ok[1 - b], TB * (i + b))
                    outputs(s, b, 0)
                    hidden(i, b, 2)
                    outputs(s, b, 1)
                    if b == 0:
                        transposes(i, 1)
                    else:
                        transposes(i + 1, 0)
                    outputs(s, b, 2)


def finish(nc, x2_d, y_d, out):
    W = 4
    whole = NODES // (W * P)
    spans = [(r, min(P, NODES - r)) for r in range(whole * W * P, NODES, P)]
    with ExitStack() as ctx:
        sb, ps, sem, sems, hold = tools(nc, ctx, "fin")
        xt, yt, ys = sb("x", [P, 2, W, DIM]), sb("y", [P, 2, W, 2, DIM]), sb("ys", [P, 2, W, DIM])
        tile_in, sum_ok, done, stored = (sems(n) for n in ("tile_in", "sum", "done", "stored"))
        block = ctx.enter_context(nc.Block())
        steps = [(j * W * P, W, P) for j in range(whole)] + [(r, 1, n) for r, n in spans]

        @block.sync
        def _(sp):
            for j, (r, w, n) in enumerate(steps):
                b = j % 2
                sp.wait_ge(stored[b], 16 * (j // 2))
                sp.dma_start(xt[0:n, b, 0:w, :], x2_d[r:r + w * n, :].rearrange("(p w) d -> p w d", w=w)).then_inc(tile_in[b], 16)
                sp.dma_start(yt[0:n, b, 0:w, :, :], y_d[2 * r:2 * (r + w * n), :].rearrange("(p w k) d -> p w k d", w=w, k=2)).then_inc(tile_in[b], 16)

        @block.vector
        def _(dve):
            for j, (r, w, n) in enumerate(steps):
                b = j % 2
                dve.wait_ge(tile_in[b], 32 * (j // 2) + 32)
                dve.wait_ge(stored[b], 16 * (j // 2))
                dve.tensor_tensor(ys[0:n, b, 0:w, :], yt[0:n, b, 0:w, 0, :], yt[0:n, b, 0:w, 1, :], ALU.add).then_inc(sum_ok[b], 1)
                dve.wait_ge(sum_ok[b], j // 2 + 1)
                dve.tensor_tensor(ys[0:n, b, 0:w, :], ys[0:n, b, 0:w, :], xt[0:n, b, 0:w, :], ALU.add).then_inc(done[b], 1)

        @block.scalar
        def _(act):
            for j, (r, w, n) in enumerate(steps):
                b = j % 2
                act.wait_ge(done[b], j // 2 + 1)
                act.dma_start(out[r:r + w * n, :].rearrange("(p w) d -> p w d", w=w), ys[0:n, b, 0:w, :]).then_inc(stored[b], 16)
            for b in range(2):
                act.wait_ge(stored[b], 16 * ((len(steps) + 1 - b) // 2))


def kernel(**inputs):
    import concourse.bacc as bacc
    from concourse.bass_utils import run_bass_kernel_spmd

    a = {k: np.asarray(v) for k, v in inputs.items()}

    def rows(v, n):
        return np.concatenate([v, np.zeros((n - v.shape[0],) + v.shape[1:], v.dtype)])

    src = rows(a["src"], EP)
    dst = np.concatenate([a["dst"], np.full(EP - EDGES, NODES, a["dst"].dtype)])
    grouped = dst.reshape(NG, P, ET)
    head, tail = grouped[:, :, 0].reshape(-1), grouped[:, :, -1].reshape(-1)
    before = np.concatenate([np.full(1, -1, dst.dtype), tail[:-1]])
    after = np.concatenate([head[1:], np.full(1, -1, dst.dtype)])
    chain = [rows(v.reshape(NG, P), NG + 2) for v in (head, tail, before, after)]
    first, last = rows(grouped[:, 0, 0], NG + 2)[None], rows(grouped[:, -1, -1], NG + 2)[None]
    columns = rows(grouped.transpose(0, 2, 1).reshape(NG, GROUP), NG + 2)
    mask = rows(a["edge_attr_4"], EP).reshape(NG, P, ET, TYPES).transpose(1, 0, 2, 3)
    epro = rows(rows(a["edge_attr_16"], EP).reshape(NG, P, ET, EPRO).transpose(0, 2, 1, 3).reshape(NG, GROUP, EPRO), NG + 2)
    epro = epro.reshape((NG + 2) * GROUP, EPRO).T
    lr = np.zeros((GHEADS, GDIM, 2, GHEADS, TYPES), np.float32)
    for h in range(GHEADS):
        lr[h, :, 0, h] = a["L0_gnn_attn_l"][h]
        lr[h, :, 1, h] = a["L0_gnn_attn_r"][h]
    attn_m = a["L0_gnn_attn_m"].transpose(1, 0, 2).reshape(EPRO, HT)
    w_qkv = a["L0_mix_w_qkv"]

    def hidden_columns(w):
        out = np.zeros((EXPERTS, DIM, HP), w.dtype)
        out[:, :, :HID] = w.transpose(0, 2, 1)
        return out

    w2T = np.zeros((EXPERTS, HP, DIM), np.float32)
    w2T[:, :HID] = a["L0_ffn_w2"].transpose(0, 2, 1)
    arrays = dict(
        x=rows(a["x"], NP), src=src.reshape(NG, P, ET).transpose(1, 0, 2), dst=grouped.transpose(1, 0, 2),
        dst_first=first, dst_last=last, dst_head=chain[0], dst_tail=chain[1], dst_before=chain[2], dst_after=chain[3],
        dst_cols=columns, mask=mask, epro=epro, w_n=a["L0_gnn_W_n"], w_nT=a["L0_gnn_W_n"].T,
        attn_lr=lr.reshape(DIM, 2 * HT), attn_m=attn_m, w_kvT=w_qkv[INNER:].T, w_q=w_qkv[:INNER],
        w_oT=a["L0_mix_w_out"].T, b_out=a["L0_mix_b_out"][None], router=a["L0_ffn_router_w"].T,
        w1T=hidden_columns(a["L0_ffn_w1"]), w3T=hidden_columns(a["L0_ffn_w3"]), w2T=w2T)
    arrays = {f"in_{k}": np.ascontiguousarray(v) for k, v in arrays.items()}
    nc = bacc.Bacc("TRN2", target_bir_lowering=False, num_devices=1)
    aps = [nc.dram_tensor(k, v.shape, mybir.dt.from_np(v.dtype), kind="ExternalInput").ap() for k, v in arrays.items()]
    out = nc.dram_tensor("out_x", [NODES, DIM], F32, kind="ExternalOutput").ap()
    build(nc, *aps, out)
    r = run_bass_kernel_spmd(nc, [arrays], core_ids=[0])
    return r.results[0]["out_x"]
```

```python
from contextlib import ExitStack

import numpy as np
import concourse.bass as bass
from concourse import mybir

P = 128
F32 = mybir.dt.float32
I32 = mybir.dt.int32
ALU = mybir.AluOpType
ACT = mybir.ActivationFunctionType
AX = mybir.AxisListType
ds = bass.ds

NODES, DIM = 6250, 256
EDGES, EPRO, TYPES = 100000, 16, 4
GHEADS, GDIM = 8, 32
MHEADS, MDIM = 8, 64
INNER = MHEADS * MDIM
EXPERTS, HID = 8, 682
EPS = 1e-5
SLOPE = 0.2
BIG = 1e30

NT = 2 * -(-NODES // (2 * P))
NP = NT * P
KC = DIM // P
ET = 7
GROUP = ET * P
NG = 4 * -(-EDGES // (4 * GROUP))
EP = NG * GROUP
NBUF = 4
WINDOW = P - EPRO
NWIN = NT - 1
HT = GHEADS * TYPES
ROW = DIM + HT
AGG = DIM + GHEADS
HC = 6
HW = -(-HID // HC)
HP = HC * HW
SENT = DIM + 2
BLK = 2 * P
CAP = NP + BLK
NBLK = 2 * -(-((2 * NODES + EXPERTS * (BLK - 1)) // BLK) // 2)
TRASH = float(1 << 20)


def build(nc, x, src, dst, dst_first, dst_last, dst_head, dst_tail, dst_before, dst_after, dst_cols, mask, epro,
          w_n, w_nT, attn_lr, attn_m, w_kvT, w_q, w_oT, b_out, router, w1T, w3T, w2T, out):
    xnT_d = nc.dram_tensor("xn_transposed", [NT, P, KC * P], F32).ap()
    table = nc.dram_tensor("node_table", [NP, ROW], F32).ap()
    er_table = nc.dram_tensor("right_scores", [NP, HT], F32).ap()
    pens_d = nc.dram_tensor("chain_penalties", [NG + 2, 4 * P], F32).ap()
    agg_d = nc.dram_tensor("aggregate", [2 * NP, AGG], F32)
    with ExitStack() as ctx:
        ident = ctx.enter_context(nc.sbuf_tensor("ident", [P, P], F32))
        iota_row = ctx.enter_context(nc.sbuf_tensor("iota_row", [P, P], F32))
        iota_col = ctx.enter_context(nc.sbuf_tensor("iota_col", [P, 1], F32))
        zeros = ctx.enter_context(nc.sbuf_tensor("zeros", [P, 512], F32))
        eps_col = ctx.enter_context(nc.sbuf_tensor("eps_col", [P, 1], F32))
        mix = ctx.enter_context(nc.sbuf_tensor("mix_matrix", [P, KC, DIM], F32))
        constants(nc, ident, iota_row, iota_col, zeros, eps_col)
        project_and_mix(nc, x, w_n, w_nT, attn_lr, w_kvT, w_q, w_oT, ident, eps_col, zeros, xnT_d, table, er_table, agg_d, mix)
        edges(nc, src, dst, dst_first, dst_last, dst_head, dst_tail, dst_before, dst_after, dst_cols, mask, epro,
              attn_m, ident, iota_row, iota_col, zeros, table, er_table, pens_d, agg_d)
        feed_forward(nc, x, xnT_d, agg_d, mix, b_out, router, w1T, w3T, w2T, ident, eps_col, out)


def turns(eng, count, last=False):
    def run(body):
        body(0)
        with eng.Fori(1, count - last) as i:
            body(i)
        if last:
            body(count - 1)
    return run


def is_first(i):
    return isinstance(i, int) and i == 0


def tools(nc, ctx, tag):
    def sb(name, shape, dt=F32):
        return ctx.enter_context(nc.sbuf_tensor(f"{tag}_{name}", shape, dt))

    def ps(name):
        return ctx.enter_context(nc.psum_tensor(f"{tag}_{name}", [P, 512], F32))

    taken = []
    ctx.callback(lambda: (nc.clear_and_free_semaphores(taken), nc.all_engine_barrier()))

    def sem(name):
        taken.append(nc.alloc_semaphore(f"{tag}_{name}"))
        return taken[-1]

    passed = sem("passed")

    def hold(eng):
        eng.sem_inc(passed, 1)

    def sems(name, n=2):
        return [sem(f"{name}{j}") for j in range(n)]

    return sb, ps, sem, sems, hold


def constants(nc, ident, iota_row, iota_col, zeros, eps_col):
    with ExitStack() as ctx:
        sb, ps, sem, sems, hold = tools(nc, ctx, "const")
        row_i, col_i = sb("row_i", [P, P], I32), sb("col_i", [P, 1], I32)
        blank, counted = sem("blank"), sem("counted")
        block = ctx.enter_context(nc.Block())

        @block.gpsimd
        def _(pool):
            pool.memset(zeros[:, :], 0.0)
            pool.memset(eps_col[:, :], EPS)
            pool.memset(ident[:, :], 0.0).then_inc(blank, 1)
            pool.iota(row_i[:, :], [[1, P]], base=0, channel_multiplier=0).then_inc(counted, 1)
            pool.iota(col_i[:, :], [[1, 1]], base=0, channel_multiplier=1).then_inc(counted, 1)
            pool.wait_ge(blank, 1)
            pool.affine_select(out=ident[:, :], in_=ident[:, :], compare_op=ALU.not_equal, fill=1.0,
                               base=0, pattern=[[-1, P]], channel_multiplier=1)

        @block.vector
        def _(dve):
            dve.wait_ge(counted, 2)
            dve.tensor_copy(iota_row[:, :], row_i[:, :])
            dve.tensor_copy(iota_col[:, :], col_i[:, :])


def project_and_mix(nc, x, w_n, w_nT, attn_lr, w_kvT, w_q, w_oT, ident, eps_col, zeros, xnT_d, table, er_table, agg_d, mix):
    WID = DIM + 2 * HT
    KV = 2 * INNER
    PAIRS = INNER // P
    GROUPS = KV // MDIM
    TURNS = NT // 2
    with ExitStack() as ctx:
        sb, ps, sem, sems, hold = tools(nc, ctx, "proj")
        wn_T, lr = sb("wnT", [P, KC, DIM]), sb("lr", [P, KC, 2 * HT])
        wcat = sb("wcat", [P, KC, WID])
        wkv, wmean = sb("wkv", [P, KC, KV]), sb("wmean", [P, KC * GROUPS])
        wq, wo = sb("wq", [P, PAIRS, DIM]), sb("wo", [P, PAIRS, DIM])
        F32R = mybir.dt.float32r
        wcat_high, wcat_low = sb("wcat_high", [P, KC, WID], F32R), sb("wcat_low", [P, KC, WID], F32R)
        wkv_high, wkv_low = sb("wkv_high", [P, KC, KV], F32R), sb("wkv_low", [P, KC, KV], F32R)
        xT_high, xT_low = sb("xT_high", [P, 2, KC, P], F32R), sb("xT_low", [P, 2, KC, P], F32R)
        xt, xn = sb("x", [P, 2, DIM]), sb("xn", [P, 2, DIM])
        stats, mv = sb("stats", [P, 2, 6]), sb("mv", [P, 2, 2])
        sd, rs = sb("sd", [P, 2]), sb("rs", [P, 2])
        xT, proj = sb("xT", [P, 2, KC, P]), sb("proj", [P, 2, WID])
        sq, var, kv_sd = sb("sq", [P, 2, KV]), sb("var", [P, 2, GROUPS]), sb("kv_sd", [P, 2, GROUPS])
        sdp, rr = sb("sdp", [P, 2, MHEADS]), sb("rr", [P, 2, MHEADS])
        kn, vc = sb("kn", [P, 2, INNER]), sb("vc", [P, 2, INNER])
        dT, t1 = sb("dotsT", [P, PAIRS, P]), sb("t1", [P, PAIRS, DIM])
        pT, pP, pdots = ps("T"), [ps("P0"), ps("P1")], ps("dots")
        pkv = [[ps("k0"), ps("v0")], [ps("k1"), ps("v1")]]
        weights_in, scores_folded, wcat_ready, centre, centred, high_weights, low_weights, cleared = (
            sem(n) for n in ("weights_in", "scores_folded", "wcat_ready", "centre", "centred", "high_weights", "low_weights", "cleared"))
        x_in, stats_ok, mv_ok, sd_ok, rs_ok, xn_ok, turned, xT_ok, xT_high_ok, xT_low_ok, projected, proj_ok, xT_stored, proj_stored = (
            sems(n) for n in ("x_in", "stats", "mv", "sd", "rs", "xn", "turned", "xT", "xT_high", "xT_low", "projected", "proj_ok",
                              "xT_stored", "proj_stored"))
        kv_ok, sq_ok, var_ok, kv_sd_ok, sdp_ok, rr_ok, kn_ok, vc_ok, dots_ok = (
            sems(n) for n in ("kv", "sq", "var", "kv_sd", "sdp", "rr", "kn", "vc", "dots"))
        dots_done, dT_zero, dT_ok, t1_done, t1_ok, m_done, m_ok = (
            sem(n) for n in ("dots_done", "dT_zero", "dT_ok", "t1_done", "t1_ok", "m_done", "m_ok"))

        def other(i, b, d):
            return i + (b + d) // 2, (b + d) % 2

        def exists(i, b, d):
            return not isinstance(i, int) or 0 <= 2 * i + b + d < NT

        block = ctx.enter_context(nc.Block())

        @block.sync
        def _(sp):
            def load(i, b):
                sp.wait_ge(xn_ok[b], i)
                hold(sp)
                sp.dma_start(xt[:, b, :], x[ds((2 * i + b) * P, P), :]).then_inc(x_in[b], 16)

            load(0, 0)
            load(0, 1)
            sp.dma_start(wn_T[:, :, :], w_nT.rearrange("(k p) n -> p k n", p=P)).then_inc(weights_in, 16)
            sp.dma_start(lr[:, :, :], attn_lr.rearrange("(k p) n -> p k n", p=P)).then_inc(weights_in, 16)
            sp.dma_start(wcat[:, :, 0:DIM], w_n.rearrange("(k p) n -> p k n", p=P)).then_inc(weights_in, 16)
            sp.dma_start(wkv[:, :, :], w_kvT.rearrange("(k p) n -> p k n", p=P)).then_inc(weights_in, 16)
            sp.dma_start(wq[:, :, :], w_q.rearrange("(k p) n -> p k n", p=P)).then_inc(weights_in, 16)
            sp.dma_start(wo[:, :, :], w_oT.rearrange("(k p) n -> p k n", p=P)).then_inc(weights_in, 16)
            sp.dma_start(agg_d[0:NP, :].rearrange("(t p) n -> p t n", p=P), zeros[:, 0:AGG].rearrange("p (o n) -> p o n", o=1)
                         .to_broadcast([P, NT, AGG])).then_inc(cleared, 16)
            with sp.Fori(1, TURNS) as i:
                for b in range(2):
                    load(i, b)
            sp.wait_ge(cleared, 16)

        @block.gpsimd
        def _(pool):
            @turns(pool, TURNS)
            def _(i):
                for b in range(2):
                    t = 2 * i + b
                    pool.wait_ge(xT_ok[b], i + 1)
                    pool.dma_start(xnT_d[ds(t, 1), :, :].rearrange("o p n -> (o p) n"),
                                   xT[:, b, :, :].rearrange("p k n -> p (k n)")).then_inc(xT_stored[b], 16)
                    pool.wait_ge(proj_ok[b], i + 1)
                    pool.dma_start(table[ds(t * P, P), :], proj[:, b, 0:ROW]).then_inc(proj_stored[b], 16)
                    pool.dma_start(er_table[ds(t * P, P), :], proj[:, b, ROW:WID]).then_inc(proj_stored[b], 16)
            for b in range(2):
                pool.wait_ge(xT_stored[b], 16 * TURNS)
                pool.wait_ge(proj_stored[b], 32 * TURNS)

        @block.vector
        def _(dve):
            def moments(i, b):
                dve.wait_ge(x_in[b], 16 * i + 16)
                dve.bn_stats(stats[:, b, :], xt[:, b, :]).then_inc(stats_ok[b], 1)
                dve.wait_ge(stats_ok[b], i + 1)
                hold(dve)
                dve.bn_aggr(mv[:, b, :], stats[:, b, :]).then_inc(mv_ok[b], 1)

            def normalise(i, b):
                dve.wait_ge(sd_ok[b], i + 1)
                dve.reciprocal(rs[:, b:b + 1], sd[:, b:b + 1]).then_inc(rs_ok[b], 1)
                dve.wait_ge(rs_ok[b], i + 1)
                dve.wait_ge(turned[b], i)
                dve.tensor_scalar(xn[:, b, :], xt[:, b, :], mv[:, b, 0:1], rs[:, b:b + 1],
                                  ALU.subtract, ALU.mult).then_inc(xn_ok[b], 1)

            def low_nodes(i, b):
                dve.wait_ge(xT_high_ok[b], i + 1)
                dve.wait_ge(xT_ok[b], i + 1)
                dve.tensor_tensor(xT_low[:, b, :, :], xT[:, b, :, :], xT_high[:, b, :, :].bitcast(F32), ALU.subtract).then_inc(xT_low_ok[b], 1)

            def variances(i, b):
                dve.wait_ge(sq_ok[b], 2 * i + 2)
                dve.tensor_reduce(var[:, b, :], sq[:, b, :].rearrange("p (g d) -> p g d", d=MDIM), AX.X,
                                  ALU.add).then_inc(var_ok[b], 1)

            def scale_keys(i, b):
                dve.wait_ge(kv_sd_ok[b], i + 1)
                dve.tensor_tensor(sdp[:, b, :], kv_sd[:, b, 0:MHEADS], kv_sd[:, b, MHEADS:GROUPS],
                                  ALU.mult).then_inc(sdp_ok[b], 1)
                dve.wait_ge(sdp_ok[b], i + 1)
                dve.reciprocal(rr[:, b, :], sdp[:, b, :]).then_inc(rr_ok[b], 1)
                dve.wait_ge(rr_ok[b], i + 1)
                dve.wait_ge(dots_ok[b], i)
                dve.tensor_tensor(kn[:, b, :].rearrange("p (g d) -> p g d", d=MDIM),
                                  pkv[b][0][:, :].rearrange("p (g d) -> p g d", d=MDIM),
                                  rr[:, b, :].rearrange("p (g o) -> p g o", o=1).to_broadcast([P, MHEADS, MDIM]),
                                  ALU.mult).then_inc(kn_ok[b], 1)

            def keep_projection(i, b):
                dve.wait_ge(projected[b], i + 1)
                dve.wait_ge(proj_stored[b], 32 * i)
                dve.tensor_copy(proj[:, b, :], pP[b][:, 0:WID]).then_inc(proj_ok[b], 1)

            moments(0, 0)
            normalise(0, 0)
            moments(0, 1)
            normalise(0, 1)
            dve.wait_ge(scores_folded, 1)
            for k in range(KC):
                dve.tensor_copy(wcat[:, k, DIM:WID], pP[0][:, k * 2 * HT:(k + 1) * 2 * HT]).then_inc(wcat_ready, 1)
            dve.wait_ge(weights_in, 96)
            w3 = wkv[:, :, :].rearrange("p k (g d) -> p (k g) d", d=MDIM)
            dve.tensor_reduce(wmean[:, :], w3, AX.X, ALU.add).then_inc(centre, 1)
            dve.wait_ge(centre, 1)
            dve.tensor_scalar(wmean[:, :], wmean[:, :], 1.0 / MDIM, None, ALU.mult).then_inc(centre, 1)
            dve.wait_ge(centre, 2)
            dve.tensor_tensor(w3, w3, wmean[:, :].rearrange("p (g o) -> p g o", o=1).to_broadcast([P, KC * GROUPS, MDIM]),
                              ALU.subtract).then_inc(centred, 1)
            for k, (low, whole, high) in enumerate(((wcat_low, wcat, wcat_high), (wkv_low, wkv, wkv_high))):
                dve.wait_ge(high_weights, k + 1)
                dve.tensor_tensor(low[:, :, :], whole[:, :, :], high[:, :, :].bitcast(F32), ALU.subtract).then_inc(low_weights, 1)
            low_nodes(0, 0)

            @turns(dve, TURNS, last=True)
            def _(i):
                for b in range(2):
                    if exists(i, b, -1):
                        variances(*other(i, b, -1))
                    if exists(i, b, 1):
                        low_nodes(*other(i, b, 1))
                    if exists(i, b, 2):
                        moments(*other(i, b, 2))
                    if exists(i, b, -1):
                        scale_keys(*other(i, b, -1))
                    if exists(i, b, 2):
                        normalise(*other(i, b, 2))
                    keep_projection(i, b)
            variances(TURNS - 1, 1)
            scale_keys(TURNS - 1, 1)
            dve.memset(dT[:, :, :], 0.0).then_inc(dT_zero, 1)
            dve.wait_ge(dT_zero, 1)
            dve.wait_ge(dots_done, 1)
            pd = pdots[:, :].rearrange("p (q n) -> p q n", q=PAIRS)
            for h in range(2):
                s = slice(h * MDIM, (h + 1) * MDIM)
                dve.tensor_copy(dT[s, :, s], pd[s, :, s]).then_inc(dT_ok, 1)
            for q in range(PAIRS):
                dve.wait_ge(t1_done, q + 1)
                dve.tensor_copy(t1[:, q, :], pP[q % 2][:, 0:DIM]).then_inc(t1_ok, 1)
            for c in range(KC):
                dve.wait_ge(m_done, c + 1)
                dve.tensor_scalar(mix[:, c, :], pP[c][:, 0:DIM], 1.0 / NODES, None, ALU.mult).then_inc(m_ok, 1)

        @block.scalar
        def _(act):
            def deviation(i, b):
                act.wait_ge(mv_ok[b], i + 1)
                act.activation(sd[:, b:b + 1], mv[:, b, 1:2], ACT.Sqrt, bias=eps_col[:, 0:1]).then_inc(sd_ok[b], 1)

            def keep_turned(i, b):
                act.wait_ge(turned[b], i + 1)
                turned_b = pT[:, b * KC * P:(b + 1) * KC * P]
                act.wait_ge(kv_ok[b], i)
                act.activation(xT_high[:, b, :, :].rearrange("p k n -> p (k n)"), turned_b, ACT.Copy).then_inc(xT_high_ok[b], 1)
                act.wait_ge(xT_stored[b], 16 * i)
                act.wait_ge(xT_low_ok[b], i)
                act.activation(xT[:, b, :, :].rearrange("p k n -> p (k n)"), turned_b, ACT.Copy).then_inc(xT_ok[b], 1)

            def squares(i, b):
                act.wait_ge(kv_ok[b], i + 1)
                act.wait_ge(var_ok[b], i)
                for h in range(2):
                    act.activation(sq[:, b, h * INNER:(h + 1) * INNER], pkv[b][h][:, :], ACT.Square).then_inc(sq_ok[b], 1)

            def keep_values(i, b):
                act.wait_ge(dots_ok[b], i)
                act.activation(vc[:, b, :], pkv[b][1][:, :], ACT.Copy).then_inc(vc_ok[b], 1)

            def key_deviations(i, b):
                act.wait_ge(var_ok[b], i + 1)
                act.activation(kv_sd[:, b, :], var[:, b, :], ACT.Sqrt, bias=eps_col[:, 0:1],
                               scale=1.0 / MDIM).then_inc(kv_sd_ok[b], 1)

            deviation(0, 0)
            deviation(0, 1)
            keep_turned(0, 0)
            act.wait_ge(wcat_ready, KC)
            act.activation(wcat_high[:, :, :], wcat[:, :, :], ACT.Copy).then_inc(high_weights, 1)
            act.wait_ge(centred, 1)
            act.activation(wkv_high[:, :, :], wkv[:, :, :], ACT.Copy).then_inc(high_weights, 1)

            @turns(act, TURNS, last=True)
            def _(i):
                for b in range(2):
                    if exists(i, b, -1):
                        squares(*other(i, b, -1))
                    if exists(i, b, 1):
                        keep_turned(*other(i, b, 1))
                    if exists(i, b, -1):
                        keep_values(*other(i, b, -1))
                        key_deviations(*other(i, b, -1))
                    if exists(i, b, 2):
                        deviation(*other(i, b, 2))
            squares(TURNS - 1, 1)
            keep_values(TURNS - 1, 1)
            key_deviations(TURNS - 1, 1)

        @block.tensor
        def _(pe):
            def turn_nodes(i, b):
                pe.wait_ge(xn_ok[b], i + 1)
                pe.wait_ge(xT_ok[1 - b], i + b)
                for k in range(KC):
                    last = pe.transpose(pT[:, (b * KC + k) * P:(b * KC + k + 1) * P], xn[:, b, k * P:(k + 1) * P], ident[:, :])
                last.then_inc(turned[b], 1)

            def product(out, b, k, high, low):
                pe.matmul(out, xT_high[:, b, k, :], high, start=(k == 0), stop=False)
                pe.matmul(out, xT_high[:, b, k, :], low, start=False, stop=False)
                return pe.matmul(out, xT_low[:, b, k, :], high, start=False, stop=(k == KC - 1))

            def project(i, b):
                pe.wait_ge(xT_low_ok[b], i + 1)
                pe.wait_ge(proj_ok[b], i)
                for k in range(KC):
                    last = product(pP[b][:, 0:WID], b, k, wcat_high[:, k, :], wcat_low[:, k, :])
                last.then_inc(projected[b], 1)

            def keys_and_values(i, b):
                pe.wait_ge(kn_ok[b], i)
                pe.wait_ge(vc_ok[b], i)
                for h in range(2):
                    columns = slice(h * INNER, (h + 1) * INNER)
                    for k in range(KC):
                        last = product(pkv[b][h][:, :], b, k, wkv_high[:, k, columns], wkv_low[:, k, columns])
                last.then_inc(kv_ok[b], 1)

            def dots(i, b):
                pe.wait_ge(kn_ok[b], i + 1)
                pe.wait_ge(vc_ok[b], i + 1)
                for q in range(PAIRS):
                    last = pe.matmul(pdots[:, q * P:(q + 1) * P], vc[:, b, q * P:(q + 1) * P],
                                     kn[:, b, q * P:(q + 1) * P], start=False, stop=False, skip_group_check=True)
                last.then_inc(dots_ok[b], 1)

            pe.wait_ge(weights_in, 96)
            for m in range(KC):
                for k in range(KC):
                    last = pe.matmul(pP[0][:, m * 2 * HT:(m + 1) * 2 * HT], wn_T[:, k, m * P:(m + 1) * P],
                                     lr[:, k, :], start=(k == 0), stop=(k == KC - 1))
            last.then_inc(scores_folded, 1)
            pe.matmul(pdots[:, :], zeros[:, 0:P], zeros[:, :], start=True, stop=False, skip_group_check=True)
            turn_nodes(0, 0)
            pe.wait_ge(low_weights, 2)

            @turns(pe, TURNS, last=True)
            def _(i):
                for b in range(2):
                    if exists(i, b, 1):
                        turn_nodes(*other(i, b, 1))
                    project(i, b)
                    keys_and_values(i, b)
                    if exists(i, b, -1):
                        dots(*other(i, b, -1))
            dots(TURNS - 1, 1)
            pe.matmul(pdots[:, :], zeros[:, 0:P], zeros[:, :], start=False, stop=True,
                      skip_group_check=True).then_inc(dots_done, 1)
            pe.wait_ge(dT_ok, 2)
            pe.wait_ge(proj_ok[0], TURNS)
            pe.wait_ge(proj_ok[1], TURNS)
            for q in range(PAIRS):
                if q >= 2:
                    pe.wait_ge(t1_ok, q - 1)
                pe.matmul(pP[q % 2][:, 0:DIM], dT[:, q, :], wo[:, q, :], start=True, stop=True).then_inc(t1_done, 1)
            pe.wait_ge(t1_ok, PAIRS)
            for c in range(KC):
                for q in range(PAIRS):
                    last = pe.matmul(pP[c][:, 0:DIM], wq[:, q, c * P:(c + 1) * P], t1[:, q, :],
                                     start=(q == 0), stop=(q == PAIRS - 1))
                last.then_inc(m_done, 1)


def edges(nc, src, dst, dst_first, dst_last, dst_head, dst_tail, dst_before, dst_after, dst_cols, mask, epro, attn_m,
          ident, iota_row, iota_col, zeros, table, er_table, pens_d, agg_d):
    GA = NG + 2
    H, TT = GHEADS, TYPES
    with ExitStack() as ctx:
        sb, ps, sem, sems, hold = tools(nc, ctx, "edge")
        src_all, dst_i, dstf = sb("src_all", [P, NG, ET], I32), sb("dst_i", [P, NG, ET], I32), sb("dstf", [P, NG, ET])
        mask_all = sb("mask_all", [P, NG, ET, TT])
        first_i, last_i = sb("first_i", [P, GA], I32), sb("last_i", [P, GA], I32)
        first_f, wcol, span, last_ind = sb("first_f", [P, GA]), sb("wcol", [P, GA]), sb("span", [P, GA]), sb("last_ind", [P, GA])
        rel = sb("rel", [P, NG, ET])
        widest_f, widest = sb("widest_f", [P, 1]), sb("widest", [P, 1], I32)
        pen_prev, pen_next, pen_head, pen_tail = (sb(n, [P, GA, ET]) for n in ("pprev", "pnext", "phead", "ptail"))
        chain_i, chain_f = sb("chain_i", [GA, 4, P], I32), sb("chain_f", [GA, 4, P])
        chain_eq, chain_pen = sb("chain_eq", [GA, 3, P]), sb("chain_pen", [GA, 4, P])
        e0 = sb("e0", [1, P])
        wneg, one, gap = sb("wneg", [P, GA]), sb("one", [P, 1]), sb("gap", [WINDOW, 2, GROUP])
        dstb, oht, oh = sb("dstb", [P, 2, GROUP], I32), sb("oht", [P, 2, GROUP]), sb("oh", [P, 2, ET, P])
        erw, pens = sb("erw", [P, 2, HT]), sb("pens", [H, 2, 4, P])
        idx = sb("idx", [P, NBUF, ET], I32)
        G = sb("G", [P, NBUF, ET, ROW])
        penx, lastc = sb("penx", [P, 2, 2, H * ET]), sb("lastc", [P, 2])
        z, e, f1, b1, m, m2, q = (sb(n, [P, 2, w]) for n, w in (("z", ET * HT), ("e", H * ET), ("f1", H * ET), ("b1", H * ET),
                                                               ("m", H * ET), ("m2", H * ET), ("q", H * ET)))
        m3, uc, ud = sb("m3", [P, 2, H * ET]), sb("uc", [P, 2, H * ET]), sb("ud", [P, 2, H * ET])
        rb, lb, cc, dd = sb("rb", [H, 2, P + 1]), sb("lb", [H, 2, P + 1]), sb("cc", [H, 2, P]), sb("dd", [H, 2, P])
        fd, fac, cs = sb("fd", [1, 2, H]), sb("fac", [1, 2, H]), sb("cs", [1, 2, AGG])
        osum = sb("osum", [P, 2, AGG])
        pR, pA, pO, pC = [ps("R0"), ps("R1")], [ps("A0"), ps("A1")], [ps("O0"), ps("O1")], ps("C")
        pB = ps("B")

        indices_in, chain_in, small_in = sem("indices_in"), sem("chain_in"), sem("small_in")
        pre, chained, pens_stored = sem("pre"), sem("chained"), sem("pens_stored")
        ready = sem("ready")
        cols_in, feats_in, pens_in, oht_ok, oh_ok, r_done, z_ok, zm_ok, s_ok, e_ok, f_ok, b_ok, m_ok, tails_up = (
            sems(n) for n in ("cols_in", "feats_in", "pens_in", "oht", "oh", "r_done", "z", "zm", "s", "e", "f", "b", "m", "tails_up"))
        seed_ok, rscan_ok, lscan_ok, c_ok, d_ok, cd_up, uc_ok, ud_ok, m2_ok, m3_ok, q_ok, fd_ok, fac_ok, cs_ok = (
            sems(n) for n in ("seed", "rscan", "lscan", "c", "d", "cd_up", "uc", "ud", "m2", "m3", "q", "fd", "fac", "cs"))
        gap_ok = sems("gap")
        penx_ok, osum_ok, stored, carry_up = (sems(n) for n in ("penx", "osum", "stored", "carry_up"))
        idx_ok, gathered, p_ok, msg_ok, out_done = (sems(n, NBUF) for n in ("idx", "gathered", "p", "msg", "out_done"))

        def place(i, b):
            return 4 * i + b, b % 2, 2 * i + b // 2

        def before(i, b):
            return (i, b - 1) if b else (i - 1, 3)

        def after(i, b):
            return (i, b + 1) if b < 3 else (i + 1, 0)

        def wait_sums_of_two_before(eng, i, b):
            eng.wait_ge(out_done[(b + 2) % 4], i + b // 2)

        narrow = ExitStack()
        block = narrow.enter_context(nc.Block())

        @block.sync
        def _(sp):
            sp.dma_start(src_all[:, :, :], src).then_inc(indices_in, 16)
            sp.dma_start(dst_i[:, :, :], dst).then_inc(indices_in, 16)
            sp.dma_start(first_i[:, :], dst_first.to_broadcast([P, GA])).then_inc(indices_in, 16)
            sp.dma_start(last_i[:, :], dst_last.to_broadcast([P, GA])).then_inc(indices_in, 16)
            for n, a in enumerate((dst_head, dst_tail, dst_before, dst_after)):
                sp.dma_start(chain_i[:, n, :], a).then_inc(chain_in, 16)
            sp.dma_start(mask_all[:, :, :, :], mask).then_inc(small_in, 16)
            for c in range(2):
                sp.dma_start(erw[WINDOW:P, c, :], attn_m).then_inc(small_in, 16)

            def load(g, c, u):
                w = sp.value_load(dst_first[0:1, ds(g, 1)], min_val=0, max_val=NP - P)
                sp.wait_ge(oht_ok[c], u)
                hold(sp)
                sp.dma_start(dstb[:, c, :], dst_cols[ds(g, 1), :].to_broadcast([P, GROUP])).then_inc(cols_in[c], 16)
                sp.wait_ge(r_done[c], u)
                hold(sp)
                sp.dma_start(oht[WINDOW:P, c, :], epro[:, ds(g * GROUP, GROUP)]).then_inc(feats_in[c], 16)
                sp.dma_start(erw[0:WINDOW, c, :], er_table[ds(w, WINDOW), :]).then_inc(feats_in[c], 16)

            load(0, 0, 0)
            load(1, 1, 0)
            sp.wait_ge(chained, 1)
            sp.dma_start(pens_d.rearrange("g (k p) -> g k p", k=4), chain_pen[:, :, :]).then_inc(pens_stored, 16)
            sp.wait_ge(pens_stored, 16)

            def load_penalties(g, c, u):
                sp.wait_ge(c_ok[c], u)
                sp.wait_ge(d_ok[c], u)
                hold(sp)
                sp.dma_start(pens[:, c, :, :], pens_d[ds(g, 1), :].rearrange("g (k p) -> g k p", k=4)
                             .to_broadcast([H, 4, P])).then_inc(pens_in[c], 16)

            def store(g, c, u):
                w = sp.value_load(dst_first[0:1, ds(g, 1)], min_val=0, max_val=NP - P)
                sp.wait_ge(osum_ok[c], u + 1)
                hold(sp)
                sp.wait_ge(stored[1 - c], 16 * (u + c))
                hold(sp)
                sp.dma_start(agg_d[ds(w, P), :], osum[:, c, :]).then_inc(stored[c], 16)

            for g in range(2):
                load_penalties(g, g, 0)

            @turns(sp, NG // 4)
            def _(i):
                for b in range(4):
                    g, c, u = 4 * i + b, b % 2, 2 * i + b // 2
                    load(g + 2, c, u + 1)
                    if not (is_first(i) and b < 2):
                        store(g - 2, c, u - 1)
                    load_penalties(g + 2, c, u + 1)
            for c in range(2):
                store(NG - 2 + c, c, NG // 2 - 1)
            for c in range(2):
                sp.wait_ge(stored[c], 16 * (NG // 2))
                sp.wait_ge(cols_in[c], 16 * (NG // 2 + 1))
                sp.wait_ge(feats_in[c], 32 * (NG // 2 + 1))
                sp.wait_ge(pens_in[c], 16 * (NG // 2 + 1))

        @block.gpsimd
        def _(pool):
            pool.wait_ge(indices_in, 64)
            @turns(pool, NG // 4)
            def _(i):
                for b in range(4):
                    g = 4 * i + b
                    pool.wait_ge(out_done[b], i)
                    pool.tensor_copy(idx[:, b, :], src_all[:, ds(g, 1), :].rearrange("p o t -> p (o t)")).then_inc(idx_ok[b], 1)
                    pool.wait_ge(idx_ok[b], i + 1)
                    hold(pool)
                    for t in range(ET):
                        pool.indirect_dma_start(G[:, b, t, :], None, table, bass.IndirectOffsetOnAxis(idx[:, b, t:t + 1], 0)
                                                ).then_inc(gathered[b], 16)

        @block.vector
        def _(dve):
            dve.wait_ge(indices_in, 64)
            n = 0

            def then(ins):
                nonlocal n
                n += 1
                ins.then_inc(pre, 1)
                dve.wait_ge(pre, n)

            then(dve.tensor_copy(dstf[:, :, :], dst_i[:, :, :]))
            then(dve.tensor_copy(first_f[:, :], first_i[:, :]))
            then(dve.tensor_copy(span[:, :], last_i[:, :]))
            then(dve.tensor_tensor(span[:, :], span[:, :], first_f[:, :], ALU.subtract))
            then(dve.tensor_reduce(widest_f[:, :], span[:, :], AX.X, ALU.max))
            then(dve.tensor_copy(widest[:, :], widest_f[:, :]))
            then(dve.tensor_scalar(last_ind[:, :], span[:, :], iota_col[:, 0:1], None, ALU.is_equal))
            then(dve.tensor_scalar(wcol[:, :], first_f[:, :], iota_col[:, 0:1], None, ALU.add))
            then(dve.tensor_scalar(wneg[:, :], wcol[:, :], -1.0, None, ALU.mult))
            then(dve.memset(one[:, :], 1.0))
            then(dve.tensor_tensor(rel[:, :, :], dstf[:, :, :], first_f[:, 0:NG].rearrange("p (g o) -> p g o", o=1)
                                   .to_broadcast([P, NG, ET]), ALU.subtract))
            for a in (pen_prev, pen_next, pen_head, pen_tail):
                then(dve.memset(a[:, :, :], 0.0))
            then(dve.tensor_tensor(pen_prev[:, 0:NG, 1:ET], dstf[:, :, 1:ET], dstf[:, :, 0:ET - 1], ALU.is_equal))
            then(dve.tensor_tensor(pen_next[:, 0:NG, 0:ET - 1], dstf[:, :, 1:ET], dstf[:, :, 0:ET - 1], ALU.is_equal))
            then(dve.tensor_tensor(pen_head[:, 0:NG, :], dstf[:, :, :], dstf[:, :, 0:1].to_broadcast([P, NG, ET]), ALU.is_equal))
            then(dve.tensor_tensor(pen_tail[:, 0:NG, :], dstf[:, :, :], dstf[:, :, ET - 1:ET].to_broadcast([P, NG, ET]), ALU.is_equal))
            for a in (pen_prev, pen_next, pen_head, pen_tail):
                then(dve.tensor_scalar(a[:, :, :], a[:, :, :], -1.0, BIG, ALU.add, ALU.mult))
            dve.wait_ge(chain_in, 64)
            then(dve.tensor_copy(chain_f[:, :, :], chain_i[:, :, :]))
            head, tail, prev_tail, next_head = (chain_f[:, k, :] for k in range(4))
            for k, (x0, x1) in enumerate(((head, prev_tail), (tail, next_head), (head, tail))):
                then(dve.tensor_tensor(chain_eq[:, k, :], x0, x1, ALU.is_equal))
            then(dve.tensor_scalar(chain_eq[:, :, :], chain_eq[:, :, :], -1.0, BIG, ALU.add, ALU.mult))
            then(dve.tensor_copy(chain_pen[:, 0:2, :], chain_eq[:, 0:2, :]))
            then(dve.tensor_tensor(chain_pen[:, 2:4, :], chain_eq[:, 0:2, :], chain_eq[:, 2:3, :].to_broadcast([GA, 2, P]), ALU.add))
            dve.memset(e0[:, :], 0.0).then_inc(chained, 1)
            then(dve.memset(rb[:, :, :], -BIG))
            then(dve.memset(lb[:, :, :], -BIG))
            dve.wait_ge(chained, 1)
            dve.memset(e0[:, 0:1], 1.0).then_inc(ready, 1)
            dve.wait_ge(small_in, 48)

            def step(i, b, front, back):
                g, c, u = place(i, b)
                ip, bp = before(i, b)
                gp, cp, up = place(ip, bp)
                m_ht = [a[:, cp, :].rearrange("p (h t) -> p h t", h=H) for a in (m, uc, ud, m2, m3)]
                z4 = z[:, c, :].rearrange("p (t h y) -> p t h y", t=ET, h=H)
                if front:
                    dve.wait_ge(gathered[b], 16 * ET * (i + 1))
                    dve.wait_ge(r_done[c], u + 1)
                    dve.tensor_tensor(z[:, c, :].rearrange("p (t n) -> p t n", t=ET), G[:, b, :, DIM:ROW],
                                      pR[c][:, 0:ET * HT].rearrange("p (t n) -> p t n", t=ET), ALU.add).then_inc(z_ok[c], 1)
                if back:
                    pc = [pB[:, cp * 2 * H + k * H:cp * 2 * H + (k + 1) * H].rearrange("p (h o) -> p h o", o=1).to_broadcast([P, H, ET]) for k in range(2)]
                    pen = [a[:, ds(gp, 1), :].to_broadcast([P, H, ET]) for a in (pen_head, pen_tail)]
                    dve.wait_ge(cd_up[cp], up + 1)
                    dve.tensor_tensor(m_ht[1], pen[0], pc[0], ALU.add).then_inc(uc_ok[cp], 1)
                    dve.tensor_tensor(m_ht[2], pen[1], pc[1], ALU.add).then_inc(ud_ok[cp], 1)
                if front:
                    mk = mask_all[:, ds(g, 1), :, :].rearrange("p o t (h y) -> p (o t) h y", h=1).to_broadcast([P, ET, H, TT])
                    dve.wait_ge(z_ok[c], u + 1)
                    dve.tensor_tensor(z4, z4, mk, ALU.mult).then_inc(zm_ok[c], 1)
                if back:
                    dve.wait_ge(uc_ok[cp], up + 1)
                    dve.wait_ge(m_ok[cp], up + 1)
                    dve.tensor_tensor(m2[:, cp, :], m[:, cp, :], uc[:, cp, :], ALU.max).then_inc(m2_ok[cp], 1)
                if front:
                    dve.wait_ge(zm_ok[c], u + 1)
                    dve.tensor_reduce(e[:, c, :].rearrange("p (h t) -> p t h", h=H), z4, AX.X, ALU.add).then_inc(s_ok[c], 1)
                if back:
                    dve.wait_ge(ud_ok[cp], up + 1)
                    dve.wait_ge(m2_ok[cp], up + 1)
                    dve.tensor_tensor(m3[:, cp, :], m2[:, cp, :], ud[:, cp, :], ALU.max).then_inc(m3_ok[cp], 1)
                if front:
                    dve.wait_ge(s_ok[c], u + 1)
                    dve.scalar_tensor_tensor(e[:, c, :], e[:, c, :], SLOPE, e[:, c, :], ALU.mult, ALU.max).then_inc(e_ok[c], 1)
                if back:
                    dve.wait_ge(m3_ok[cp], up + 1)
                    dve.tensor_tensor(q[:, cp, :], e[:, cp, :], m3[:, cp, :], ALU.subtract).then_inc(q_ok[cp], 1)
                    dve.tensor_tensor(fd[:, cp, :], pB[0:1, cp * 2 * H:cp * 2 * H + H], m_ht[4][0:1, :, 0], ALU.subtract).then_inc(fd_ok[cp], 1)
                if front:
                    dve.wait_ge(e_ok[c], u + 1)
                    dve.wait_ge(penx_ok[c], 2 * u + 2)
                    dve.tensor_tensor_scan(f1[:, c, :], penx[:, c, 0, :], e[:, c, :], -BIG, ALU.add, ALU.max).then_inc(f_ok[c], 1)
                    dve.tensor_tensor_scan(b1[:, c, ::-1], penx[:, c, 1, ::-1], e[:, c, ::-1], -BIG, ALU.add, ALU.max).then_inc(b_ok[c], 1)
                    dve.wait_ge(b_ok[c], u + 1)
                    dve.tensor_tensor(m[:, c, :], f1[:, c, :], b1[:, c, :], ALU.max).then_inc(m_ok[c], 1)
                if back:
                    g4 = G[:, bp, :, 0:DIM].rearrange("p t (h d) -> p t h d", h=H)
                    dve.wait_ge(p_ok[bp], ip + 1)
                    dve.tensor_tensor(g4, g4, G[:, bp, :, DIM:AGG].rearrange("p t (h o) -> p t h o", o=1)
                                      .to_broadcast([P, ET, H, GDIM]), ALU.mult).then_inc(msg_ok[bp], 1)
                if front:
                    if back:
                        dve.wait_ge(rscan_ok[cp], up + 1)
                    dve.tensor_copy(rb[:, c, 0:1], rb[:, 1 - c, P:P + 1]).then_inc(seed_ok[c], 1)
                    dve.wait_ge(tails_up[c], u + 1)
                    dve.wait_ge(pens_in[c], 16 * u + 16)
                    dve.tensor_tensor_scan(rb[:, c, 1:P + 1], pens[:, c, 2, :], pA[c][0:H, 0:P], rb[:, 1 - c, P:P + 1],
                                           ALU.add, ALU.max).then_inc(rscan_ok[c], 1)
                    dve.tensor_tensor_scan(lb[:, c, P - 1::-1], pens[:, c, 3, ::-1], pA[c][0:H, 2 * P - 1:P - 1:-1], -BIG,
                                           ALU.add, ALU.max).then_inc(lscan_ok[c], 1)
                if front:
                    dve.wait_ge(rscan_ok[c], u + 1)
                    dve.wait_ge(seed_ok[c], u + 1)
                    dve.wait_ge(cd_up[c], u)
                    dve.tensor_tensor(cc[:, c, :], rb[:, c, 0:P], pens[:, c, 0, :], ALU.add).then_inc(c_ok[c], 1)
                    dve.wait_ge(lscan_ok[c], u + 1)
                    dve.tensor_tensor(dd[:, c, :], lb[:, c, 1:P + 1], pens[:, c, 1, :], ALU.add).then_inc(d_ok[c], 1)
                    if not (is_first(i) and b < 2):
                        wait_sums_of_two_before(dve, i, b)
                    dve.tensor_tensor(oh[:, c, :, :], iota_row[:, :].rearrange("p (o n) -> p o n", o=1).to_broadcast([P, ET, P]),
                                      rel[:, ds(g, 1), :].rearrange("p o (t n) -> p (o t) n", n=1).to_broadcast([P, ET, P]),
                                      ALU.is_equal).then_inc(oh_ok[c], 1)
                if back:
                    if not (is_first(ip) and bp < 2):
                        wait_sums_of_two_before(dve, ip, bp)
                    dve.wait_ge(fac_ok[cp], up + 1)
                    dve.wait_ge(carry_up[1 - cp], up + 1)
                    dve.tensor_tensor(cs[:, cp, 0:DIM].rearrange("p (h d) -> p h d", h=H), pC[0:1, 0:DIM].rearrange("p (h d) -> p h d", h=H),
                                      fac[:, cp, :].rearrange("p (h o) -> p h o", o=1).to_broadcast([1, H, GDIM]), ALU.mult).then_inc(cs_ok[cp], 1)
                    dve.tensor_tensor(cs[:, cp, DIM:AGG], pC[0:1, DIM:AGG], fac[:, cp, :], ALU.mult).then_inc(cs_ok[cp], 1)

            @turns(dve, NG // 4)
            def _(i):
                for b in range(4):
                    step(i, b, True, not (is_first(i) and b == 0))
            step(NG // 4, 0, False, True)

        @block.scalar
        def _(act):
            act.wait_ge(ready, 1)

            def one_hot_nodes(i, b):
                g, c, u = place(i, b)
                act.wait_ge(cols_in[c], 16 * u + 16)
                act.activation(gap[:, c, :], dstb[0:WINDOW, c, :], ACT.Abs, bias=wneg[0:WINDOW, ds(g, 1)]).then_inc(gap_ok[c], 1)
                act.wait_ge(gap_ok[c], u + 1)
                act.wait_ge(r_done[c], u)
                act.activation(oht[0:WINDOW, c, :], gap[:, c, :], ACT.Relu, bias=one[0:WINDOW, 0:1], scale=-1.0).then_inc(oht_ok[c], 1)

            def spread_penalties(i, b):
                g, c, u = place(i, b)
                act.wait_ge(b_ok[c], u)
                for k, a in enumerate((pen_prev, pen_next)):
                    act.activation(penx[:, c, k, :].rearrange("p (h t) -> p h t", h=H), a[:, ds(g, 1), :].to_broadcast([P, H, ET]),
                                   ACT.Copy).then_inc(penx_ok[c], 1)

            def keep_sums(i, b):
                g, c, u = place(i, b)
                if not (is_first(i) and b < 2):
                    act.wait_ge(carry_up[c], u + c)
                act.activation(lastc[:, c:c + 1], last_ind[:, ds(g, 1)], ACT.Copy)
                act.wait_ge(out_done[b], i + 1)
                if not (is_first(i) and b < 2):
                    act.wait_ge(stored[c], 16 * u)
                act.activation(osum[:, c, :], pO[c][:, 0:AGG], ACT.Copy).then_inc(osum_ok[c], 1)

            def weights(i, b):
                g, c, u = place(i, b)
                act.wait_ge(q_ok[c], u + 1)
                act.activation(G[:, b, :, DIM:AGG].rearrange("p t h -> p h t"), q[:, c, :].rearrange("p (h t) -> p h t", h=H),
                               ACT.Exp, scale=1.0 / 3).then_inc(p_ok[b], 1)
                act.wait_ge(fd_ok[c], u + 1)
                act.wait_ge(cs_ok[c], 2 * u)
                act.activation(fac[:, c, :], fd[:, c, :], ACT.Exp, scale=1.0 / 3).then_inc(fac_ok[c], 1)

            spread_penalties(0, 0)
            one_hot_nodes(0, 0)

            def step(i, b, front, back, sums):
                if back:
                    weights(*before(i, b))
                if front:
                    one_hot_nodes(*after(i, b))
                    spread_penalties(*after(i, b))
                if sums:
                    keep_sums(*before(*before(i, b)))

            @turns(act, NG // 4)
            def _(i):
                for b in range(4):
                    step(i, b, True, not (is_first(i) and b < 1), not (is_first(i) and b < 2))
            step(NG // 4, 0, False, True, True)
            step(NG // 4, 1, False, False, True)

        @block.tensor
        def _(pe):
            pe.wait_ge(ready, 1)
            pe.wait_ge(small_in, 48)

            def scores(i, b):
                g, c, u = place(i, b)
                pe.wait_ge(oht_ok[c], u + 1)
                pe.wait_ge(feats_in[c], 32 * u + 32)
                pe.wait_ge(z_ok[c], u)
                for t in range(ET):
                    last = pe.matmul(pR[c][:, t * HT:(t + 1) * HT], oht[:, c, t * P:(t + 1) * P], erw[:, c, :], start=True, stop=True)
                last.then_inc(r_done[c], 1)

            def carry(i, b):
                g, c, u = place(i, b)
                pe.wait_ge(osum_ok[c], u + 1)
                pe.matmul(pC[0:1, 0:AGG], lastc[:, c:c + 1], osum[:, c, :], start=True, stop=True).then_inc(carry_up[c], 1)

            def turn_ends(i, b):
                g, c, u = place(i, b)
                ends = [a[:, c, :].rearrange("p (h t) -> p h t", h=H) for a in (f1, b1)]
                pe.wait_ge(f_ok[c], u + 1)
                pe.wait_ge(b_ok[c], u + 1)
                pe.wait_ge(rscan_ok[c], u)
                pe.wait_ge(lscan_ok[c], u)
                pe.transpose(pA[c][0:H, 0:P], ends[0][:, :, ET - 1], ident[:, :])
                pe.transpose(pA[c][0:H, P:2 * P], ends[1][:, :, 0], ident[:, :]).then_inc(tails_up[c], 1)

            def turn_back(i, b):
                g, c, u = place(i, b)
                pe.wait_ge(c_ok[c], u + 1)
                pe.wait_ge(d_ok[c], u + 1)
                pe.wait_ge(fd_ok[c], u)
                pe.wait_ge(ud_ok[c], u)
                hold(pe)
                pe.transpose(pB[:, c * 2 * H:c * 2 * H + H], cc[:, c, :], ident[0:H, 0:H])
                pe.transpose(pB[:, c * 2 * H + H:c * 2 * H + 2 * H], dd[:, c, :], ident[0:H, 0:H]).then_inc(cd_up[c], 1)

            def sums(i, b):
                g, c, u = place(i, b)
                pe.wait_ge(msg_ok[b], i + 1)
                pe.wait_ge(oh_ok[c], u + 1)
                pe.wait_ge(osum_ok[c], u)
                for t in range(ET):
                    pe.matmul(pO[c][:, 0:AGG], oh[:, c, t, :], G[:, b, t, 0:AGG], start=(t == 0), stop=False)

            def add_carried(i, b):
                g, c, u = place(i, b)
                pe.wait_ge(cs_ok[c], 2 * u + 2)
                pe.matmul(pO[c][:, 0:AGG], e0[:, :], cs[:, c, :], start=False, stop=True).then_inc(out_done[b], 1)

            def step(i, b, front, back, carried):
                if front:
                    turn_ends(i, b)
                    scores(*after(i, b))
                if carried:
                    carry(*before(*before(i, b)))
                if front:
                    turn_back(i, b)
                if back:
                    sums(*before(i, b))
                    add_carried(*before(i, b))

            pe.matmul(pC[0:1, 0:AGG], zeros[:, 0:1], zeros[:, 0:AGG], start=True, stop=True).then_inc(carry_up[1], 1)
            scores(0, 0)

            @turns(pe, NG // 4)
            def _(i):
                for b in range(4):
                    step(i, b, True, not (is_first(i) and b < 1), not (is_first(i) and b < 2))
            step(NG // 4, 0, False, True, True)
            step(NG // 4, 1, False, False, True)

        narrow.close()
        edges_of_wide_groups(nc, widest, src_all, dst_i, dst_first, rel, span, mask_all, (pen_prev, pen_next, pen_head, pen_tail),
                             e0, oht, erw, pens, oh[:, 0], (pR[0], pA[0], pB, pO[0], pC), G, z, rb, lb, osum, epro, ident, iota_row, iota_col, table, er_table,
                             pens_d, agg_d)


def edges_of_wide_groups(nc, widest, src_all, dst_i, dst_first, rel, span, mask_all, edge_pens, e0, features, erw, pens,
                         oh, banks, G, z, rb, lb, osum, epro, ident, iota_row, iota_col, table, er_table, pens_d, agg_d):
    H = GHEADS
    pen_prev, pen_next, pen_head, pen_tail = edge_pens
    with ExitStack() as ctx:
        sb, ps, sem, sems, hold = tools(nc, ctx, "wide")
        idx, rows_of_target = sb("idx", [P, 2, ET], I32), sb("rows_of_target", [P, ET, HT])
        pair = [P, 2, H * ET]
        penx, scan = sb("penx", pair), sb("scan", pair)
        e, m, ends = sb("e", [P, H * ET]), sb("m", [P, H * ET]), sb("ends", pair)
        turn, fd, fac = sb("turn", [H, 2, P]), sb("fd", [1, H]), sb("fac", [1, H])
        kept, carried = sb("kept", [1, AGG]), sb("carried", [1, AGG])
        distance, to_last, is_last = sb("distance", [P, ET]), sb("to_last", [P, 1]), sb("is_last", [P, 1])
        pR, pA, pB, pO, pC = banks

        cleared, loaded, gathered, indexed, edge_scores, spread = (
            sem(n) for n in ("cleared", "loaded", "gathered", "indexed", "edge_scores", "spread"))
        scored, scanned, tails_up, chain_scanned, turned, turned_back, shifted, scaled, weighted, fac_ok, fd_ok = (
            sem(n) for n in ("scored", "scanned", "tails_up", "chain_scanned", "turned", "turned_back", "shifted", "scaled",
                             "weighted", "fac", "fd"))
        messages, carried_ok, oh_ok, moved, summed, kept_ok, last_up, stored, osum_ok = (
            sem(n) for n in ("messages", "carried", "oh", "moved", "summed", "kept", "last_up", "stored", "osum"))

        block = ctx.enter_context(nc.Block())

        def windows(eng, g, body):
            body(g * NWIN, 0)
            with eng.Fori(1, NWIN) as j:
                body(g * NWIN + j, j)

        @block.sync
        def _(sp):
            def group(g):
                sp.wait_ge(kept_ok, g * NWIN)
                sp.wait_ge(cleared, 1)
                hold(sp)
                sp.dma_start(features[WINDOW:P, 0, :], epro[:, ds(g * GROUP, GROUP)]).then_inc(loaded, 16)
                sp.dma_start(pens[:, 0, :, :], pens_d[ds(g, 1), :].rearrange("g (k p) -> g k p", k=4)
                             .to_broadcast([H, 4, P])).then_inc(loaded, 16)
                w = sp.value_load(dst_first[0:1, ds(g, 1)], min_val=0, max_val=NP - P)

                def window(v, j):
                    sp.wait_ge(osum_ok, v + 1)
                    hold(sp)
                    sp.dma_start(agg_d[ds(w + j * P, P), :], osum[:, 0, :]).then_inc(stored, 16)
                    sp.wait_ge(stored, v * 16 + 16)
                    hold(sp)

                windows(sp, g, window)

            span_max = sp.value_load(widest[0:1, 0:1], min_val=0, max_val=NP)
            with sp.If(span_max >= WINDOW):
                turns(sp, NG)(group)

        @block.gpsimd
        def _(pool):
            def group(g):
                pool.wait_ge(kept_ok, g * NWIN)
                pool.tensor_copy(idx[:, 0, :], src_all[:, ds(g, 1), :].rearrange("p o t -> p (o t)")).then_inc(indexed, 1)
                pool.tensor_copy(idx[:, 1, :], dst_i[:, ds(g, 1), :].rearrange("p o t -> p (o t)")).then_inc(indexed, 1)
                pool.wait_ge(indexed, 2 * g + 2)
                hold(pool)
                for t in range(ET):
                    pool.indirect_dma_start(G[:, 0, t, :], None, table, bass.IndirectOffsetOnAxis(idx[:, 0, t:t + 1], 0)
                                            ).then_inc(gathered, 16)
                    pool.indirect_dma_start(rows_of_target[:, t, :], None, er_table, bass.IndirectOffsetOnAxis(idx[:, 1, t:t + 1], 0)
                                            ).then_inc(gathered, 16)

            span_max = pool.value_load(widest[0:1, 0:1], min_val=0, max_val=NP)
            with pool.If(span_max >= WINDOW):
                turns(pool, NG)(group)

        @block.vector
        def _(dve):
            def group(g):
                z3 = z[:, 0, :].rearrange("p (t n) -> p t n", t=ET)
                z4 = z[:, 0, :].rearrange("p (t h y) -> p t h y", t=ET, h=H)
                dve.wait_ge(gathered, 32 * ET * (g + 1))
                dve.wait_ge(edge_scores, g + 1)
                dve.tensor_tensor(z3, G[:, 0, :, DIM:ROW], pR[:, 0:ET * HT].rearrange("p (t n) -> p t n", t=ET),
                                  ALU.add).then_inc(scored, 1)
                dve.wait_ge(scored, 5 * g + 1)
                dve.tensor_tensor(z3, z3, rows_of_target[:, :, :], ALU.add).then_inc(scored, 1)
                dve.wait_ge(scored, 5 * g + 2)
                mk = mask_all[:, ds(g, 1), :, :].rearrange("p o t (h y) -> p (o t) h y", h=1).to_broadcast([P, ET, H, TYPES])
                dve.tensor_tensor(z4, z4, mk, ALU.mult).then_inc(scored, 1)
                dve.wait_ge(scored, 5 * g + 3)
                dve.tensor_reduce(e[:, :].rearrange("p (h t) -> p t h", h=H), z4, AX.X, ALU.add).then_inc(scored, 1)
                dve.wait_ge(scored, 5 * g + 4)
                dve.scalar_tensor_tensor(e[:, :], e[:, :], SLOPE, e[:, :], ALU.mult, ALU.max).then_inc(scored, 1)
                dve.wait_ge(scored, 5 * g + 5)
                dve.wait_ge(spread, 2 * g + 2)
                dve.tensor_tensor_scan(scan[:, 0, :], penx[:, 0, :], e[:, :], -BIG, ALU.add, ALU.max).then_inc(scanned, 1)
                dve.tensor_tensor_scan(scan[:, 1, ::-1], penx[:, 1, ::-1], e[:, ::-1], -BIG, ALU.add, ALU.max).then_inc(scanned, 1)
                dve.wait_ge(scanned, 3 * g + 2)
                dve.tensor_tensor(m[:, :], scan[:, 0, :], scan[:, 1, :], ALU.max).then_inc(scanned, 1)
                dve.wait_ge(chain_scanned, 3 * g)
                dve.tensor_copy(rb[:, 0, 0:1], rb[:, 0, P:P + 1]).then_inc(chain_scanned, 1)
                dve.wait_ge(chain_scanned, 3 * g + 1)
                dve.wait_ge(tails_up, g + 1)
                dve.wait_ge(loaded, 32 * g + 32)
                dve.tensor_tensor_scan(rb[:, 0, 1:P + 1], pens[:, 0, 2, :], pA[0:H, 0:P], rb[:, 0, 0:1],
                                       ALU.add, ALU.max).then_inc(chain_scanned, 1)
                dve.tensor_tensor_scan(lb[:, 0, P - 1::-1], pens[:, 0, 3, ::-1], pA[0:H, 2 * P - 1:P - 1:-1], -BIG,
                                       ALU.add, ALU.max).then_inc(chain_scanned, 1)
                dve.wait_ge(chain_scanned, 3 * g + 3)
                dve.tensor_tensor(turn[:, 0, :], rb[:, 0, 0:P], pens[:, 0, 0, :], ALU.add).then_inc(turned, 1)
                dve.tensor_tensor(turn[:, 1, :], lb[:, 0, 1:P + 1], pens[:, 0, 1, :], ALU.add).then_inc(turned, 1)
                dve.wait_ge(turned_back, g + 1)
                for k, pen in enumerate((pen_head, pen_tail)):
                    dve.tensor_tensor(ends[:, k, :].rearrange("p (h t) -> p h t", h=H), pen[:, ds(g, 1), :].to_broadcast([P, H, ET]),
                                      pB[:, k * H:(k + 1) * H].rearrange("p (h o) -> p h o", o=1).to_broadcast([P, H, ET]),
                                      ALU.add).then_inc(shifted, 1)
                dve.wait_ge(shifted, 5 * g + 2)
                dve.wait_ge(scanned, 3 * g + 3)
                dve.tensor_tensor(m[:, :], m[:, :], ends[:, 0, :], ALU.max).then_inc(shifted, 1)
                dve.wait_ge(shifted, 5 * g + 3)
                dve.tensor_tensor(m[:, :], m[:, :], ends[:, 1, :], ALU.max).then_inc(shifted, 1)
                dve.wait_ge(shifted, 5 * g + 4)
                dve.tensor_tensor(e[:, :], e[:, :], m[:, :], ALU.subtract).then_inc(shifted, 1)
                dve.tensor_tensor(fd[:, :], pB[0:1, 0:H], m[0:1, :].rearrange("p (h t) -> p h t", h=H)[:, :, 0],
                                  ALU.subtract).then_inc(fd_ok, 1)
                g4 = G[:, 0, :, 0:DIM].rearrange("p t (h d) -> p t h d", h=H)
                dve.wait_ge(weighted, g + 1)
                dve.tensor_tensor(g4, g4, G[:, 0, :, DIM:AGG].rearrange("p t (h o) -> p t h o", o=1)
                                  .to_broadcast([P, ET, H, GDIM]), ALU.mult).then_inc(messages, 1)
                dve.wait_ge(fac_ok, g + 1)
                dve.wait_ge(kept_ok, g * NWIN)
                dve.tensor_tensor(carried[:, 0:DIM].rearrange("p (h d) -> p h d", h=H), kept[:, 0:DIM].rearrange("p (h d) -> p h d", h=H),
                                  fac[:, :].rearrange("p (h o) -> p h o", o=1).to_broadcast([1, H, GDIM]), ALU.mult).then_inc(carried_ok, 1)
                dve.tensor_tensor(carried[:, DIM:AGG], kept[:, DIM:AGG], fac[:, :], ALU.mult).then_inc(carried_ok, 1)
                dve.wait_ge(carried_ok, 2 * g + 2)

                def window(v, j):
                    dve.wait_ge(oh_ok, 2 * v)
                    if isinstance(j, int):
                        dve.tensor_copy(distance[:, :], rel[:, ds(g, 1), :].rearrange("p o t -> p (o t)")).then_inc(moved, 1)
                        dve.tensor_tensor(to_last[:, :], span[:, ds(g, 1)], iota_col[:, :], ALU.subtract).then_inc(moved, 1)
                    else:
                        dve.tensor_scalar(distance[:, :], distance[:, :], -float(P), None, ALU.add).then_inc(moved, 1)
                        dve.tensor_scalar(to_last[:, :], to_last[:, :], -float(P), None, ALU.add).then_inc(moved, 1)
                    dve.wait_ge(moved, 2 * v + 2)
                    dve.wait_ge(summed, v)
                    dve.wait_ge(last_up, v)
                    dve.tensor_tensor(oh[:, :, :], iota_row[:, :].rearrange("p (o n) -> p o n", o=1).to_broadcast([P, ET, P]),
                                      distance[:, :].rearrange("p (t n) -> p t n", n=1).to_broadcast([P, ET, P]),
                                      ALU.is_equal).then_inc(oh_ok, 1)
                    dve.tensor_scalar(is_last[:, :], to_last[:, :], 0.0, None, ALU.is_equal).then_inc(oh_ok, 1)
                    dve.wait_ge(last_up, v + 1)
                    if isinstance(j, int):
                        dve.tensor_copy(kept[:, :], pC[0:1, 0:AGG]).then_inc(kept_ok, 1)
                    else:
                        dve.wait_ge(kept_ok, v)
                        dve.tensor_tensor(kept[:, :], kept[:, :], pC[0:1, 0:AGG], ALU.add).then_inc(kept_ok, 1)

                windows(dve, g, window)

            span_max = dve.value_load(widest[0:1, 0:1], min_val=0, max_val=NP)
            with dve.If(span_max >= WINDOW):
                dve.memset(features[0:WINDOW, 0, :], 0.0)
                dve.memset(rb[:, 0, :], -BIG)
                dve.memset(kept[:, :], 0.0)
                dve.memset(erw[0:WINDOW, 0, :], 0.0).then_inc(cleared, 1)
                dve.wait_ge(cleared, 1)
                turns(dve, NG)(group)

        @block.scalar
        def _(act):
            def group(g):
                for k, a in enumerate((pen_prev, pen_next)):
                    act.wait_ge(kept_ok, g * NWIN)
                    act.activation(penx[:, k, :].rearrange("p (h t) -> p h t", h=H), a[:, ds(g, 1), :].to_broadcast([P, H, ET]),
                                   ACT.Copy).then_inc(spread, 1)
                act.wait_ge(shifted, 5 * g + 5)
                act.activation(G[:, 0, :, DIM:AGG].rearrange("p t h -> p h t"), e[:, :].rearrange("p (h t) -> p h t", h=H),
                               ACT.Exp, scale=1.0 / 3).then_inc(weighted, 1)
                act.wait_ge(fd_ok, g + 1)
                act.activation(fac[:, :], fd[:, :], ACT.Exp, scale=1.0 / 3).then_inc(fac_ok, 1)

                def window(v, j):
                    act.wait_ge(summed, v + 1)
                    act.wait_ge(stored, v * 16)
                    act.activation(osum[:, 0, :], pO[:, 0:AGG], ACT.Copy).then_inc(osum_ok, 1)

                windows(act, g, window)

            span_max = act.value_load(widest[0:1, 0:1], min_val=0, max_val=NP)
            with act.If(span_max >= WINDOW):
                turns(act, NG)(group)

        @block.tensor
        def _(pe):
            def group(g):
                pe.wait_ge(cleared, 1)
                pe.wait_ge(loaded, 32 * g + 32)
                for t in range(ET):
                    part = pe.matmul(pR[:, t * HT:(t + 1) * HT], features[:, 0, t * P:(t + 1) * P], erw[:, 0, :], start=True, stop=True)
                part.then_inc(edge_scores, 1)
                pe.wait_ge(scanned, 3 * g + 2)
                pe.transpose(pA[0:H, 0:P], scan[:, 0, :].rearrange("p (h t) -> p h t", h=H)[:, :, ET - 1], ident[:, :])
                pe.transpose(pA[0:H, P:2 * P], scan[:, 1, :].rearrange("p (h t) -> p h t", h=H)[:, :, 0], ident[:, :]).then_inc(tails_up, 1)
                pe.wait_ge(turned, 2 * g + 2)
                hold(pe)
                pe.transpose(pB[:, 0:H], turn[:, 0, :], ident[0:H, 0:H])
                pe.transpose(pB[:, H:2 * H], turn[:, 1, :], ident[0:H, 0:H]).then_inc(turned_back, 1)

                def window(v, j):
                    pe.wait_ge(messages, g + 1)
                    pe.wait_ge(carried_ok, 2 * g + 2)
                    pe.wait_ge(oh_ok, 2 * v + 2)
                    pe.wait_ge(osum_ok, v)
                    for t in range(ET):
                        part = pe.matmul(pO[:, 0:AGG], oh[:, t, :], G[:, 0, t, 0:AGG], start=(t == 0),
                                         stop=(t == ET - 1 and not isinstance(j, int)))
                    if isinstance(j, int):
                        part = pe.matmul(pO[:, 0:AGG], e0[:, :], carried[:, :], start=False, stop=True)
                    part.then_inc(summed, 1)
                    pe.wait_ge(osum_ok, v + 1)
                    pe.wait_ge(kept_ok, v)
                    pe.matmul(pC[0:1, 0:AGG], is_last[:, :], osum[:, 0, :], start=True, stop=True).then_inc(last_up, 1)

                windows(pe, g, window)

            span_max = pe.value_load(widest[0:1, 0:1], min_val=0, max_val=NP)
            with pe.If(span_max >= WINDOW):
                turns(pe, NG)(group)


def feed_forward(nc, x, xnT_d, agg_d, mix, b_out, router, w1T, w3T, w2T, ident, eps_col, out):
    E = EXPERTS
    sent_d = nc.dram_tensor("rows_by_expert", [E * CAP + BLK, SENT], F32).ap()
    y_d = nc.dram_tensor("expert_outputs", [2 * NP, DIM], F32).ap()
    with ExitStack() as outer:
        counts = outer.enter_context(nc.sbuf_tensor("counts", [P, E], F32))
        x2 = outer.enter_context(nc.sbuf_tensor("x_after_mixing", [P, NT, DIM], F32))
        with ExitStack() as inner:
            xn = inner.enter_context(nc.sbuf_tensor("x_normalised", [P, NT, DIM], F32))
            logits = inner.enter_context(nc.sbuf_tensor("logits", [P, NT, E], F32))
            combine(nc, x, xnT_d, agg_d, mix, b_out, router, ident, eps_col, x2, xn, logits)
            route(nc, xn, logits, sent_d, counts)
        experts(nc, sent_d, counts, w1T, w3T, w2T, ident, y_d)
        finish(nc, x2, y_d, out)


def combine(nc, x, xnT_d, agg_d, mix, b_out, router, ident, eps_col, x2, xn_kept, logits):
    E, TURNS = EXPERTS, NT // 2
    with ExitStack() as ctx:
        sb, ps, sem, sems, hold = tools(nc, ctx, "comb")
        xt, ag, xT = sb("x", [P, 2, DIM]), sb("agg", [P, 2, AGG]), sb("xT", [P, 2, KC * P])
        bias, rw, xb = sb("bias", [P, DIM]), sb("rw", [P, KC, E]), sb("xb", [P, 2, DIM])
        den, rden, gr, xa = sb("den", [P, 2, GHEADS]), sb("rden", [P, 2, GHEADS]), sb("gr", [P, 2, DIM]), sb("xa", [P, 2, DIM])
        stats, mv, sd, rs = sb("stats", [P, 2, 6]), sb("mv", [P, 2, 2]), sb("sd", [P, 2]), sb("rs", [P, 2])
        xn, xT2 = sb("xn", [P, 2, DIM]), sb("xT2", [P, 2, KC * P])
        pm, pT, pl = [ps("m0"), ps("m1")], [ps("T0"), ps("T1")], [ps("l0"), ps("l1")]
        const_in = sem("const_in")
        tile_in, biased, mixed, turned, xT2_ok, routed, lg_ok, kept = (
            sems(n) for n in ("tile_in", "biased", "mixed", "turned", "xT2", "routed", "lg", "kept"))
        den_ok, rden_ok, gr_ok, xa_ok, x2_ok, stats_ok, mv_ok, sd_ok, rs_ok, xn_ok = (
            sems(n) for n in ("den", "rden", "gr", "xa", "x2", "stats", "mv", "sd", "rs", "xn"))

        def other(i, b, d):
            return i + (b + d) // 2, (b + d) % 2

        def exists(i, b, d):
            return not isinstance(i, int) or 0 <= 2 * i + b + d < NT

        block = ctx.enter_context(nc.Block())

        @block.sync
        def _(sp):
            def load(i, b):
                t = 2 * i + b
                sp.wait_ge(xa_ok[b], i)
                sp.wait_ge(mixed[b], i)
                hold(sp)
                sp.dma_start(xt[:, b, :], x[ds(t * P, P), :]).then_inc(tile_in[b], 16)
                sp.dma_start(ag[:, b, :], agg_d[ds(t * P, P), :]).then_inc(tile_in[b], 16)
                sp.dma_start(xT[:, b, :], xnT_d[ds(t, 1), :, :].rearrange("o p n -> (o p) n")).then_inc(tile_in[b], 16)

            load(0, 0)
            sp.dma_start(bias[:, :], b_out.to_broadcast([P, DIM])).then_inc(const_in, 16)
            sp.dma_start(rw[:, :, :], router.rearrange("(k p) e -> p k e", p=P)).then_inc(const_in, 16)
            load(0, 1)
            with sp.Fori(1, TURNS) as i:
                for b in range(2):
                    load(i, b)

        @block.gpsimd
        def _(pool):
            pool.wait_ge(const_in, 32)

            @turns(pool, TURNS)
            def _(i):
                for b in range(2):
                    pool.wait_ge(tile_in[b], 48 * i + 48)
                    pool.wait_ge(xa_ok[b], i)
                    pool.tensor_tensor(xb[:, b, :], xt[:, b, :], bias[:, :], ALU.add).then_inc(biased[b], 1)

        @block.vector
        def _(dve):
            def weight_sums(i, b):
                dve.wait_ge(tile_in[b], 48 * i + 48)
                dve.tensor_scalar(den[:, b, :], ag[:, b, DIM:AGG], 1e-30, None, ALU.max).then_inc(den_ok[b], 1)

            def inverse_sums(i, b):
                dve.wait_ge(den_ok[b], i + 1)
                dve.reciprocal(rden[:, b, :], den[:, b, :]).then_inc(rden_ok[b], 1)

            def graph_part(i, b):
                dve.wait_ge(rden_ok[b], i + 1)
                dve.tensor_tensor(gr[:, b, :].rearrange("p (h d) -> p h d", h=GHEADS), ag[:, b, 0:DIM].rearrange("p (h d) -> p h d", h=GHEADS),
                                  rden[:, b, :].rearrange("p (h o) -> p h o", o=1).to_broadcast([P, GHEADS, GDIM]), ALU.mult).then_inc(gr_ok[b], 1)

            def add_graph_part(i, b):
                dve.wait_ge(gr_ok[b], i + 1)
                dve.wait_ge(biased[b], i + 1)
                dve.tensor_tensor(xa[:, b, :], gr[:, b, :], xb[:, b, :], ALU.add).then_inc(xa_ok[b], 1)

            weight_sums(0, 0)
            inverse_sums(0, 0)
            graph_part(0, 0)
            add_graph_part(0, 0)

            @turns(dve, TURNS, last=True)
            def _(i):
                for b in range(2):
                    following, more = other(i, b, 1), exists(i, b, 1)
                    x2_t = x2[:, ds(2 * i + b, 1), :].rearrange("p o n -> p (o n)")
                    dve.wait_ge(xa_ok[b], i + 1)
                    dve.wait_ge(mixed[b], i + 1)
                    dve.tensor_tensor(x2_t, xa[:, b, :], pm[b][:, 0:DIM], ALU.add).then_inc(x2_ok[b], 1)
                    if more:
                        weight_sums(*following)
                    dve.wait_ge(x2_ok[b], i + 1)
                    hold(dve)
                    dve.bn_stats(stats[:, b, :], x2_t).then_inc(stats_ok[b], 1)
                    if more:
                        inverse_sums(*following)
                    dve.wait_ge(stats_ok[b], i + 1)
                    hold(dve)
                    dve.bn_aggr(mv[:, b, :], stats[:, b, :]).then_inc(mv_ok[b], 1)
                    if more:
                        graph_part(*following)
                    dve.wait_ge(sd_ok[b], i + 1)
                    dve.reciprocal(rs[:, b:b + 1], sd[:, b:b + 1]).then_inc(rs_ok[b], 1)
                    if more:
                        add_graph_part(*following)
                    dve.wait_ge(rs_ok[b], i + 1)
                    dve.wait_ge(turned[b], i)
                    dve.wait_ge(kept[b], i)
                    dve.tensor_scalar(xn[:, b, :], x2_t, mv[:, b, 0:1], rs[:, b:b + 1], ALU.subtract, ALU.mult).then_inc(xn_ok[b], 1)

        @block.scalar
        def _(act):
            def keep_logits(i, b):
                act.wait_ge(routed[b], i + 1)
                act.activation(logits[:, ds(2 * i + b, 1), :].rearrange("p o e -> p (o e)"), pl[b][:, 0:E], ACT.Copy).then_inc(lg_ok[b], 1)

            @turns(act, TURNS)
            def _(i):
                for b in range(2):
                    act.wait_ge(mv_ok[b], i + 1)
                    act.activation(sd[:, b:b + 1], mv[:, b, 1:2], ACT.Sqrt, bias=eps_col[:, 0:1]).then_inc(sd_ok[b], 1)
                    if not (is_first(i) and b == 0):
                        keep_logits(*other(i, b, -1))
                    act.wait_ge(turned[b], i + 1)
                    act.wait_ge(routed[b], i)
                    act.activation(xT2[:, b, :], pT[b][:, 0:KC * P], ACT.Copy).then_inc(xT2_ok[b], 1)
                    act.activation(xn_kept[:, ds(2 * i + b, 1), :].rearrange("p o n -> p (o n)"), xn[:, b, :], ACT.Copy).then_inc(kept[b], 1)
            keep_logits(TURNS - 1, 1)

        @block.tensor
        def _(pe):
            def attention_part(i, b):
                pe.wait_ge(tile_in[b], 48 * i + 48)
                pe.wait_ge(x2_ok[b], i)
                for k in range(KC):
                    last = pe.matmul(pm[b][:, 0:DIM], xT[:, b, k * P:(k + 1) * P], mix[:, k, :], start=(k == 0), stop=(k == KC - 1))
                last.then_inc(mixed[b], 1)

            def turn_nodes(i, b):
                pe.wait_ge(xn_ok[b], i + 1)
                pe.wait_ge(xT2_ok[b], i)
                for k in range(KC):
                    last = pe.transpose(pT[b][:, k * P:(k + 1) * P], xn[:, b, k * P:(k + 1) * P], ident[:, :])
                last.then_inc(turned[b], 1)

            def expert_logits(i, b):
                pe.wait_ge(xT2_ok[b], i + 1)
                pe.wait_ge(lg_ok[b], i)
                for k in range(KC):
                    last = pe.matmul(pl[b][:, 0:E], xT2[:, b, k * P:(k + 1) * P], rw[:, k, :], start=(k == 0), stop=(k == KC - 1))
                last.then_inc(routed[b], 1)

            pe.wait_ge(const_in, 32)
            attention_part(0, 0)

            @turns(pe, TURNS, last=True)
            def _(i):
                for b in range(2):
                    if exists(i, b, 1):
                        attention_part(*other(i, b, 1))
                    if exists(i, b, -1):
                        expert_logits(*other(i, b, -1))
                    turn_nodes(i, b)
            expert_logits(TURNS - 1, 1)


def route(nc, xn, logits, sent_d, counts):
    E, RB = EXPERTS, 5
    with ExitStack() as ctx:
        sb, ps, sem, sems, hold = tools(nc, ctx, "route")
        iota_i, node_i, code = sb("iota_i", [P, E], I32), sb("node_i", [P, NT], I32), sb("code", [P, NT, 2], I32)
        iota_e, region, node_f = sb("iota_e", [P, E]), sb("region", [P, E]), sb("node_f", [P, NT])
        valid, past_all = sb("valid", [P, NT]), sb("past_all", [P, NT])
        upper, ones = sb("upper", [P, P]), sb("ones", [P, P])
        wide = [P, NT, E]
        prob, work, equal, index = sb("prob", wide), sb("work", wide), sb("equal", wide), sb("index", wide)
        chosen, chosen_of = sb("chosen", [P, 2, NT, E]), sb("chosen_of", wide)
        tile_max, tile_sum, first = sb("tile_max", [P, NT]), sb("tile_sum", [P, NT]), sb("first", [P, NT])
        top, gates, slot, slot_i = sb("top", [P, 2, NT]), sb("gates", [P, NT, 2]), sb("slot", [P, NT, 2]), sb("slot_i", [P, NT, 2], I32)
        before = [sb("before0", wide), sb("before1", wide)]
        rows, slot_now = sb("rows", [P, RB, 2, SENT]), sb("slot_now", [P, RB, 2], I32)
        p_rank, p_total = ps("rank"), ps("total")
        counted, tri, own, exponents_in, exponents, chosen_ok, ranked, slots_ok, counts_ok = (
            sem(n) for n in ("counted", "tri", "own", "exponents_in", "exponents", "chosen", "ranked", "slots_ok", "counts_ok"))
        rows_ok, sent = sems("rows", RB), sems("sent", RB)

        def over_experts(a):
            return a.rearrange("p (t o) -> p t o", o=1).to_broadcast([P, NT, E])

        def over_nodes(a):
            return a.rearrange("p (o e) -> p o e", o=1).to_broadcast([P, NT, E])

        block = ctx.enter_context(nc.Block())

        @block.gpsimd
        def _(pool):
            pool.iota(iota_i[:, :], [[1, E]], base=0, channel_multiplier=0).then_inc(counted, 1)
            pool.iota(node_i[:, :], [[P, NT]], base=0, channel_multiplier=1).then_inc(counted, 1)
            pool.iota(code[:, :, :], [[2 * P, NT], [1, 2]], base=0, channel_multiplier=2).then_inc(counted, 1)
            pool.memset(ones[:, :], 1.0).then_inc(counted, 1)
            pool.memset(upper[:, :], 1.0).then_inc(tri, 1)
            pool.wait_ge(tri, 1)
            pool.affine_select(out=upper[:, :], in_=upper[:, :], compare_op=ALU.is_gt, fill=0.0,
                               base=0, pattern=[[1, P]], channel_multiplier=-1).then_inc(counted, 1)

            @turns(pool, NT // RB)
            def _(i):
                for b in range(RB):
                    pool.wait_ge(rows_ok[b], 4 * i + 4)
                    hold(pool)
                    for k in range(2):
                        pool.indirect_dma_start(sent_d, bass.IndirectOffsetOnAxis(slot_now[:, b, k:k + 1], 0), rows[:, b, k, :], None,
                                                bounds_check=E * CAP - 1, oob_is_err=False).then_inc(sent[b], 16)
            for b in range(RB):
                pool.wait_ge(sent[b], 32 * (NT // RB))

        @block.vector
        def _(dve):
            n = 0

            def then(ins):
                nonlocal n
                n += 1
                ins.then_inc(own, 1)
                dve.wait_ge(own, n)

            then(dve.tensor_reduce(tile_max[:, :], logits[:, :, :], AX.X, ALU.max))
            dve.tensor_tensor(work[:, :, :], logits[:, :, :], over_experts(tile_max[:, :]), ALU.subtract).then_inc(exponents_in, 1)
            dve.wait_ge(counted, 5)
            then(dve.tensor_copy(iota_e[:, :], iota_i[:, :]))
            then(dve.tensor_copy(node_f[:, :], node_i[:, :]))
            then(dve.tensor_scalar(region[:, :], iota_e[:, :], float(CAP), None, ALU.mult))
            then(dve.tensor_scalar(valid[:, :], node_f[:, :], float(NODES), None, ALU.is_lt))
            then(dve.tensor_scalar(past_all[:, :], valid[:, :], -TRASH, TRASH, ALU.mult, ALU.add))
            dve.wait_ge(exponents, 1)
            then(dve.tensor_reduce(tile_sum[:, :], equal[:, :, :], AX.X, ALU.add))
            then(dve.reciprocal(first[:, :], tile_sum[:, :]))
            then(dve.tensor_tensor(prob[:, :, :], equal[:, :, :], over_experts(first[:, :]), ALU.mult))
            for k in range(2):
                left = (prob, work)[k]
                then(dve.tensor_reduce(top[:, k, :], left[:, :, :], AX.X, ALU.max))
                then(dve.tensor_tensor(equal[:, :, :], left[:, :, :], over_experts(top[:, k, :]), ALU.is_equal))
                then(dve.scalar_tensor_tensor(index[:, :, :], equal[:, :, :], -float(E), over_nodes(iota_e[:, :]), ALU.mult, ALU.add))
                then(dve.tensor_reduce(first[:, :], index[:, :, :], AX.X, ALU.min))
                then(dve.tensor_tensor(chosen[:, k, :, :], index[:, :, :], over_experts(first[:, :]), ALU.is_equal))
                if k == 0:
                    then(dve.scalar_tensor_tensor(work[:, :, :], chosen[:, 0, :, :], -2.0, prob[:, :, :], ALU.mult, ALU.add))
            then(dve.tensor_tensor(equal[:, :, :], chosen[:, 0, :, :], chosen[:, 1, :, :], ALU.add))
            dve.tensor_tensor(chosen_of[:, :, :], equal[:, :, :], over_experts(valid[:, :]), ALU.mult).then_inc(chosen_ok, 1)
            then(dve.tensor_tensor(tile_sum[:, :], top[:, 0, :], top[:, 1, :], ALU.add))
            then(dve.tensor_scalar(tile_max[:, :], tile_sum[:, :], 1e-9, None, ALU.add))
            then(dve.reciprocal(first[:, :], tile_max[:, :]))
            for k in range(2):
                then(dve.tensor_tensor(gates[:, :, k], top[:, k, :], first[:, :], ALU.mult))
            dve.wait_ge(ranked, 1)
            then(dve.tensor_copy(before[0][:, :, :].rearrange("p t e -> p (t e)"), p_total[:, 0:NT * E]))
            now, step = 0, 1
            while step < NT:
                then(dve.tensor_copy(before[1 - now][:, 0:step, :], before[now][:, 0:step, :]))
                then(dve.tensor_tensor(before[1 - now][:, step:NT, :], before[now][:, step:NT, :], before[now][:, 0:NT - step, :], ALU.add))
                now, step = 1 - now, 2 * step
            total = before[now]
            then(dve.tensor_tensor(index[:, :, :], p_rank[:, 0:NT * E].rearrange("p (t e) -> p t e", e=E), over_nodes(region[:, :]), ALU.add))
            then(dve.tensor_tensor(index[:, 1:NT, :], index[:, 1:NT, :], total[:, 0:NT - 1, :], ALU.add))
            for k in range(2):
                then(dve.tensor_tensor(equal[:, :, :], chosen[:, k, :, :], index[:, :, :], ALU.mult))
                then(dve.tensor_reduce(slot[:, :, k], equal[:, :, :], AX.X, ALU.add))
            then(dve.tensor_tensor(slot_i[:, :, :], slot[:, :, :], past_all[:, :].rearrange("p (t o) -> p t o", o=1).to_broadcast([P, NT, 2]), ALU.add))
            dve.tensor_tensor(counts[:, :], total[:, NT - 1, :], region[:, :], ALU.add).then_inc(counts_ok, 1)

            @turns(dve, NT // RB)
            def _(i):
                for b in range(RB):
                    t = ds(RB * i + b, 1)
                    dve.wait_ge(sent[b], 32 * i)
                    dve.tensor_copy(rows[:, b, :, DIM:DIM + 1].bitcast(I32), code[:, t, :].rearrange("p o (k n) -> p (o k) n", n=1)).then_inc(rows_ok[b], 1)
                    dve.tensor_copy(rows[:, b, :, DIM + 1:SENT], gates[:, t, :].rearrange("p o (k n) -> p (o k) n", n=1)).then_inc(rows_ok[b], 1)
                    dve.tensor_copy(slot_now[:, b, :], slot_i[:, t, :].rearrange("p o k -> p (o k)")).then_inc(rows_ok[b], 1)

        @block.scalar
        def _(act):
            act.wait_ge(exponents_in, 1)
            act.activation(equal[:, :, :], work[:, :, :], ACT.Exp).then_inc(exponents, 1)

            @turns(act, NT // RB)
            def _(i):
                for b in range(RB):
                    act.wait_ge(sent[b], 32 * i)
                    act.activation(rows[:, b, :, 0:DIM], xn[:, ds(RB * i + b, 1), :].to_broadcast([P, 2, DIM]), ACT.Copy).then_inc(rows_ok[b], 1)

        @block.tensor
        def _(pe):
            pe.wait_ge(counted, 5)
            pe.wait_ge(chosen_ok, 1)
            every = chosen_of[:, :, :].rearrange("p t e -> p (t e)")
            pe.matmul(p_total[:, 0:NT * E], ones[:, :], every, start=True, stop=True)
            pe.matmul(p_rank[:, 0:NT * E], upper[:, :], every, start=True, stop=True).then_inc(ranked, 1)


def experts(nc, sent_d, counts, w1T, w3T, w2T, ident, y_d):
    E, TB = EXPERTS, BLK // P
    with ExitStack() as ctx:
        sb, ps, sem, sems, hold = tools(nc, ctx, "ffn")
        F32R = mybir.dt.float32r
        shapes = ([P, KC, HP], [P, KC, HP], [HW, HC, DIM])
        w_whole = [sb(f"w_whole{j}", [p, n, m]) for j, (p, n, m) in enumerate(shapes)]
        w_high = [sb(f"w_high{j}", [p, 2, n, m], F32R) for j, (p, n, m) in enumerate(shapes)]
        w_low = [sb(f"w_low{j}", [p, 2, n, m], F32R) for j, (p, n, m) in enumerate(shapes)]
        xr, tags, y = sb("xr", [P, 2, TB, SENT]), sb("tags", [P, 2, TB, 2]), sb("y", [P, 2, TB, DIM])
        x_high, x_low = sb("x_high", [P, 2, KC, BLK], F32R), sb("x_low", [P, 2, KC, BLK], F32R)
        s1, h = sb("s1", [HW, 2, 2, BLK]), sb("h", [HW, 2, BLK])
        h_high, h_low = sb("h_high", [HW, 3, 2, BLK], F32R), sb("h_low", [HW, 3, 2, BLK], F32R)
        J = NP // BLK
        ENTRIES = NBLK + 2
        filler = sb("filler", [P, TB, SENT])
        cap_i, cap_f, cnt, step_i, step_f = sb("cap_i", [1, E], I32), sb("cap_f", [1, E]), sb("cnt", [1, E]), sb("step_i", [1, J], I32), sb("step_f", [1, J])
        more, nblk, ends = sb("more", [1, E, J]), sb("nblk", [1, E]), sb("ends", [1, E])
        blk_i, blk_f = sb("blk_i", [1, ENTRIES], I32), sb("blk_f", [1, ENTRIES])
        past, which, took, start = sb("past", [1, ENTRIES, E]), sb("which", [1, ENTRIES]), sb("took", [1, ENTRIES, E]), sb("start", [1, ENTRIES])
        row_f, row0 = sb("row_f", [1, ENTRIES]), sb("row0", [1, ENTRIES])
        started, turns_f, turns_i = sb("started", [1, NBLK // 2]), sb("turns_f", [1, 2]), sb("turns_i", [1, 2], I32)
        tab, fill_i = sb("tab", [1, 2, ENTRIES], I32), sb("fill_i", [1, E], I32)
        ph1, ph3, py, pT = [ps("h1a"), ps("h1b")], [ps("h3a"), ps("h3b")], [ps("ya"), ps("yb")], [ps("Ta"), ps("Tb")]
        counted, own, table_ok, fillers_in = sem("counted"), sem("own"), sem("table_ok"), sem("fillers_in")
        x_in, turned, x_high_ok, x_low_ok, tags_ok, y_ok, stored = (
            sems(n) for n in ("x_in", "turned", "x_high", "x_low", "tags", "y", "stored"))
        h_up, s_ok = sems("h_up"), sems("s")
        w_in, w_high_ok, w_low_ok, h_ok, h_high_ok, h_low_ok, used = (
            sems(n, 3) for n in ("w_in", "w_high", "w_low", "h", "h_high", "h_low", "used"))
        TURNS = NBLK // 2
        FEWEST = -(-2 * NODES // (2 * BLK))

        def banks_of(i, b, g):
            return (3 * b + g) % 2, 3 * i + (3 * b + g) // 2

        def following(i, b):
            return (i, 1) if b == 0 else (i + 1, 0)

        def preceding(i, b):
            return (i, 0) if b == 1 else (i - 1, 1)

        def exists(i, b):
            return not isinstance(i, int) or i >= 0

        def filled_turns(eng):
            eng.wait_ge(table_ok, 1)
            hold(eng)
            return (eng.value_load(turns_i[0:1, 0:1], min_val=FEWEST, max_val=TURNS),
                    eng.value_load(turns_i[0:1, 1:2], min_val=FEWEST - 1, max_val=TURNS - 1))

        def turns_until(eng, end, most):
            def run(body):
                body(0)
                with eng.Fori(1, most) as i:
                    with eng.If(end > i):
                        body(i)
            return run

        block = ctx.enter_context(nc.Block())

        @block.gpsimd
        def _(pool):
            pool.iota(cap_i[:, :], [[CAP, E]], base=0, channel_multiplier=0).then_inc(counted, 1)
            pool.iota(step_i[:, :], [[BLK, J]], base=0, channel_multiplier=0).then_inc(counted, 1)
            pool.iota(blk_i[:, :], [[1, ENTRIES]], base=0, channel_multiplier=0).then_inc(counted, 1)
            pool.iota(filler[:, :, DIM:DIM + 1].bitcast(I32), [[0, TB], [0, 1]], base=2 * NP, channel_multiplier=0).then_inc(counted, 1)

            def low_output_weights(i, b):
                pool.wait_ge(w_high_ok[2], 2 * i + b + 1)
                pool.tensor_tensor(w_low[2][:, b, :, :], w_whole[2][:, :, :], w_high[2][:, b, :, :].bitcast(F32),
                                   ALU.subtract).then_inc(w_low_ok[2], 1)

            low_output_weights(0, 0)
            filled, last_turn = filled_turns(pool)

            @turns_until(pool, filled, TURNS)
            def _(i):
                for b in range(2):
                    low_output_weights(*following(i, b))
                    pool.wait_ge(y_ok[b], TB * i + TB)
                    hold(pool)
                    for tt in range(TB):
                        pool.indirect_dma_start(y_d, bass.IndirectOffsetOnAxis(tags[:, b, tt, 0:1].bitcast(I32), 0),
                                                y[:, b, tt, :], None, bounds_check=2 * NODES - 1, oob_is_err=False).then_inc(stored[b], 16)
            for b in range(2):
                pool.wait_ge(stored[b], filled * (16 * TB))
                hold(pool)

        @block.vector
        def _(dve):
            n = 0

            def then(ins):
                nonlocal n
                n += 1
                ins.then_inc(own, 1)
                dve.wait_ge(own, n)

            dve.wait_ge(counted, 4)
            then(dve.memset(filler[:, :, 0:DIM], 0.0))
            then(dve.memset(filler[:, :, DIM + 1:SENT], 0.0))
            then(dve.tensor_copy(cap_f[:, :], cap_i[:, :]))
            then(dve.tensor_copy(step_f[:, :], step_i[:, :]))
            then(dve.tensor_copy(blk_f[:, :], blk_i[:, :]))
            then(dve.tensor_copy(fill_i[:, :], counts[0:1, :]))
            then(dve.tensor_tensor(cnt[:, :], counts[0:1, :], cap_f[:, :], ALU.subtract))
            then(dve.tensor_tensor(more[:, :, :], cnt[:, :].rearrange("p (e o) -> p e o", o=1).to_broadcast([1, E, J]),
                                   step_f[:, :].rearrange("p (o j) -> p o j", o=1).to_broadcast([1, E, J]), ALU.is_gt))
            then(dve.tensor_reduce(nblk[:, :], more[:, :, :], AX.X, ALU.add))
            then(dve.tensor_copy(ends[:, :], nblk[:, :]))
            for e in range(1, E):
                then(dve.tensor_tensor(ends[:, e:e + 1], ends[:, e:e + 1], ends[:, e - 1:e], ALU.add))
            then(dve.tensor_tensor(past[:, :, :], blk_f[:, :].rearrange("p (s o) -> p s o", o=1).to_broadcast([1, ENTRIES, E]),
                                   ends[:, :].rearrange("p (o e) -> p o e", o=1).to_broadcast([1, ENTRIES, E]), ALU.is_ge))
            then(dve.tensor_reduce(which[:, :], past[:, :, :], AX.X, ALU.add))
            then(dve.tensor_tensor(took[:, :, :], past[:, :, :], nblk[:, :].rearrange("p (o e) -> p o e", o=1).to_broadcast([1, ENTRIES, E]), ALU.mult))
            then(dve.tensor_reduce(start[:, :], took[:, :, :], AX.X, ALU.add))
            then(dve.tensor_tensor(row0[:, :], blk_f[:, :], start[:, :], ALU.subtract))
            then(dve.tensor_scalar(row0[:, :], row0[:, :], float(BLK), None, ALU.mult))
            then(dve.scalar_tensor_tensor(row_f[:, :], which[:, :], float(CAP), row0[:, :], ALU.mult, ALU.add))
            then(dve.tensor_scalar(tab[:, 0, :], row_f[:, :], float(E * CAP), None, ALU.min))
            then(dve.tensor_scalar(tab[:, 1, :], which[:, :], float(E - 1), None, ALU.min))
            first_of_turn = blk_f[:, 0:NBLK].rearrange("p (i b) -> p i b", b=2)[:, :, 0]
            then(dve.tensor_scalar(started[:, :], first_of_turn, ends[:, E - 1:E], None, ALU.is_lt))
            then(dve.tensor_reduce(turns_f[:, 0:1], started[:, :], AX.X, ALU.add))
            then(dve.tensor_scalar(turns_f[:, 1:2], turns_f[:, 0:1], -1.0, None, ALU.add))
            then(dve.tensor_copy(turns_i[:, :], turns_f[:, :]))
            dve.sem_inc(table_ok, 1)
            filled, last_turn = filled_turns(dve)

            def low_weights(i, b, j):
                dve.wait_ge(w_high_ok[j], 2 * i + b + 1)
                dve.tensor_tensor(w_low[j][:, b, :, :], w_whole[j][:, :, :], w_high[j][:, b, :, :].bitcast(F32),
                                  ALU.subtract).then_inc(w_low_ok[j], 1)

            def low_rows(i, b):
                dve.wait_ge(x_high_ok[b], i + 1)
                dve.tensor_tensor(x_low[:, b, :, :].rearrange("p k n -> p (k n)"), pT[b][:, :],
                                  x_high[:, b, :, :].rearrange("p k n -> p (k n)").bitcast(F32), ALU.subtract).then_inc(x_low_ok[b], 1)

            def keep_tags(i, b):
                dve.wait_ge(x_in[b], 16 * i + 16)
                dve.wait_ge(stored[b], 16 * TB * i)
                dve.tensor_copy(tags[:, b, :, :].bitcast(I32), xr[:, b, :, DIM:SENT].bitcast(I32)).then_inc(tags_ok[b], 1)

            def gated_rows(i, b):
                dve.wait_ge(stored[b], 16 * TB * i)
                dve.wait_ge(used[2], 2 * i + b + 1)
                dve.wait_ge(tags_ok[b], i + 1)
                for tt in range(TB):
                    dve.tensor_scalar(y[:, b, tt, :], py[tt][:, 0:DIM], tags[:, b, tt, 1:2], None, ALU.mult).then_inc(y_ok[b], 1)

            low_rows(0, 0)
            keep_tags(0, 0)
            for j in range(2):
                low_weights(0, 0, j)

            @turns_until(dve, filled, TURNS)
            def _(i):
                for b in range(2):
                    s, before, after = 2 * i + b, preceding(i, b), following(i, b)
                    for g in range(3):
                        q, nq = banks_of(i, b, g)
                        dve.wait_ge(s_ok[q], nq + 1)
                        dve.wait_ge(h_low_ok[(g - 1) % 3], s + (g > 0))
                        dve.tensor_tensor(h[:, :, :].rearrange("p c n -> p (c n)"), s1[:, q, :, :].rearrange("p c n -> p (c n)"),
                                          ph3[q][0:HW, :], ALU.mult).then_inc(h_ok[g], 1)
                        if g == 0 and exists(*before):
                            gated_rows(*before)
                        dve.wait_ge(h_high_ok[g], s + 1)
                        dve.tensor_tensor(h_low[:, g, :, :], h[:, :, :], h_high[:, g, :, :].bitcast(F32), ALU.subtract).then_inc(h_low_ok[g], 1)
                        if g == 1:
                            low_rows(*after)
                        if g == 2:
                            keep_tags(*after)
                        else:
                            low_weights(*after, g)
            gated_rows(last_turn, 1)

        @block.sync
        def _(sp):
            sp.wait_ge(table_ok, 1)
            for e in range(E):
                r0 = sp.value_load(fill_i[0:1, e:e + 1], min_val=0, max_val=E * CAP - BLK)
                sp.dma_start(sent_d[ds(r0, BLK), :].rearrange("(t p) n -> p t n", p=P), filler[:, :, :]).then_inc(fillers_in, 16)
            sp.dma_start(sent_d[E * CAP:E * CAP + BLK, :].rearrange("(t p) n -> p t n", p=P), filler[:, :, :]).then_inc(fillers_in, 16)
            sp.wait_ge(fillers_in, 16 * (E + 1))

            filled, last_turn = filled_turns(sp)

            @turns_until(sp, filled + 1, TURNS + 1)
            def _(i):
                for b in range(2):
                    s = 2 * i + b
                    r0 = sp.value_load(tab[0:1, 0, ds(s, 1)], min_val=0, max_val=E * CAP)
                    ex = sp.value_load(tab[0:1, 1, ds(s, 1)], min_val=0, max_val=E - 1)
                    sp.wait_ge(turned[b], i)
                    sp.wait_ge(tags_ok[b], i)
                    hold(sp)
                    sp.dma_start(xr[:, b, :, :], sent_d[ds(r0, BLK), :].rearrange("(t p) n -> p t n", p=P)).then_inc(x_in[b], 16)
                    for j, wT in enumerate((w1T, w3T, w2T)):
                        sp.wait_ge(w_low_ok[j], s)
                        hold(sp)
                        sp.dma_start(w_whole[j][:, :, :], wT[ds(ex, 1), :, :].rearrange("o (k p) n -> p (o k) n", p=(P, P, HW)[j])
                                     ).then_inc(w_in[j], 16)
            for b in range(2):
                sp.wait_ge(x_in[b], filled * 16 + 16)
                hold(sp)
            for j in range(3):
                sp.wait_ge(w_in[j], filled * 32 + 32)
                hold(sp)

        @block.scalar
        def _(act):
            def high_weights(i, b, j):
                act.wait_ge(w_in[j], 16 * (2 * i + b) + 16)
                if not is_first(i):
                    if j < 2:
                        q, nq = banks_of(i, b, 2)
                        act.wait_ge(h_up[q], nq - 2)
                    else:
                        act.wait_ge(used[2], 2 * i + b - 1)
                act.activation(w_high[j][:, b, :, :], w_whole[j][:, :, :], ACT.Copy).then_inc(w_high_ok[j], 1)

            def high_rows(i, b):
                act.wait_ge(turned[b], i + 1)
                if not is_first(i):
                    q, nq = banks_of(i, b, 2)
                    act.wait_ge(h_up[q], nq - 2)
                act.activation(x_high[:, b, :, :].rearrange("p k n -> p (k n)"), pT[b][:, :], ACT.Copy).then_inc(x_high_ok[b], 1)

            high_rows(0, 0)
            for j in range(3):
                high_weights(0, 0, j)

            filled, last_turn = filled_turns(act)

            @turns_until(act, filled, TURNS)
            def _(i):
                for b in range(2):
                    s, after = 2 * i + b, following(i, b)
                    for g in range(3):
                        q, nq = banks_of(i, b, g)
                        act.wait_ge(h_up[q], nq + 1)
                        act.activation(s1[:, q, :, :].rearrange("p c n -> p (c n)"), ph1[q][0:HW, :], ACT.Silu).then_inc(s_ok[q], 1)
                        act.wait_ge(h_ok[g], s + 1)
                        act.wait_ge(used[g], s)
                        act.activation(h_high[:, g, :, :], h[:, :, :], ACT.Copy).then_inc(h_high_ok[g], 1)
                        if g == 1:
                            high_rows(*after)
                        high_weights(*after, g)

        @block.tensor
        def _(pe):
            def transposes(i, b):
                pe.wait_ge(x_in[b], 16 * i + 16)
                pe.wait_ge(x_low_ok[b], i)
                for k in range(KC):
                    for tt in range(TB):
                        last = pe.transpose(pT[b][:, k * BLK + tt * P:k * BLK + (tt + 1) * P], xr[:, b, tt, k * P:(k + 1) * P], ident[:, :])
                last.then_inc(turned[b], 1)

            def product(out, left, right, start, stop):
                pe.matmul(out, left[0], right[0], start=start, stop=False)
                pe.matmul(out, left[0], right[1], start=False, stop=False)
                return pe.matmul(out, left[1], right[0], start=False, stop=stop)

            def hidden(i, b, g):
                q, nq = banks_of(i, b, g)
                for j, p in ((0, ph1), (1, ph3)):
                    if g == 0:
                        pe.wait_ge(w_low_ok[j], 2 * i + b + 1)
                    for m in range(2):
                        for k in range(KC):
                            c0 = (2 * g + m) * HW
                            last = product(p[q][0:HW, m * BLK:(m + 1) * BLK], [w[j][:, b, k, c0:c0 + HW] for w in (w_high, w_low)],
                                           [a[:, b, k, :] for a in (x_high, x_low)], k == 0, k == KC - 1)
                last.then_inc(h_up[q], 1)

            def outputs(i, b, g):
                pe.wait_ge(h_low_ok[g], 2 * i + b + 1)
                if g == 0:
                    pe.wait_ge(w_low_ok[2], 2 * i + b + 1)
                for tt in range(TB):
                    for m in range(2):
                        last = product(py[tt][:, 0:DIM], [a[:, g, m, tt * P:(tt + 1) * P] for a in (h_high, h_low)],
                                       [w[2][:, b, 2 * g + m, :] for w in (w_high, w_low)], g == 0 and m == 0, g == 2 and m == 1)
                last.then_inc(used[g], 1)

            transposes(0, 0)

            filled, last_turn = filled_turns(pe)

            @turns_until(pe, filled, TURNS)
            def _(i):
                for b in range(2):
                    s = 2 * i + b
                    pe.wait_ge(x_low_ok[b], i + 1)
                    pe.wait_ge(h_ok[1], s)
                    hidden(i, b, 0)
                    if exists(*preceding(i, b)):
                        outputs(*preceding(i, b), 2)
                    pe.wait_ge(h_ok[2], s)
                    hidden(i, b, 1)
                    pe.wait_ge(y_ok[1 - b], TB * (i + b))
                    outputs(i, b, 0)
                    transposes(*following(i, b))
                    pe.wait_ge(h_ok[0], s + 1)
                    hidden(i, b, 2)
                    outputs(i, b, 1)
            outputs(last_turn, 1, 2)


def finish(nc, x2, y_d, out):
    W = 4
    whole = NODES // (W * P)
    steps = [(W * j, W, P) for j in range(whole)]
    steps += [(r // P, 1, min(P, NODES - r)) for r in range(whole * W * P, NODES, P)]
    with ExitStack() as ctx:
        sb, ps, sem, sems, hold = tools(nc, ctx, "fin")
        B = 3
        yt, ys = sb("y", [P, B, W, 2, DIM]), sb("ys", [P, B, W, DIM])
        y_in, sum_ok, done, stored = (sems(n, B) for n in ("y_in", "sum", "done", "stored"))
        block = ctx.enter_context(nc.Block())

        @block.sync
        def _(sp):
            for j, (t, w, n) in enumerate(steps):
                b, u = j % B, j // B
                sp.wait_ge(sum_ok[b], u)
                sp.dma_start(yt[0:n, b, 0:w, :, :], y_d[2 * t * P:2 * (t * P + (w - 1) * P + n), :]
                             .rearrange("(w p k) d -> p w k d", w=w, k=2)).then_inc(y_in[b], 16)

        @block.vector
        def _(dve):
            for j, (t, w, n) in enumerate(steps):
                b, u = j % B, j // B
                dve.wait_ge(y_in[b], 16 * u + 16)
                dve.wait_ge(stored[b], 16 * u)
                dve.tensor_tensor(ys[0:n, b, 0:w, :], yt[0:n, b, 0:w, 0, :], yt[0:n, b, 0:w, 1, :], ALU.add).then_inc(sum_ok[b], 1)
                dve.wait_ge(sum_ok[b], u + 1)
                dve.tensor_tensor(ys[0:n, b, 0:w, :], ys[0:n, b, 0:w, :], x2[0:n, t:t + w, :], ALU.add).then_inc(done[b], 1)

        @block.scalar
        def _(act):
            for j, (t, w, n) in enumerate(steps):
                b, u = j % B, j // B
                act.wait_ge(done[b], u + 1)
                act.dma_start(out[t * P:t * P + (w - 1) * P + n, :].rearrange("(w p) d -> p w d", w=w), ys[0:n, b, 0:w, :]).then_inc(stored[b], 16)
            for b in range(B):
                act.wait_ge(stored[b], 16 * ((len(steps) + B - 1 - b) // B))


def kernel(**inputs):
    import concourse.bacc as bacc
    from concourse.bass_utils import run_bass_kernel_spmd

    a = {k: np.asarray(v) for k, v in inputs.items()}

    def rows(v, n):
        return np.concatenate([v, np.zeros((n - v.shape[0],) + v.shape[1:], v.dtype)])

    src = rows(a["src"], EP)
    dst = np.concatenate([a["dst"], np.full(EP - EDGES, NODES, a["dst"].dtype)])
    grouped = dst.reshape(NG, P, ET)
    head, tail = grouped[:, :, 0].reshape(-1), grouped[:, :, -1].reshape(-1)
    before = np.concatenate([np.full(1, -1, dst.dtype), tail[:-1]])
    after = np.concatenate([head[1:], np.full(1, -1, dst.dtype)])
    chain = [rows(v.reshape(NG, P), NG + 2) for v in (head, tail, before, after)]
    first, last = rows(grouped[:, 0, 0], NG + 2)[None], rows(grouped[:, -1, -1], NG + 2)[None]
    columns = rows(grouped.transpose(0, 2, 1).reshape(NG, GROUP), NG + 2)
    mask = rows(a["edge_attr_4"], EP).reshape(NG, P, ET, TYPES).transpose(1, 0, 2, 3)
    epro = rows(rows(a["edge_attr_16"], EP).reshape(NG, P, ET, EPRO).transpose(0, 2, 1, 3).reshape(NG, GROUP, EPRO), NG + 2)
    epro = epro.reshape((NG + 2) * GROUP, EPRO).T
    lr = np.zeros((GHEADS, GDIM, 2, GHEADS, TYPES), np.float32)
    for h in range(GHEADS):
        lr[h, :, 0, h] = a["L0_gnn_attn_l"][h]
        lr[h, :, 1, h] = a["L0_gnn_attn_r"][h]
    attn_m = a["L0_gnn_attn_m"].transpose(1, 0, 2).reshape(EPRO, HT)
    w_qkv = a["L0_mix_w_qkv"]

    def hidden_columns(w):
        out = np.zeros((EXPERTS, DIM, HP), w.dtype)
        out[:, :, :HID] = w.transpose(0, 2, 1)
        return out

    w2T = np.zeros((EXPERTS, HP, DIM), np.float32)
    w2T[:, :HID] = a["L0_ffn_w2"].transpose(0, 2, 1)
    arrays = dict(
        x=rows(a["x"], NP), src=src.reshape(NG, P, ET).transpose(1, 0, 2), dst=grouped.transpose(1, 0, 2),
        dst_first=first, dst_last=last, dst_head=chain[0], dst_tail=chain[1], dst_before=chain[2], dst_after=chain[3],
        dst_cols=columns, mask=mask, epro=epro, w_n=a["L0_gnn_W_n"], w_nT=a["L0_gnn_W_n"].T,
        attn_lr=lr.reshape(DIM, 2 * HT), attn_m=attn_m, w_kvT=w_qkv[INNER:].T, w_q=w_qkv[:INNER],
        w_oT=a["L0_mix_w_out"].T, b_out=a["L0_mix_b_out"][None], router=a["L0_ffn_router_w"].T,
        w1T=hidden_columns(a["L0_ffn_w1"]), w3T=hidden_columns(a["L0_ffn_w3"]), w2T=w2T)
    arrays = {f"in_{k}": np.ascontiguousarray(v) for k, v in arrays.items()}
    nc = bacc.Bacc("TRN2", target_bir_lowering=False, num_devices=1)
    aps = [nc.dram_tensor(k, v.shape, mybir.dt.from_np(v.dtype), kind="ExternalInput").ap() for k, v in arrays.items()]
    out = nc.dram_tensor("out_x", [NODES, DIM], F32, kind="ExternalOutput").ap()
    build(nc, *aps, out)
    r = run_bass_kernel_spmd(nc, [arrays], core_ids=[0])
    return r.results[0]["out_x"]
```
